# Optimizing a Trainium2 kernel written in Bass

```python
import numpy as np
import jax
import jax.numpy as jnp

def _softmax(x, axis=-1):
    return jax.nn.softmax(x, axis=axis)

def _gelu(x):
    return jax.nn.gelu(x, approximate=True)

def _silu(x):
    return jax.nn.silu(x)

def _sigmoid(x):
    return jax.nn.sigmoid(x)

def _layernorm(x, axis=-1, eps=1e-05):
    m = jnp.mean(x, axis=axis, keepdims=True)
    v = jnp.var(x, axis=axis, keepdims=True)
    return (x - m) / jnp.sqrt(v + eps)

def _scatter_add(tgt, idx, src, axis=0):
    return tgt.at[idx].add(src)

def _segment_sum(src, seg, n):
    return jax.ops.segment_sum(src, seg, n)
kernel_name = 'mk_adaln_ffn_d2_seqx_r4_725009'

def setup_inputs(seed: int=0):
    np.random.seed(seed)
    _w = jnp.asarray

    def _rec_inputs():
        import jax
        import jax.numpy as jnp
        _rk = jax.random.key(seed)
        x = 7.22e-05 + 1 * jax.random.normal(jax.random.fold_in(_rk, 1), (8, 256, 256), jnp.float32)
        _lenS = 256 - jax.random.randint(jax.random.fold_in(_rk, 7), (8,), 0, max(1, 256 // 4) + 1, jnp.int32)
        _lenS2 = 256 - jax.random.randint(jax.random.fold_in(_rk, 8), (8,), 0, max(1, 256 // 4) + 1, jnp.int32)
        cond_64 = -0.104238 + 1.01173 * jax.random.normal(jax.random.fold_in(_rk, 11), (8, 64), jnp.float32)
        fside_16xSxS_0 = -5.72187e-05 + 0.999849 * jax.random.normal(jax.random.fold_in(_rk, 12), (16, 256, 256), jnp.float32)
        _validS = jnp.arange(256)[None, :] < _lenS[:, None]
        _validS2 = jnp.arange(256)[None, :] < _lenS2[:, None]
        _causal = jnp.tril(jnp.ones((256, 256), dtype=bool))
        mask_BxS_bk0 = jnp.logical_not(jnp.broadcast_to(_validS[:, :], (8, 256)))
        return (x, cond_64, fside_16xSxS_0, mask_BxS_bk0)
    x, cond_64, fside_16xSxS_0, mask_BxS_bk0 = _rec_inputs()

    def _L0_cond_setup():
        import jax, jax.numpy as jnp
        import numpy as np
        B, S, H = (4, 512, 256)
        E = 8
        M = 128
        K = 2
        N_SHARED = 2
        SM = M * N_SHARED
        G = 64
        GE_TEMP = 1.0
        ALPHA = 0.001
        SEQ_AUX = True
        NORM_TOPK = True
        COS_TEMP = 0.78
        CONS_ALPHA = 0.01
        LEAKY_SLOPE = 0.01
        EPS_COS = 1e-08

        def _leaky(x):
            return jnp.where(x >= 0, x, LEAKY_SLOPE * x)

        def _moe_forward(hidden_states, g, wt, wg, w_gate, w_up, w_down, sw_gate, sw_up, sw_down):
            b, s, h = hidden_states.shape
            x = hidden_states.reshape(-1, h)
            T = x.shape[0]
            logits_h = x @ wt.T
            logits_g = g @ wg.T
            logits_g = jnp.repeat(logits_g, s, axis=0)
            logits = (logits_h + logits_g / GE_TEMP) / (1.0 + 1.0 / GE_TEMP)
            scores = jax.nn.softmax(logits, axis=-1)
            topk_w, topk_idx = jax.lax.top_k(scores, K)
            if K > 1 and NORM_TOPK:
                topk_w = topk_w / (topk_w.sum(-1, keepdims=True) + 1e-20)
            onehot = jax.nn.one_hot(topk_idx.reshape(b, s * K), E, dtype=jnp.float32)
            ce = onehot.sum(1) / (s * K / E)
            aux_loss = (ce * scores.reshape(b, s, E).mean(1)).sum(1).mean() * ALPHA
            gp = _leaky(jnp.einsum('th,ehm->etm', x, w_gate))
            up = jnp.einsum('th,ehm->etm', x, w_up)
            y_all = jnp.einsum('etm,emh->eth', gp * up, w_down)
            y_sel = y_all[topk_idx, jnp.arange(T)[:, None], :]
            y = (y_sel * topk_w[..., None]).sum(1).reshape(b, s, h)
            p = _leaky(hidden_states @ sw_gate) * (hidden_states @ sw_up) @ sw_down
            y = y + p
            num = jnp.sum(y * p, -1)
            den = jnp.maximum(jnp.linalg.norm(y, axis=-1), EPS_COS) * jnp.maximum(jnp.linalg.norm(p, axis=-1), EPS_COS)
            closs = CONS_ALPHA * jnp.mean(num / den / (1.0 + COS_TEMP))
            return (y, aux_loss + closs)
        key = jax.random.key(seed)
        ks = jax.random.split(key, 12)
        sh = 1.0 / np.sqrt(H)
        sm = 1.0 / np.sqrt(M)
        ssm = 1.0 / np.sqrt(SM)
        sg = 1.0 / np.sqrt(G)
        return {'hidden_states': jax.random.normal(ks[0], (B, S, H), jnp.float32), 'g': jax.random.normal(ks[1], (B, G), jnp.float32), 'wt': jax.random.uniform(ks[2], (E, H), jnp.float32, -sh, sh), 'wg': jax.random.uniform(ks[3], (E, G), jnp.float32, -sg, sg), 'w_gate': jax.random.uniform(ks[4], (E, H, M), jnp.float32, -sh, sh), 'w_up': jax.random.uniform(ks[5], (E, H, M), jnp.float32, -sh, sh), 'w_down': jax.random.uniform(ks[6], (E, M, H), jnp.float32, -sm, sm), 'sw_gate': jax.random.uniform(ks[7], (H, SM), jnp.float32, -sh, sh), 'sw_up': jax.random.uniform(ks[8], (H, SM), jnp.float32, -sh, sh), 'sw_down': jax.random.uniform(ks[9], (SM, H), jnp.float32, -ssm, ssm)}
    _L0_cond_all = _L0_cond_setup()
    _L0_cond_in = {k: v for k, v in _L0_cond_all.items() if k in ('wt', 'wg', 'w_gate', 'w_up', 'w_down', 'sw_gate', 'sw_up', 'sw_down')}
    del _L0_cond_all

    def _L0_ffn_setup():
        import jax, jax.numpy as jnp
        import numpy as np
        B, S, D, H, E, K = (4, 512, 256, 512, 8, 2)
        TEMP = 5.0
        EPS = 1e-09
        key = jax.random.key(seed)
        k_x, k_wg, k_w1, k_w2 = jax.random.split(key, 4)
        scale = 0.02
        return {'x': jax.random.normal(k_x, (B, S, D), dtype=jnp.float32), 'Wg': jax.random.normal(k_wg, (D, E), dtype=jnp.float32) * scale, 'bg': jnp.zeros((E,), dtype=jnp.float32), 'W1': jax.random.normal(k_w1, (E, D, H), dtype=jnp.float32) * scale, 'b1': jnp.zeros((E, H), dtype=jnp.float32), 'W2': jax.random.normal(k_w2, (E, H, D), dtype=jnp.float32) * scale, 'b2': jnp.zeros((E, D), dtype=jnp.float32)}
    _L0_ffn_all = _L0_ffn_setup()
    _L0_ffn_in = {k: v for k, v in _L0_ffn_all.items() if k in ('Wg', 'bg', 'W1', 'b1', 'W2', 'b2')}
    del _L0_ffn_all

    def _L1_cond_setup():
        import jax, jax.numpy as jnp
        import numpy as np
        B, N, DIM, H, DH = (2, 512, 256, 16, 64)
        INNER = H * DH
        EPS = 1e-05

        def layernorm(x, g):
            mean = jnp.mean(x, axis=-1, keepdims=True)
            var = jnp.var(x, axis=-1, keepdims=True)
            return (x - mean) * jax.lax.rsqrt(var + EPS) * g
        key = jax.random.key(seed)
        ks = jax.random.split(key, 10)
        x = jax.random.normal(ks[0], (B, N, DIM), dtype=jnp.float32)
        attn_bias = jax.random.normal(ks[1], (H, N, N), dtype=jnp.float32)
        mask = jax.random.randint(ks[2], (B, N), 0, 2).astype(bool)
        g_in = jnp.ones((DIM,), dtype=jnp.float32)
        null_attn_bias = jax.random.normal(ks[3], (H,), dtype=jnp.float32)
        null_kv = jax.random.normal(ks[4], (2, DH), dtype=jnp.float32)
        Wq = jax.random.normal(ks[5], (DIM, INNER), dtype=jnp.float32) * 0.02
        Wkv = jax.random.normal(ks[6], (DIM, 2 * DH), dtype=jnp.float32) * 0.02
        Wo = jax.random.normal(ks[7], (INNER, DIM), dtype=jnp.float32) * 0.02
        g_out = jnp.ones((DIM,), dtype=jnp.float32)
        return {'x': x, 'attn_bias': attn_bias, 'mask': mask, 'g_in': g_in, 'null_attn_bias': null_attn_bias, 'null_kv': null_kv, 'Wq': Wq, 'Wkv': Wkv, 'Wo': Wo, 'g_out': g_out}
    _L1_cond_all = _L1_cond_setup()
    _L1_cond_in = {k: v for k, v in _L1_cond_all.items() if k in ('g_in', 'null_attn_bias', 'Wq', 'Wkv', 'Wo', 'g_out')}
    del _L1_cond_all

    def _L1_ffn_setup():
        import jax, jax.numpy as jnp
        import numpy as np
        B, S, D = (4, 512, 256)
        DFF = 128
        E = 16
        TOP_K = 2
        N_SHARED = 2
        FUSED_DFF = DFF * N_SHARED
        key = jax.random.key(seed)
        ks = jax.random.split(key, 16)
        sc_d = 1.0 / np.sqrt(D)
        sc_f = 1.0 / np.sqrt(DFF)
        sc_sf = 1.0 / np.sqrt(FUSED_DFF)
        inp = {'x': jax.random.normal(ks[0], (B, S, D), dtype=jnp.float32), 'gate_w': jax.random.uniform(ks[1], (E, D), dtype=jnp.float32, minval=-sc_d, maxval=sc_d), 'expert_bias': jnp.zeros((E,), dtype=jnp.float32), 'w1': jax.random.uniform(ks[2], (E, DFF, D), dtype=jnp.float32, minval=-sc_d, maxval=sc_d), 'b1': jax.random.uniform(ks[3], (E, DFF), dtype=jnp.float32, minval=-sc_d, maxval=sc_d), 'w3': jax.random.uniform(ks[4], (E, DFF, D), dtype=jnp.float32, minval=-sc_d, maxval=sc_d), 'b3': jax.random.uniform(ks[5], (E, DFF), dtype=jnp.float32, minval=-sc_d, maxval=sc_d), 'w2': jax.random.uniform(ks[6], (E, D, DFF), dtype=jnp.float32, minval=-sc_f, maxval=sc_f), 'b2': jax.random.uniform(ks[7], (E, D), dtype=jnp.float32, minval=-sc_f, maxval=sc_f), 'sw1': jax.random.uniform(ks[8], (FUSED_DFF, D), dtype=jnp.float32, minval=-sc_d, maxval=sc_d), 'sb1': jax.random.uniform(ks[9], (FUSED_DFF,), dtype=jnp.float32, minval=-sc_d, maxval=sc_d), 'sw3': jax.random.uniform(ks[10], (FUSED_DFF, D), dtype=jnp.float32, minval=-sc_d, maxval=sc_d), 'sb3': jax.random.uniform(ks[11], (FUSED_DFF,), dtype=jnp.float32, minval=-sc_d, maxval=sc_d), 'sw2': jax.random.uniform(ks[12], (D, FUSED_DFF), dtype=jnp.float32, minval=-sc_sf, maxval=sc_sf), 'sb2': jax.random.uniform(ks[13], (D,), dtype=jnp.float32, minval=-sc_sf, maxval=sc_sf)}
        return inp
    _L1_ffn_all = _L1_ffn_setup()
    _L1_ffn_in = {k: v for k, v in _L1_ffn_all.items() if k in ('gate_w', 'expert_bias', 'w1', 'b1', 'w2', 'b2', 'w3', 'b3', 'sw1', 'sb1', 'sw2', 'sb2', 'sw3', 'sb3')}
    del _L1_ffn_all
    return {'x': x, 'cond_64': cond_64, 'fside_16xSxS_0': fside_16xSxS_0, 'mask_BxS_bk0': mask_BxS_bk0, 'L0_cond_wt': _L0_cond_in['wt'], 'L0_cond_wg': _L0_cond_in['wg'], 'L0_cond_w_gate': _L0_cond_in['w_gate'], 'L0_cond_w_up': _L0_cond_in['w_up'], 'L0_cond_w_down': _L0_cond_in['w_down'], 'L0_cond_sw_gate': _L0_cond_in['sw_gate'], 'L0_cond_sw_up': _L0_cond_in['sw_up'], 'L0_cond_sw_down': _L0_cond_in['sw_down'], 'L0_ffn_Wg': _L0_ffn_in['Wg'], 'L0_ffn_bg': _L0_ffn_in['bg'], 'L0_ffn_W1': _L0_ffn_in['W1'], 'L0_ffn_b1': _L0_ffn_in['b1'], 'L0_ffn_W2': _L0_ffn_in['W2'], 'L0_ffn_b2': _L0_ffn_in['b2'], 'L1_cond_g_in': _L1_cond_in['g_in'], 'L1_cond_null_attn_bias': _L1_cond_in['null_attn_bias'], 'L1_cond_Wq': _L1_cond_in['Wq'], 'L1_cond_Wkv': _L1_cond_in['Wkv'], 'L1_cond_Wo': _L1_cond_in['Wo'], 'L1_cond_g_out': _L1_cond_in['g_out'], 'L1_ffn_gate_w': _L1_ffn_in['gate_w'], 'L1_ffn_expert_bias': _L1_ffn_in['expert_bias'], 'L1_ffn_w1': _L1_ffn_in['w1'], 'L1_ffn_b1': _L1_ffn_in['b1'], 'L1_ffn_w2': _L1_ffn_in['w2'], 'L1_ffn_b2': _L1_ffn_in['b2'], 'L1_ffn_w3': _L1_ffn_in['w3'], 'L1_ffn_b3': _L1_ffn_in['b3'], 'L1_ffn_sw1': _L1_ffn_in['sw1'], 'L1_ffn_sb1': _L1_ffn_in['sb1'], 'L1_ffn_sw2': _L1_ffn_in['sw2'], 'L1_ffn_sb2': _L1_ffn_in['sb2'], 'L1_ffn_sw3': _L1_ffn_in['sw3'], 'L1_ffn_sb3': _L1_ffn_in['sb3']}

def reference(x, cond_64, fside_16xSxS_0, mask_BxS_bk0, L0_cond_wt, L0_cond_wg, L0_cond_w_gate, L0_cond_w_up, L0_cond_w_down, L0_cond_sw_gate, L0_cond_sw_up, L0_cond_sw_down, L0_ffn_Wg, L0_ffn_bg, L0_ffn_W1, L0_ffn_b1, L0_ffn_W2, L0_ffn_b2, L1_cond_g_in, L1_cond_null_attn_bias, L1_cond_Wq, L1_cond_Wkv, L1_cond_Wo, L1_cond_g_out, L1_ffn_gate_w, L1_ffn_expert_bias, L1_ffn_w1, L1_ffn_b1, L1_ffn_w2, L1_ffn_b2, L1_ffn_w3, L1_ffn_b3, L1_ffn_sw1, L1_ffn_sb1, L1_ffn_sw2, L1_ffn_sb2, L1_ffn_sw3, L1_ffn_sb3):
    import jax
    import jax.numpy as jnp

    def _L0_cond_ref(hidden_states, g, wt, wg, w_gate, w_up, w_down, sw_gate, sw_up, sw_down):
        import jax, jax.numpy as jnp
        import numpy as np
        B, S, H = (4, 512, 256)
        E = 8
        M = 128
        K = 2
        N_SHARED = 2
        SM = M * N_SHARED
        G = 64
        GE_TEMP = 1.0
        ALPHA = 0.001
        SEQ_AUX = True
        NORM_TOPK = True
        COS_TEMP = 0.78
        CONS_ALPHA = 0.01
        LEAKY_SLOPE = 0.01
        EPS_COS = 1e-08

        def _leaky(x):
            return jnp.where(x >= 0, x, LEAKY_SLOPE * x)

        def _moe_forward(hidden_states, g, wt, wg, w_gate, w_up, w_down, sw_gate, sw_up, sw_down):
            b, s, h = hidden_states.shape
            x = hidden_states.reshape(-1, h)
            T = x.shape[0]
            logits_h = x @ wt.T
            logits_g = g @ wg.T
            logits_g = jnp.repeat(logits_g, s, axis=0)
            logits = (logits_h + logits_g / GE_TEMP) / (1.0 + 1.0 / GE_TEMP)
            scores = jax.nn.softmax(logits, axis=-1)
            topk_w, topk_idx = jax.lax.top_k(scores, K)
            if K > 1 and NORM_TOPK:
                topk_w = topk_w / (topk_w.sum(-1, keepdims=True) + 1e-20)
            onehot = jax.nn.one_hot(topk_idx.reshape(b, s * K), E, dtype=jnp.float32)
            ce = onehot.sum(1) / (s * K / E)
            aux_loss = (ce * scores.reshape(b, s, E).mean(1)).sum(1).mean() * ALPHA
            gp = _leaky(jnp.einsum('th,ehm->etm', x, w_gate))
            up = jnp.einsum('th,ehm->etm', x, w_up)
            y_all = jnp.einsum('etm,emh->eth', gp * up, w_down)
            y_sel = y_all[topk_idx, jnp.arange(T)[:, None], :]
            y = (y_sel * topk_w[..., None]).sum(1).reshape(b, s, h)
            p = _leaky(hidden_states @ sw_gate) * (hidden_states @ sw_up) @ sw_down
            y = y + p
            num = jnp.sum(y * p, -1)
            den = jnp.maximum(jnp.linalg.norm(y, axis=-1), EPS_COS) * jnp.maximum(jnp.linalg.norm(p, axis=-1), EPS_COS)
            closs = CONS_ALPHA * jnp.mean(num / den / (1.0 + COS_TEMP))
            return (y, aux_loss + closs)
        y, _ = _moe_forward(hidden_states, g, wt, wg, w_gate, w_up, w_down, sw_gate, sw_up, sw_down)
        return y

    def _L0_ffn_ref(x, Wg, bg, W1, b1, W2, b2):
        import jax, jax.numpy as jnp
        import numpy as np
        B, S, D, H, E, K = (4, 512, 256, 512, 8, 2)
        TEMP = 5.0
        EPS = 1e-09
        logits = jnp.einsum('bsd,de->bse', x, Wg) + bg
        probs = jax.nn.softmax(logits / TEMP, axis=-1)
        vals, idx = jax.lax.top_k(probs, K)
        onehot = jax.nn.one_hot(idx, E, dtype=x.dtype)
        mask = jnp.einsum('bske,bsk->bse', onehot, vals)
        gates = mask / (jnp.sum(mask, axis=-1, keepdims=True) + EPS)
        h = jax.nn.gelu(jnp.einsum('bsd,edh->besh', x, W1) + b1[None, :, None, :], approximate=False)
        out = jnp.einsum('besh,ehd->besd', h, W2) + b2[None, :, None, :]
        y = jnp.einsum('bse,besd->bsd', gates, out)
        return y

    def _L1_cond_ref(x, attn_bias, mask, g_in, null_attn_bias, null_kv, Wq, Wkv, Wo, g_out):
        import jax, jax.numpy as jnp
        import numpy as np
        B, N, DIM, H, DH = (2, 512, 256, 16, 64)
        INNER = H * DH
        EPS = 1e-05

        def layernorm(x, g):
            mean = jnp.mean(x, axis=-1, keepdims=True)
            var = jnp.var(x, axis=-1, keepdims=True)
            return (x - mean) * jax.lax.rsqrt(var + EPS) * g
        b, n, _ = x.shape
        scale = DH ** (-0.5)
        xn = layernorm(x, g_in)
        q = (xn @ Wq).reshape(b, n, H, DH).transpose(0, 2, 1, 3) * scale
        kv = xn @ Wkv
        k, v = (kv[..., :DH], kv[..., DH:])
        nk = jnp.broadcast_to(null_kv[0], (b, 1, DH))
        nv = jnp.broadcast_to(null_kv[1], (b, 1, DH))
        k = jnp.concatenate([nk, k], axis=1)
        v = jnp.concatenate([nv, v], axis=1)
        sim = jnp.einsum('bhid,bjd->bhij', q, k)
        null_col = jnp.broadcast_to(null_attn_bias[:, None, None], (H, n, 1))
        bias = jnp.concatenate([null_col, attn_bias], axis=-1)
        sim = sim + bias
        neg = -jnp.finfo(sim.dtype).max
        j = n + 1
        causal_mask = jnp.triu(jnp.ones((n, j), dtype=bool), k=j - n + 1)
        sim = jnp.where(causal_mask, neg, sim)
        mask_p = jnp.pad(mask, ((0, 0), (1, 0)), constant_values=True)
        sim = jnp.where(mask_p[:, None, None, :], sim, neg)
        attn = jax.nn.softmax(sim, axis=-1)
        out = jnp.einsum('bhij,bjd->bhid', attn, v)
        out = out.transpose(0, 2, 1, 3).reshape(b, n, INNER)
        out = out @ Wo
        return layernorm(out, g_out)

    def _L1_ffn_ref(x, gate_w, expert_bias, w1, b1, w2, b2, w3, b3, sw1, sb1, sw2, sb2, sw3, sb3):
        import jax, jax.numpy as jnp
        import numpy as np
        B, S, D = (4, 512, 256)
        DFF = 128
        E = 16
        TOP_K = 2
        N_SHARED = 2
        FUSED_DFF = DFF * N_SHARED
        Bv, Sv, Dv = x.shape
        xf = x.reshape(-1, Dv)
        logits = xf @ gate_w.T
        scores = jax.nn.sigmoid(logits)
        biased = logits + expert_bias.astype(logits.dtype)[None, :]
        _, topk_idx = jax.lax.top_k(biased, TOP_K)
        topk_w = jnp.take_along_axis(scores, topk_idx, axis=-1)
        topk_w = topk_w / (topk_w.sum(-1, keepdims=True) + 1e-10)
        gatew = (jax.nn.one_hot(topk_idx, E, dtype=xf.dtype) * topk_w[..., None]).sum(1)
        y = jnp.zeros_like(xf)
        for e in range(E):
            h = jax.nn.silu(xf @ w1[e].T + b1[e]) * (xf @ w3[e].T + b3[e])
            y = y + gatew[:, e:e + 1] * (h @ w2[e].T + b2[e])
        hs = jax.nn.silu(xf @ sw1.T + sb1) * (xf @ sw3.T + sb3)
        y = y + hs @ sw2.T + sb2
        return y.reshape(Bv, Sv, Dv)
    x = x + _L0_ffn_ref(_L0_cond_ref(x, cond_64, L0_cond_wt, L0_cond_wg, L0_cond_w_gate, L0_cond_w_up, L0_cond_w_down, L0_cond_sw_gate, L0_cond_sw_up, L0_cond_sw_down), L0_ffn_Wg, L0_ffn_bg, L0_ffn_W1, L0_ffn_b1, L0_ffn_W2, L0_ffn_b2)
    x = x + _L1_ffn_ref(_L1_cond_ref(x, fside_16xSxS_0, mask_BxS_bk0, L1_cond_g_in, L1_cond_null_attn_bias, cond_64, L1_cond_Wq, L1_cond_Wkv, L1_cond_Wo, L1_cond_g_out), L1_ffn_gate_w, L1_ffn_expert_bias, L1_ffn_w1, L1_ffn_b1, L1_ffn_w2, L1_ffn_b2, L1_ffn_w3, L1_ffn_b3, L1_ffn_sw1, L1_ffn_sb1, L1_ffn_sw2, L1_ffn_sb2, L1_ffn_sw3, L1_ffn_sb3)
    return x

_drawn_inputs = setup_inputs


def setup_inputs(seed=0):
    import zlib

    import numpy as np

    out = dict(_drawn_inputs(seed))
    spreads = {'L0_ffn_bg': (0.0, 0.1),
     'L0_ffn_b1': (0.0, 0.442),
     'L0_ffn_b2': (0.0, 0.1),
     'L1_cond_g_in': (1.0, 0.6),
     'L1_cond_g_out': (1.0, 0.2),
     'L1_ffn_expert_bias': (0.0, 0.585)}
    factors = {'L0_ffn_W1': 6.392,
     'L0_ffn_W2': 2.898,
     'L1_cond_Wq': 2.843,
     'L1_ffn_b1': 8.0,
     'L1_ffn_b3': 8.0,
     'L1_ffn_sb1': 7.491,
     'L1_ffn_sb3': 7.665}
    for name, (base, spread) in spreads.items():
        noise = np.random.default_rng([zlib.crc32(name.encode()), seed]).standard_normal(out[name].shape)
        drawn = base * np.exp(spread * noise) if base else spread * noise
        out[name] = jnp.asarray(drawn.astype(out[name].dtype))
    for name, factor in factors.items():
        out[name] = (out[name] * factor).astype(out[name].dtype)
    return out
```

```python
from contextlib import ExitStack

import concourse.bass as bass
from concourse import mybir

F32 = mybir.dt.float32
F16 = mybir.dt.float16
I32 = mybir.dt.int32
U32 = mybir.dt.uint32
U8 = mybir.dt.uint8
ALU = mybir.AluOpType
ACT = mybir.ActivationFunctionType
AX_X = mybir.AxisListType.X

P = 128
BATCH, SEQ, DIM = 8, 256, 256
TOKENS = BATCH * SEQ
TT = TOKENS // P
KD = DIM // P
PAIRS = 2 * TOKENS
RING = 4
HEADS, DH = 16, 64
QT = SEQ // P
KEYS0, KEYS1 = 1 + P, 1 + SEQ
KEYS = KEYS0 + KEYS1
HIDDEN_KEY = 1e30
LOWEST = -3e38
NPAIR = HEADS // 2


def slot_tiles(experts):
    return (PAIRS - experts) // P + experts


def live(s0, off, n):
    return not isinstance(s0, int) or 0 <= s0 + off < n


def wait(eng, sem, value):
    if not isinstance(value, int) or value > 0:
        eng.wait_ge(sem, value)


def steps(eng, n, body, lead, lag):
    lo = max(RING, -(-lag // RING) * RING)
    hi = lo + (n - lead - lo) // RING * RING
    for s in range(0, lo):
        body(s - s % RING, s % RING)
    with eng.Fori(lo // RING, hi // RING) as i:
        for u in range(RING):
            body(i * RING, u)
    for s in range(hi, n + lag):
        body(s - s % RING, s % RING)


def one(ap, i):
    return ap[:, bass.ds(i, 1), :].rearrange("p o n -> p (o n)")


class Ring:
    def __init__(self, sem, name):
        self.sems = [sem(f"{name}{r}") for r in range(RING)]
        self.count = [0] * RING


class Use:
    def __init__(self, ring, tiles, dmas=1):
        self.sems, self.dmas = ring.sems, dmas
        self.before = list(ring.count)
        for r in range(RING):
            ring.count[r] += 16 * dmas * len(range(r, tiles, RING))
        self.after = list(ring.count)


class Stage:
    def __init__(self, sem, name, experts, src, loads, eps):
        self.name, self.E, self.NT, self.src, self.loads, self.eps = name, experts, slot_tiles(experts), src, loads, eps
        self.weights_loaded = sem(f"{name}_weights_loaded")
        self.tok_turned = sem(f"{name}_tok_turned")
        self.tokT_ready = sem(f"{name}_tokT_ready")
        self.logits_done = sem(f"{name}_logits_done")
        self.route_step = sem(f"{name}_route_step")
        self.exp_wanted = sem(f"{name}_exp_wanted")
        self.exp_done = sem(f"{name}_exp_done")
        self.onehot_ready = sem(f"{name}_onehot_ready")
        self.prefix_done = sem(f"{name}_prefix_done")
        self.eqrow_ready = sem(f"{name}_eqrow_ready")
        self.eqrow_used = sem(f"{name}_eqrow_used")
        self.inv_done = sem(f"{name}_inv_done")
        self.routed = sem(f"{name}_routed")
        self.combined = sem(f"{name}_combined")
        self.combine_step = sem(f"{name}_combine_step")


class Ffn:
    def __init__(self, sem, name, n, hw, hk, kind, st, rows, shared, w_in, w_out, b_in, b_out):
        self.name, self.n, self.hw, self.hk, self.kind, self.st, self.rows, self.shared = name, n, hw, hk, kind, st, rows, shared
        self.w_in, self.w_out, self.b_in, self.b_out = w_in, w_out, b_in, b_out
        self.turned = sem(f"{name}_turned")
        self.xT_ready = sem(f"{name}_xT_ready")
        self.h_mm = sem(f"{name}_h_mm")
        self.h_pre = sem(f"{name}_h_pre")
        self.h_gate = sem(f"{name}_h_gate")
        self.h_ready = sem(f"{name}_h_ready")
        self.h_turned = sem(f"{name}_h_turned")
        self.hT_ready = sem(f"{name}_hT_ready")
        self.y_mm = sem(f"{name}_y_mm")
        self.y_out = sem(f"{name}_y_out")


class Attention:
    def __init__(self, sem, loads):
        self.loads = loads
        self.loaded = sem("c_loaded")
        self.stat = sem("c_stat")
        self.mom_done = sem("c_mom_done")
        self.var_done = sem("c_var_done")
        self.std_done = sem("c_std_done")
        self.rstd_done = sem("c_rstd_done")
        self.bias_ready = sem("c_bias_ready")
        self.kT_fixed = sem("c_kT_fixed")
        self.xn_ready = sem("c_xn_ready")
        self.xn_turned = sem("c_xn_turned")
        self.xnT_ready = sem("c_xnT_ready")
        self.kv_mm = sem("c_kv_mm")
        self.kT_ready = sem("c_kT_ready")
        self.v_ready = sem("c_v_ready")
        self.q_mm = sem("c_q_mm")
        self.qT_ready = sem("c_qT_ready")
        self.s_mm = sem("c_s_mm")
        self.mask_ready = sem("c_mask_ready")
        self.bm_ready = sem("c_bm_ready")
        self.score_ready = sem("c_score_ready")
        self.p_ready = sem("c_p_ready")
        self.rec_ready = sem("c_rec_ready")
        self.pn_ready = sem("c_pn_ready")
        self.p_turned = sem("c_p_turned")
        self.pT_ready = sem("c_pT_ready")
        self.pv_mm = sem("c_pv_mm")
        self.o_ready = sem("c_o_ready")
        self.wo_mm = sem("c_wo_mm")
        self.ao_ready = sem("c_ao_ready")
        self.ao_stat = sem("c_ao_stat")
        self.z_step = sem("c_z_step")


def build(nc, io):
    ctx = ExitStack()
    with ctx:
        def sb(name, shape, dt=F32):
            return ctx.enter_context(nc.sbuf_tensor(name, shape, dt))

        def sem(name):
            return ctx.enter_context(nc.semaphore(name))

        def carve(region, sizes):
            at, parts = 0, []
            for n in sizes:
                parts.append(region[:, at:at + n])
                at += n
            return parts

        x2 = sb("x2", [P, TT, DIM])
        acc = sb("acc", [P, TT, DIM])
        region_ac = sb("region_ac", [P, 10784])
        region_bd = sb("region_bd", [P, 22784])
        work = sb("work", [P, 8704])

        a_gu, a_down, a_sgu, a_sdown = carve(region_ac, [4096, 2048, 1024, 512])
        a_gu = a_gu.rearrange("p (e k n) -> p e k n", e=8, k=KD)
        a_down = a_down.rearrange("p (e n) -> p e n", e=8)
        a_sgu = a_sgu.rearrange("p (k n) -> p k n", k=KD)
        a_sdown = a_sdown.rearrange("p (k n) -> p k n", k=2)
        c_wq, c_wkk, c_wvv, c_wo, c_bias = carve(region_ac, [2048, 256, 256, 2048, HEADS * KEYS])
        c_wq = c_wq.rearrange("p (k n) -> p k n", k=KD)
        c_wkk = c_wkk.rearrange("p (k n) -> p k n", k=KD)
        c_wvv = c_wvv.rearrange("p (k n) -> p k n", k=KD)
        c_wo = c_wo.rearrange("p (j n) -> p j n", j=NPAIR)
        c_bias = c_bias.rearrange("p (h n) -> p h n", h=HEADS)
        b_w1, b_w2, b_b1, b_b2 = carve(region_bd, [8192, 8192, 4096, 2048])
        b_w1 = b_w1.rearrange("p (e k n) -> p e k n", e=8, k=KD)
        b_w2 = b_w2.rearrange("p (e k n) -> p e k n", e=8, k=4)
        b_b1 = b_b1.rearrange("p (e n) -> p e n", e=8)
        b_b2 = b_b2.rearrange("p (e n) -> p e n", e=8)
        d_w13, d_w2, d_s13, d_s2, d_b13, d_b2, d_sb13, d_sb2 = carve(
            region_bd, [8192, 4096, 1024, 512, 4096, 4096, 512, 256])
        d_w13 = d_w13.rearrange("p (e k n) -> p e k n", e=16, k=KD)
        d_w2 = d_w2.rearrange("p (e n) -> p e n", e=16)
        d_s13 = d_s13.rearrange("p (k n) -> p k n", k=KD)
        d_s2 = d_s2.rearrange("p (k n) -> p k n", k=2)
        d_b13 = d_b13.rearrange("p (e n) -> p e n", e=16)
        d_b2 = d_b2.rearrange("p (e n) -> p e n", e=16)

        xs, xT, hbuf, hT, ys, xr, xrT, gat = carve(work, [1024, 512, 1024, 1024, 1024, 1024, 512, 2048])
        xs = xs.rearrange("p (r n) -> p r n", r=RING)
        xT = xT.rearrange("p (r k n) -> p r k n", r=2, k=KD)
        hbuf = hbuf.rearrange("p (r n) -> p r n", r=2)
        hT = hT.rearrange("p (r n) -> p r n", r=2)
        xr = xr.rearrange("p (r n) -> p r n", r=RING)
        xrT = xrT.rearrange("p (r k n) -> p r k n", r=2, k=KD)
        rt_lg, rt_key, rt_tmp, rt_oh1, rt_oh2, rt_sc, rt_pos, rt_small = carve(gat, [256] * 8)
        eq_tile = ys[:, 0:768].bitcast(F16)
        eq_row = ys[:, 768:1024].bitcast(F16).rearrange("p (r n) -> p r n", r=RING)
        ys = ys.rearrange("p (r n) -> p r n", r=RING)
        gat = gat.rearrange("p (r c n) -> p r c n", r=RING, c=2)
        (c_xn, c_xnT, c_qT, c_kT, c_v, c_bm, c_sc, c_p, c_pT, c_oT, c_mp, c_small) = carve(
            work, [512, 512, 512, 2 * KEYS1, 128, 2 * KEYS, 2 * KEYS, 2 * KEYS, 768, 2048, KEYS, 32])
        c_xn = c_xn.rearrange("p (i n) -> p i n", i=QT)
        c_xnT = c_xnT.rearrange("p (k n) -> p k n", k=KD)
        c_qT = c_qT.rearrange("p (r n) -> p r n", r=2)
        c_kT = c_kT.rearrange("p (o n) -> p o n", o=2)
        c_v = c_v.rearrange("p (j n) -> p j n", j=QT)
        c_bm = c_bm.rearrange("p (r n) -> p r n", r=2)
        c_sc = c_sc.rearrange("p (r n) -> p r n", r=2)
        c_p = c_p.rearrange("p (r n) -> p r n", r=2)
        c_pT = c_pT.rearrange("p (r n) -> p r n", r=2)
        c_oT = c_oT.rearrange("p (j n) -> p j n", j=NPAIR)
        c_min = c_small[:, 0:6].rearrange("p (r i) -> p r i", r=3)
        c_sum = c_small[:, 6:12].rearrange("p (r i) -> p r i", r=3)
        c_rec = c_small[:, 12:18].rearrange("p (r i) -> p r i", r=3)

        oh16 = sb("oh16", [P, 256], F16)
        inv = sb("inv", [P, 48], U32)
        slots = sb("slots", [P, 2, TT], U32)
        gates = sb("gates", [P, 2, TT])
        len_te = slot_tiles(16) + 1
        tile_expert = sb("tile_expert", [1, len_te], I32)

        ident = sb("ident", [P, P])
        before16 = sb("before16", [P, P], F16)
        ones16 = sb("ones16", [P, P], F16)
        iota_p16 = sb("iota_p16", [P, P], F16)
        iota_t = sb("iota_t", [P, 48])
        iota_128 = sb("iota_128", [P, TT])
        token_id = sb("token_id", [P, 2, TT])
        rank8 = sb("rank8", [P, 16])
        not_first = sb("not_first", [P, 16, TT])
        ones_f = sb("ones_f", [P, P])
        a_wt = sb("a_wt", [P, KD, 8])
        b_wg = sb("b_wg", [P, KD, 8])
        b_bg = sb("b_bg", [P, 8])
        d_gw = sb("d_gw", [P, KD, 16])
        d_eb = sb("d_eb", [P, 16])
        condT = sb("condT", [64, BATCH])
        a_wgT = sb("a_wgT", [64, 8])
        cg = sb("cg", [64, BATCH, 8])
        lg_g = sb("lg_g", [P, BATCH, 8])
        g_in = sb("g_in", [P, KD])
        g_out = sb("g_out", [P, DIM])
        nvb = sb("nvb", [P, DH])
        nv2 = sb("nv2", [P, 1])
        nk2 = sb("nk2", [P, 1])
        nullb = sb("nullb", [P, HEADS])
        mask8 = sb("mask8", [P, BATCH, SEQ], U8)
        stats = sb("stats", [P, TT, 6])
        mv = sb("mv", [P, TT, 2])
        mv2 = sb("mv2", [P, TT, 2])
        rstd = sb("rstd", [P, TT])
        std = sb("std", [P, TT])

        psX = ctx.enter_context(nc.psum_tensor("psX", [P, 512], F32))
        psH = ctx.enter_context(nc.psum_tensor("psH", [P, 2, 512], F32))
        psHT = ctx.enter_context(nc.psum_tensor("psHT", [P, 2, 512], F32))
        psY = ctx.enter_context(nc.psum_tensor("psY", [P, 512], F32))
        psL = ctx.enter_context(nc.psum_tensor("psL", [P, 512], F32))
        psM = ctx.enter_context(nc.psum_tensor("psM", [P, 512], F32))
        router_x = [b[:, 0:DIM].rearrange("p (k n) -> p k n", k=KD) for b in (psX, psY)]
        ffn_x = [b[:, 0:DIM].rearrange("p (k n) -> p k n", k=KD) for b in (psX, psL)]
        ffn_y = [b[:, 0:DIM] for b in (psY, psM)]
        rows_x = psX[:, :].rearrange("p (k i n) -> p k i n", k=KD, i=QT)
        keys_x = psX[:, 0:SEQ]
        values_x = psX[:, SEQ:512].rearrange("p (i n) -> p i n", i=QT)

        y0_dram = nc.dram_tensor("y0_scratch", [TOKENS, DIM], F32, kind="Internal").ap()
        z_dram = nc.dram_tensor("z_scratch", [TOKENS, DIM], F32, kind="Internal").ap()

        def by_tile(dram):
            return dram.rearrange("(t p) d -> t p d", p=P)

        def dram_tile(dram, t):
            return by_tile(dram)[bass.ds(t, 1), :, :].rearrange("o p d -> (o p) d")

        consts_made = sem("consts_made")
        consts_loaded = sem("consts_loaded")
        x_loaded = sem("x_loaded")

        def done_dmas(use, s0, off):
            each = 16 * use.dmas
            return (each // RING) * s0 + each * (off // RING + 1) + use.before[off % RING]

        def wait_dma(eng, use, s0, off):
            eng.wait_ge(use.sems[off % RING], done_dmas(use, s0, off))

        def wait_slot_free(eng, use, s0, off):
            wait(eng, use.sems[off % RING], done_dmas(use, s0, off) - 16 * use.dmas)

        def wait_dmas(eng, use):
            for r in range(RING):
                eng.wait_ge(use.sems[r], use.after[r])

        tokens_loaded, rows_gathered, slots_stored, gathered, tokens_stored = (
            Ring(sem, n) for n in ("tokens_loaded", "rows_gathered", "slots_stored", "gathered", "tokens_stored"))

        def stage(name, experts, src, loads, eps):
            s = Stage(sem, name, experts, src, 16 * loads, eps)
            s.slot_dram = nc.dram_tensor(f"{name}_slots", [s.NT * P, DIM], F32, kind="Internal").ap()
            s.slots_stored = Use(slots_stored, s.NT)
            s.token_ready = sem(f"{name}_token_ready") if name != "a" else None
            s.gathered = Use(gathered, TT, 2)
            s.token_stored = Use(tokens_stored, TT) if name != "a" else None
            s.token_loaded = Use(tokens_loaded, TT) if name == "a" else None
            return s

        def ffn(name, n, hw, hk, kind, st, rows, w_in, w_out, b_in, b_out, shared=False):
            f = Ffn(sem, name, n, hw, hk, kind, st, rows, shared, w_in, w_out, b_in, b_out)
            f.loaded = Use(tokens_loaded if shared else rows_gathered, n)
            f.h_read = f.h_ready if kind == "leaky" else f.h_pre
            return f

        A = stage("a", 8, io["x"], 4, 1e-20)
        B = stage("b", 8, y0_dram, 4, 1e-9)
        D = stage("d", 16, z_dram, 8, 1e-10)
        fA = ffn("af", A.NT, 256, 1, "leaky", st=A, rows=xs,
                 w_in=lambda k, e: a_gu[:, bass.ds(e, 1), k, :].rearrange("p o n -> p (o n)"),
                 w_out=lambda j, e: one(a_down, e), b_in=None, b_out=None)
        fAs = ffn("as", TT, 512, 2, "leaky", st=A, rows=xr, shared=True,
                  w_in=lambda k, e: a_sgu[:, k, :], w_out=lambda j, e: a_sdown[:, j, :], b_in=None, b_out=None)
        fB = ffn("bf", B.NT, 512, 4, "gelu", st=B, rows=xs,
                 w_in=lambda k, e: b_w1[:, bass.ds(e, 1), k, :].rearrange("p o n -> p (o n)"),
                 w_out=lambda j, e: b_w2[:, bass.ds(e, 1), j, :].rearrange("p o n -> p (o n)"),
                 b_in=lambda e: one(b_b1, e), b_out=lambda e: one(b_b2, e))
        fD = ffn("df", D.NT, 256, 1, "silu", st=D, rows=xs,
                 w_in=lambda k, e: d_w13[:, bass.ds(e, 1), k, :].rearrange("p o n -> p (o n)"),
                 w_out=lambda j, e: one(d_w2, e), b_in=lambda e: one(d_b13, e), b_out=lambda e: one(d_b2, e))
        fDs = ffn("ds", TT, 512, 2, "silu", st=D, rows=xr, shared=True,
                  w_in=lambda k, e: d_s13[:, k, :], w_out=lambda j, e: d_s2[:, j, :],
                  b_in=lambda e: d_sb13, b_out=lambda e: d_sb2)
        A.ffn, B.ffn, D.ffn = fA, fB, fD

        def experts_of(eng, f, s0):
            if f.shared:
                return {o: 0 for o in range(-RING, RING)}
            first = 0 if isinstance(s0, int) and s0 == 0 else -RING
            last = RING if not isinstance(s0, int) or s0 + RING <= len_te else 0
            _, values = nc.values_load_multi_w_load_instructions(
                tile_expert[0:1, bass.ds(s0 + first, last - first)], engines=[eng.engine], min_val=0, max_val=f.st.E - 1)
            return {first + n: v for n, v in enumerate(values)}

        def pe_router(pe, st, w, loaded):
            def body(s0, u):
                if live(s0, u, TT):
                    t = s0 + u
                    if loaded:
                        wait_dma(pe, st.token_loaded, s0, u)
                    else:
                        pe.wait_ge(st.token_ready, t + 1)
                    wait(pe, st.tokT_ready, t - 1)
                    for k in range(KD):
                        last = pe.transpose(router_x[u % 2][:, k, :], xr[:, u, k * P:(k + 1) * P], ident[:, :])
                    last.then_inc(st.tok_turned, 1)
                if live(s0, u - 1, TT):
                    t = s0 + (u - 1)
                    pe.wait_ge(st.tokT_ready, t + 1)
                    for k in range(KD):
                        last = pe.matmul(psL[:, bass.ds(t * st.E, st.E)], xrT[:, (u - 1) % 2, k, :], w[:, k, :],
                                         start=(k == 0), stop=(k == KD - 1))
                    last.then_inc(st.logits_done, 1)
            steps(pe, TT, body, 0, 1)

        def pe_route(pe, st):
            n = TT * st.E
            pe.wait_ge(st.onehot_ready, 1)
            oh_et = oh16[:, 0:n].rearrange("p (t e) -> p e t", e=st.E)
            pe.matmul(psM[:, 0:n], before16[:, :], oh_et, start=True, stop=True)
            pe.matmul(psM[:, 256:256 + n], ones16[:, :], oh_et, start=True, stop=True).then_inc(st.prefix_done, 1)
            eq = eq_tile[:, 0:2 * TT * st.NT].rearrange("p (k a) -> p k a", a=st.NT)

            def body(s0, u):
                k = s0 + u
                pe.wait_ge(st.eqrow_ready, k + 1)
                first = isinstance(k, int) and k == 0
                final = isinstance(k, int) and k == 2 * TT - 1
                mm = pe.matmul(psL[:, 0:st.NT], eq_row[:, u, :], one(eq, k), start=first, stop=final)
                mm.then_inc(st.inv_done if final else st.eqrow_used, 1)
            for k in range(RING):
                body(0, k)
            with pe.Fori(1, 2 * TT // RING - 1) as i:
                for u in range(RING):
                    body(i * RING, u)
            for k in range(RING):
                body(2 * TT - RING, k)

        def pe_ffn(pe, f):
            held = {}

            def body(s0, u):
                if u == 0:
                    held["e"] = experts_of(pe, f, s0)
                if live(s0, u + 1, f.n):
                    r, t = (u + 1) % RING, s0 + (u + 1)
                    wait_dma(pe, f.loaded, s0, u + 1)
                    wait(pe, f.xT_ready, t - 1)
                    for k in range(KD):
                        last = pe.transpose(ffn_x[r % 2][:, k, :], f.rows[:, r, k * P:(k + 1) * P], ident[:, :])
                    last.then_inc(f.turned, 1)
                if live(s0, u, f.n):
                    t, h = s0 + u, u % 2
                    e = held["e"][u]
                    pe.wait_ge(f.xT_ready, t + 1)
                    wait(pe, f.h_read, t - 1)
                    for k in range(KD):
                        last = pe.matmul(psH[:, h, 0:f.hw], xT[:, h, k, :], f.w_in(k, e),
                                         start=(k == 0), stop=(k == KD - 1))
                    last.then_inc(f.h_mm, 1)
                if live(s0, u - 1, f.n):
                    t, h = s0 + (u - 1), (u - 1) % 2
                    pe.wait_ge(f.h_ready, t + 1)
                    wait(pe, f.hT_ready, t - 1)
                    for j in range(f.hk):
                        last = pe.transpose(psHT[:, h, j * P:(j + 1) * P], hbuf[:, h, j * P:(j + 1) * P], ident[:, :])
                    last.then_inc(f.h_turned, 1)
                if live(s0, u - 2, f.n):
                    t, h = s0 + (u - 2), u % 2
                    e = held["e"][u - 2]
                    pe.wait_ge(f.hT_ready, t + 1)
                    wait(pe, f.y_out, t - 1)
                    for j in range(f.hk):
                        last = pe.matmul(ffn_y[h], hT[:, h, j * P:(j + 1) * P], f.w_out(j, e),
                                         start=(j == 0), stop=(j == f.hk - 1))
                    last.then_inc(f.y_mm, 1)
            wait_dma(pe, f.loaded, 0, 0)
            for k in range(KD):
                last = pe.transpose(ffn_x[0][:, k, :], f.rows[:, 0, k * P:(k + 1) * P], ident[:, :])
            last.then_inc(f.turned, 1)
            steps(pe, f.n, body, 1, 2)

        def act_router(act, st):
            def body(s0, u):
                t = s0 + u
                act.wait_ge(st.tok_turned, t + 1)
                wait(act, st.logits_done, t - 1)
                nc.scalar.copy(xrT[:, u % 2, :, :], router_x[u % 2]).then_inc(st.tokT_ready, 1)
            steps(act, TT, body, 0, 0)

        def act_ffn(act, f):
            def copy_x(s0, o):
                t, h = s0 + o, o % 2
                act.wait_ge(f.turned, t + 1)
                wait(act, f.h_mm, t - 1)
                nc.scalar.copy(xT[:, h, :, :], ffn_x[h]).then_inc(f.xT_ready, 1)

            def body(s0, u):
                if live(s0, u + 1, f.n):
                    copy_x(s0, u + 1)
                if live(s0, u, f.n) and f.kind == "leaky":
                    t, h = s0 + u, u % 2
                    act.wait_ge(f.h_mm, t + 1)
                    wait(act, f.h_turned, t - 1)
                    nc.scalar.mul(hbuf[:, h, 0:f.hw // 2], psH[:, h, 0:f.hw // 2], 0.01).then_inc(f.h_pre, 1)
                elif live(s0, u, f.n):
                    t, h = s0 + u, u % 2
                    act.wait_ge(f.h_pre, t + 1)
                    if f.kind == "gelu":
                        nc.scalar.activation(hbuf[:, h, :], hbuf[:, h, :], ACT.Gelu).then_inc(f.h_ready, 1)
                    else:
                        m = f.hw // 2
                        nc.scalar.activation(hbuf[:, h, 0:m], hbuf[:, h, 0:m], ACT.Silu).then_inc(f.h_gate, 1)
                if live(s0, u - 1, f.n):
                    t, h = s0 + (u - 1), (u - 1) % 2
                    act.wait_ge(f.h_turned, t + 1)
                    wait(act, f.y_mm, t - 1)
                    nc.scalar.copy(hT[:, h, 0:f.hk * P], psHT[:, h, 0:f.hk * P]).then_inc(f.hT_ready, 1)
            copy_x(0, 0)
            steps(act, f.n, body, 1, 2)

        def dve_ffn(dve, f):
            m = f.hw // 2
            held = {}

            def body(s0, u):
                if u == 0 and f.b_in is not None:
                    held["e"] = experts_of(dve, f, s0)
                if live(s0, u, f.n):
                    t, h = s0 + u, u % 2
                    if f.b_in is not None:
                        e = held["e"][u]
                    dve.wait_ge(f.h_mm, t + 1)
                    wait(dve, f.h_turned, t - 1)
                    if f.kind == "leaky":
                        dve.wait_ge(f.h_pre, t + 1)
                        nc.vector.tensor_tensor(hbuf[:, h, 0:m], hbuf[:, h, 0:m], psH[:, h, 0:m], ALU.max
                                                ).then_inc(f.h_gate, 1)
                        dve.wait_ge(f.h_gate, t + 1)
                        nc.vector.tensor_tensor(hbuf[:, h, 0:m], hbuf[:, h, 0:m], psH[:, h, m:2 * m], ALU.mult
                                                ).then_inc(f.h_ready, 1)
                    else:
                        nc.vector.tensor_tensor(hbuf[:, h, 0:f.hw], psH[:, h, 0:f.hw], f.b_in(e), ALU.add
                                                ).then_inc(f.h_pre, 1)
                if live(s0, u - 2, f.n):
                    t, r = s0 + (u - 2), (u - 2) % RING
                    if f.b_out is not None:
                        e = held["e"][u - 2]
                    dve.wait_ge(f.y_mm, t + 1)
                    if f.shared:
                        dst = one(acc[:, :, :], t)
                    else:
                        wait_slot_free(dve, f.st.slots_stored, s0, u - 2)
                        dst = ys[:, r, :]
                    if f.b_out is None:
                        nc.vector.tensor_copy(dst, ffn_y[u % 2]).then_inc(f.y_out, 1)
                    else:
                        nc.vector.tensor_tensor(dst, ffn_y[u % 2], f.b_out(e), ALU.add).then_inc(f.y_out, 1)
                if live(s0, u, f.n) and f.kind == "silu":
                    t, h = s0 + u, u % 2
                    dve.wait_ge(f.h_gate, t + 1)
                    nc.vector.tensor_tensor(hbuf[:, h, 0:m], hbuf[:, h, 0:m], hbuf[:, h, m:2 * m], ALU.mult
                                            ).then_inc(f.h_ready, 1)
            steps(dve, f.n, body, 1, 2)

        def dve_route(dve, st):
            E, NT, n = st.E, st.NT, TT * st.E
            count = [0]

            def done(ins):
                count[0] += 1
                ins.then_inc(st.route_step, 1)
                dve.wait_ge(st.route_step, count[0])

            def te(ap):
                return ap[:, 0:n].rearrange("p (t e) -> p t e", e=E)

            def et(ap):
                return ap[:, 0:n].rearrange("p (e t) -> p e t", e=E)

            def as_te(ap):
                return ap[:, 0:n].rearrange("p (e t) -> p t e", e=E)

            def per_token(ap):
                return ap.unsqueeze(2).to_broadcast([P, TT, E])

            v = nc.vector
            lg, key, tmp, oh1, oh2, sc = (te(a) for a in (rt_lg, rt_key, rt_tmp, rt_oh1, rt_oh2, rt_sc))
            best, w1, w2, den = (rt_small[:, i * TT:(i + 1) * TT] for i in range(4))
            c_e, nt_e, end_e, base_e = (rt_small[:, 64 + i * 16:64 + i * 16 + E] for i in range(4))
            half = rt_small[:, 128:160]
            row_f = rt_small[:, 160:192]
            slot_f = rt_small[:, 192:224]
            dve.wait_ge(st.logits_done, TT)
            lps = psL[:, 0:n].rearrange("p (t e) -> p t e", e=E)
            if st is A:
                dve.wait_ge(st.weights_loaded, st.loads)
                lb = lg.rearrange("p (b i) e -> p b i e", i=QT)
                pb = psL[:, 0:n].rearrange("p (b i e) -> p b i e", i=QT, e=E)
                for i in range(QT):
                    done(v.tensor_tensor(lb[:, :, i, :], pb[:, :, i, :], lg_g[:, :, :], ALU.add))
            elif st is B:
                done(v.tensor_tensor(lg, lps, b_bg[:, :].unsqueeze(1).to_broadcast([P, TT, E]), ALU.add))
            else:
                v.tensor_copy(lg, lps).then_inc(st.exp_wanted, 1)
                dve.wait_ge(st.exp_wanted, 1)
                done(v.tensor_tensor(key, lg, d_eb[:, :].unsqueeze(1).to_broadcast([P, TT, E]), ALU.add))
            if st is not D:
                done(v.tensor_reduce(best, lg, AX_X, ALU.max))
                v.tensor_tensor(lg, lg, per_token(best), ALU.subtract).then_inc(st.exp_wanted, 1)
                dve.wait_ge(st.exp_done, 1)
                done(v.tensor_reduce(den, sc, AX_X, ALU.add))
                done(v.reciprocal(den, den))
                done(v.tensor_tensor(sc, sc, per_token(den), ALU.mult))
                key = sc
            rank = rank8[:, 16 - E:16].unsqueeze(1).to_broadcast([P, TT, E])
            for oh, w in ((oh1, w1), (oh2, w2)):
                done(v.tensor_reduce(best, key, AX_X, ALU.max))
                done(v.tensor_tensor(tmp, key, per_token(best), ALU.is_equal))
                done(v.tensor_tensor(tmp, tmp, rank, ALU.mult))
                done(v.tensor_reduce(den, tmp, AX_X, ALU.max))
                done(v.tensor_tensor(oh, tmp, per_token(den), ALU.is_equal))
                if st is D:
                    if oh is oh1:
                        dve.wait_ge(st.exp_done, 1)
                    done(v.tensor_tensor(tmp, oh, sc, ALU.mult))
                    done(v.tensor_reduce(w, tmp, AX_X, ALU.add))
                else:
                    done(v.tensor_copy(w, best))
                if oh is oh1:
                    done(v.scalar_tensor_tensor(out=te(rt_key), in0=oh, scalar=LOWEST, in1=key, op0=ALU.mult, op1=ALU.add))
                    key = te(rt_key)
            v.tensor_tensor(oh16[:, 0:n].rearrange("p (t e) -> p t e", e=E), oh1, oh2, ALU.add).then_inc(st.onehot_ready, 1)
            done(v.tensor_tensor(den, w1, w2, ALU.add))
            done(v.tensor_scalar(den, den, st.eps, None, ALU.add))
            done(v.reciprocal(den, den))
            v.tensor_tensor(gates[:, 0, :], w1, den, ALU.mult)
            done(v.tensor_tensor(gates[:, 1, :], w2, den, ALU.mult))
            dve.wait_ge(st.prefix_done, 1)
            within, total = et(psM[:, 0:256]), et(psM[:, 256:512])
            incl = rt_lg[:, 0:n]
            done(v.tensor_tensor_scan(incl, not_first[:, 0:E, :].rearrange("p e t -> p (e t)"), psM[:, 256:256 + n],
                                      0.0, ALU.mult, ALU.add))
            incl = et(rt_lg)
            done(v.tensor_copy(c_e, incl[:, :, TT - 1:TT].rearrange("p e o -> p (e o)")))
            done(v.tensor_tensor(et(rt_tmp), c_e.unsqueeze(2).to_broadcast([P, E, TT]),
                                 iota_128[:, :].unsqueeze(1).to_broadcast([P, E, TT]), ALU.is_gt))
            done(v.tensor_reduce(nt_e, et(rt_tmp), AX_X, ALU.add))
            done(v.tensor_tensor_scan(end_e, ones_f[:, 0:E], nt_e, 0.0, ALU.mult, ALU.add))
            done(v.tensor_tensor(base_e, end_e, nt_e, ALU.subtract))
            done(v.tensor_scalar(base_e, base_e, float(P), None, ALU.mult))
            done(v.tensor_tensor(et(rt_pos), incl, total, ALU.subtract))
            done(v.tensor_tensor(et(rt_pos), et(rt_pos), within, ALU.add))
            done(v.tensor_tensor(et(rt_pos), et(rt_pos), base_e.unsqueeze(2).to_broadcast([P, E, TT]), ALU.add))
            for c, oh in enumerate((oh1, oh2)):
                done(v.tensor_tensor(tmp, oh, as_te(rt_pos), ALU.mult))
                done(v.tensor_reduce(slot_f[:, c * TT:(c + 1) * TT], tmp, AX_X, ALU.add))
            slot_i = slots[:, :, :].rearrange("p c t -> p (c t)")
            done(v.tensor_copy(slot_i, slot_f))
            hi = half.bitcast(I32)
            done(v.tensor_scalar(hi, slot_i.bitcast(I32), P - 1, None, ALU.bitwise_and))
            done(v.tensor_copy(row_f, hi))
            done(v.tensor_scalar(hi, slot_i.bitcast(I32), 7, None, ALU.logical_shift_right))
            done(v.tensor_copy(slot_f, hi))
            eq = eq_tile[:, 0:2 * TT * NT].rearrange("p (k a) -> p k a", a=NT)
            done(v.tensor_tensor(eq, slot_f.unsqueeze(2).to_broadcast([P, 2 * TT, NT]),
                                 iota_t[:, 0:NT].unsqueeze(1).to_broadcast([P, 2 * TT, NT]), ALU.is_equal))
            tok = token_id[:, :, :].rearrange("p c t -> p (c t)")

            def body(s0, u):
                k = s0 + u
                wait(dve, st.eqrow_used, k - RING + 1)
                nc.vector.tensor_scalar(eq_row[:, u, :], iota_p16[:, :], row_f[:, bass.ds(k, 1)], tok[:, bass.ds(k, 1)],
                                        ALU.is_equal, ALU.mult).then_inc(st.eqrow_ready, 1)
            steps(dve, 2 * TT, body, 0, 0)
            cmp = rt_tmp[0:1, :]
            spare = rt_pos[0:1, 0:len_te]
            for a in range(0, len_te, TT):
                w = TT
                c3 = cmp[:, 0:w * E].rearrange("p (t e) -> p t e", e=E)
                done(v.tensor_tensor(c3, end_e[0:1, :].unsqueeze(1).to_broadcast([1, w, E]),
                                     iota_t[0:1, a:a + w].unsqueeze(2).to_broadcast([1, w, E]), ALU.is_le))
                done(v.tensor_reduce(spare[:, a:a + w], c3, AX_X, ALU.add))
            done(v.tensor_scalar(spare, spare, float(E - 1), None, ALU.min))
            done(v.tensor_copy(tile_expert[0:1, :], spare))
            dve.wait_ge(st.inv_done, 1)
            v.tensor_copy(inv[:, 0:NT], psL[:, 0:NT]).then_inc(st.routed, 1)

        def act_route(act, st):
            n = TT * st.E
            act.wait_ge(st.exp_wanted, 1)
            act_f, scale = {"a": (ACT.Exp, 0.5), "b": (ACT.Exp, 0.2), "d": (ACT.Sigmoid, 1.0)}[st.name]
            nc.scalar.activation(rt_sc[:, 0:n], rt_lg[:, 0:n], act_f, scale=scale).then_inc(st.exp_done, 1)

        def pool_gather_rows(pool, st):
            f = st.ffn
            pool.wait_ge(st.routed, 1)
            if st is not A:
                wait_dmas(pool, st.token_stored)
            for t in range(f.n):
                wait(pool, f.turned, t - RING + 1)
                pool.indirect_dma_start(out=xs[:, t % RING, :], out_offset=None, in_=st.src,
                                        in_offset=bass.IndirectOffsetOnAxis(ap=inv[:, t:t + 1], axis=0)
                                        ).then_inc(f.loaded.sems[t % RING], 16)

        def pool_gather_results(pool, st):
            wait_dmas(pool, st.slots_stored)
            for t in range(TT):
                wait(pool, st.combined, t - RING + 1)
                for c in range(2):
                    pool.indirect_dma_start(out=gat[:, t % RING, c, :], out_offset=None, in_=st.slot_dram,
                                            in_offset=bass.IndirectOffsetOnAxis(ap=slots[:, c, t:t + 1], axis=0)
                                            ).then_inc(st.gathered.sems[t % RING], 16)

        def sp_store_slots(sp, f):
            def body(s0, u):
                t = s0 + u
                sp.wait_ge(f.y_out, t + 1)
                sp.dma_start(dram_tile(f.st.slot_dram, t), ys[:, u, :]).then_inc(f.st.slots_stored.sems[u], 16)
            steps(sp, f.n, body, 0, 0)

        def sp_load_tokens(sp, src, loaded, used):
            def body(s0, u):
                t = s0 + u
                wait(sp, used, t - RING + 1)
                sp.dma_start(xr[:, u, :], dram_tile(src, t)).then_inc(loaded.sems[u], 16)
            steps(sp, TT, body, 0, 0)

        def sp_store_tokens(sp, dst, st):
            def body(s0, u):
                t = s0 + u
                sp.wait_ge(st.token_ready, t + 1)
                sp.dma_start(dram_tile(dst, t), xr[:, u, :]).then_inc(st.token_stored.sems[u], 16)
            steps(sp, TT, body, 0, 0)

        C = Attention(sem, 16 * 6)


        def pe_q(pe, pair, j, b):
            if j == 0:
                pe.wait_ge(C.xnT_ready, 2 * b + 2)
            wait(pe, C.qT_ready, pair)
            for k in range(KD):
                last = pe.matmul(psY[:, 0:SEQ], c_wq[:, k, j * P:(j + 1) * P], c_xnT[:, k, :],
                                 start=(k == 0), stop=(k == KD - 1))
            last.then_inc(C.q_mm, 1)

        def pe_scores(pe, g, h, b):
            pe.wait_ge(C.qT_ready, 8 * b + h // 2 + 1)
            if h == 0:
                pe.wait_ge(C.kT_ready, 2 * b + 2)
            wait(pe, C.score_ready, g - 1)
            q = c_qT[:, (h // 2) % 2, :]
            pe.matmul(psH[:, h % 2, 0:KEYS0], q[:, 0:P], c_kT[:, h % 2, 0:KEYS0], start=True, stop=True)
            pe.matmul(psH[:, h % 2, KEYS0:KEYS], q[:, P:2 * P], c_kT[:, h % 2, :], start=True, stop=True
                      ).then_inc(C.s_mm, 1)

        def pe_turn(pe, g, h):
            pe.wait_ge(C.pn_ready, g + 1)
            wait(pe, C.pT_ready, g - 1)
            for n, at in enumerate((1, KEYS0 + 1, KEYS0 + 1 + P)):
                last = pe.transpose(psHT[:, h % 2, n * P:(n + 1) * P], c_p[:, h % 2, at:at + P], ident[:, :])
            last.then_inc(C.p_turned, 1)

        def pe_sum(pe, pair, j, b):
            pe.wait_ge(C.pT_ready, 2 * pair + 2)
            if j == 0:
                pe.wait_ge(C.v_ready, b + 1)
            wait(pe, C.o_ready, pair)
            for n, keys, queries in ((0, 0, slice(0, SEQ)), (1, 1, slice(P, SEQ))):
                at = slice(n * SEQ, n * SEQ + queries.stop - queries.start)
                for o in range(2):
                    last = pe.matmul(psL[DH * o:DH * o + DH, queries], c_v[:, keys, :], c_pT[:, o, at],
                                     start=(n == 0), stop=(n == 1))
            last.then_inc(C.pv_mm, 1)

        def pe_out(pe, b):
            pe.wait_ge(C.o_ready, 8 * b + 8)
            wait(pe, C.ao_ready, b)
            wait(pe, C.ao_stat, 2 * b)
            for i in range(QT):
                for j in range(NPAIR):
                    last = pe.matmul(psM[:, i * DIM:(i + 1) * DIM], c_oT[:, j, i * P:(i + 1) * P], c_wo[:, j, :],
                                     start=(j == 0), stop=(j == NPAIR - 1))
            last.then_inc(C.wo_mm, 1)

        def pe_rows(pe, b):
            pe.wait_ge(C.xn_ready, 2 * b + 2)
            wait(pe, C.v_ready, b)
            for i in range(QT):
                for k in range(KD):
                    last = pe.transpose(rows_x[:, k, i, :], c_xn[:, i, k * P:(k + 1) * P], ident[:, :])
            last.then_inc(C.xn_turned, 1)

        def pe_kv(pe, b):
            pe.wait_ge(C.xnT_ready, 2 * b + 2)
            for k in range(KD):
                pe.matmul(keys_x, c_wkk[:, k, :], c_xnT[:, k, :],
                          start=(k == 0), stop=(k == KD - 1))
            for i in range(QT):
                for k in range(KD):
                    last = pe.matmul(values_x[:, i, :], c_xnT[:, k, i * P:(i + 1) * P], c_wvv[:, k, :],
                                     start=(k == 0), stop=(k == KD - 1))
            last.then_inc(C.kv_mm, 1)

        def pe_batch(pe, b, first, last):
            for h in range(HEADS):
                g = 16 * b + h
                if not (last and h >= 14):
                    pe_scores(pe, g + 2, (h + 2) % HEADS, b + (h + 2) // HEADS)
                if h % 2 == 1 and not (last and h >= 13):
                    j = (h + 3) // 2
                    pe_q(pe, 8 * b + j, j % NPAIR, b + j // NPAIR)
                if h == 1 and not first:
                    pe_out(pe, b - 1)
                if h % 2 == 0 and h > 0:
                    pe_sum(pe, 8 * b + h // 2 - 1, h // 2 - 1, b)
                elif h == 0 and not first:
                    pe_sum(pe, 8 * b - 1, NPAIR - 1, b - 1)
                if h == 11 and not last:
                    pe_rows(pe, b + 1)
                if h == 12 and not last:
                    pe_kv(pe, b + 1)
                pe_turn(pe, g, h)

        def batches(eng, batch):
            batch(eng, 0, True, False)
            with eng.Fori(1, BATCH - 1) as b:
                batch(eng, b, False, False)
            batch(eng, BATCH - 1, False, True)

        def pe_attention(pe):
            pe.wait_ge(C.kT_fixed, 4)
            pe_rows(pe, 0)
            pe_kv(pe, 0)
            pe_q(pe, 0, 0, 0)
            pe_q(pe, 1, 1, 0)
            pe_scores(pe, 0, 0, 0)
            pe_scores(pe, 1, 1, 0)
            batches(pe, pe_batch)
            pe_sum(pe, NPAIR * BATCH - 1, NPAIR - 1, BATCH - 1)
            pe_out(pe, BATCH - 1)

        def act_rowsT(act, b):
            act.wait_ge(C.xn_turned, b + 1)
            wait(act, C.q_mm, 8 * b)
            wait(act, C.kv_mm, b)
            for k in range(KD):
                nc.scalar.activation(c_xnT[:, k, :], rows_x[:, k, :, :].rearrange("p i n -> p (i n)"), ACT.Identity,
                                     scale=g_in[:, k:k + 1]).then_inc(C.xnT_ready, 1)

        def act_mask(act, b):
            wait(act, C.bm_ready, 16 * b)
            m = mask8[:, bass.ds(b, 1), :].rearrange("p o n -> p (o n)")
            for dst, src in ((c_mp[:, 1:KEYS0], m[:, 0:P]), (c_mp[:, KEYS0 + 1:KEYS], m)):
                nc.scalar.activation(dst, src, ACT.Copy, scale=-HIDDEN_KEY, bias=HIDDEN_KEY).then_inc(C.mask_ready, 1)

        def act_q(act, pair, j):
            act.wait_ge(C.q_mm, pair + 1)
            wait(act, C.s_mm, 2 * pair - 2)
            nc.scalar.mul(c_qT[:, j % 2, :], psY[:, 0:SEQ], -(float(DH) ** -0.5)).then_inc(C.qT_ready, 1)

        def act_exp(act, g, h):
            act.wait_ge(C.score_ready, g + 1)
            wait(act, C.p_turned, g - 1)
            for i, (a, z) in enumerate(((0, KEYS0), (KEYS0, KEYS))):
                nc.scalar.activation(c_p[:, h % 2, a:z], c_sc[:, h % 2, a:z], ACT.Exp, scale=-1.0,
                                     bias=c_min[:, h % 2, i:i + 1], accum_out=c_sum[:, h % 2, i:i + 1]
                                     ).then_inc(C.p_ready, 1)

        def act_o(act, pair, j, b):
            act.wait_ge(C.pv_mm, pair + 1)
            if j == 0:
                wait(act, C.wo_mm, b)
            nc.scalar.activation(c_oT[:, j, :], psL[:, 0:SEQ], ACT.Identity, bias=nv2[:, 0:1]).then_inc(C.o_ready, 1)

        def act_out(act, b):
            act.wait_ge(C.wo_mm, b + 1)
            nc.scalar.copy(acc[:, bass.ds(2 * b, 2), :].rearrange("p i n -> p (i n)"), psM[:, :]).then_inc(C.ao_ready, 1)

        def act_batch(act, b, first, last):
            for h in range(HEADS):
                g = 16 * b + h
                if h % 2 == 1 and not (last and h >= 13):
                    j = (h + 3) // 2
                    act_q(act, 8 * b + j, j % NPAIR)
                if not (last and h >= 14):
                    act_exp(act, g + 2, (h + 2) % HEADS)
                if h == 11 and not last:
                    act_rowsT(act, b + 1)
                if h == 13 and not last:
                    act_mask(act, b + 1)
                if h == 2 and not first:
                    act_out(act, b - 1)
                if h % 2 == 0 and h > 0:
                    act_o(act, 8 * b + h // 2 - 1, h // 2 - 1, b)
                elif h == 0 and not first:
                    act_o(act, 8 * b - 1, NPAIR - 1, b - 1)

        def act_attention(act):
            act.wait_ge(C.var_done, 1)
            nc.scalar.activation(std[:, :], rstd[:, :], ACT.Sqrt).then_inc(C.std_done, 1)
            act_rowsT(act, 0)
            act.wait_ge(B.combined, TT)
            act_mask(act, 0)
            act_q(act, 0, 0)
            act_q(act, 1, 1)
            act_exp(act, 0, 0)
            act_exp(act, 1, 1)
            batches(act, act_batch)
            act_o(act, 8 * BATCH - 1, NPAIR - 1, BATCH - 1)
            act_out(act, BATCH - 1)
            act.wait_ge(C.var_done, 2)
            nc.scalar.activation(std[:, :], rstd[:, :], ACT.Sqrt).then_inc(C.std_done, 1)

        def dve_rows(dve, b):
            wait(dve, C.xn_turned, b)
            for i in range(QT):
                t = 2 * b + i
                nc.vector.tensor_scalar(c_xn[:, i, :], one(x2[:, :, :], t), mv[:, bass.ds(t, 1), 0:1].rearrange("p a b -> p (a b)"),
                                        rstd[:, bass.ds(t, 1)], ALU.subtract, ALU.mult).then_inc(C.xn_ready, 1)

        def dve_k(dve, b):
            dve.wait_ge(C.kv_mm, b + 1)
            wait(dve, C.s_mm, 16 * b)
            for o in range(2):
                half = slice(DH * o, DH * o + DH)
                nc.vector.tensor_copy(c_kT[half, o, 1:KEYS1], keys_x[half, :]
                                      ).then_inc(C.kT_ready, 1)

        def dve_v(dve, b):
            dve.wait_ge(C.kv_mm, b + 1)
            wait(dve, C.pv_mm, 8 * b)
            nc.vector.tensor_tensor(c_v, values_x[:, :, 0:DH], nvb[:, :].unsqueeze(1).to_broadcast([P, QT, DH]), ALU.subtract
                                    ).then_inc(C.v_ready, 1)

        def dve_scores(dve, g, h):
            for i, (a, z) in enumerate(((0, KEYS0), (KEYS0, KEYS))):
                last = nc.vector.tensor_tensor_reduce(c_sc[:, h % 2, a:z], psH[:, h % 2, a:z], c_bm[:, h % 2, a:z], 1.0, -LOWEST,
                                                      ALU.add, ALU.min, c_min[:, h % 2, i:i + 1])
            last.then_inc(C.score_ready, 1)

        def dve_scores_wait(dve, g):
            dve.wait_ge(C.s_mm, g + 1)
            dve.wait_ge(C.bm_ready, g + 1)

        def dve_sums(dve, g, h):
            dve.wait_ge(C.p_ready, 2 * g + 2)
            nc.vector.reciprocal(c_rec[:, h % 2, :], c_sum[:, h % 2, :]).then_inc(C.rec_ready, 1)

        def dve_norm(dve, g, h):
            dve.wait_ge(C.rec_ready, g + 1)
            nc.vector.tensor_scalar(c_p[:, h % 2, 1:KEYS0], c_p[:, h % 2, 1:KEYS0], c_rec[:, h % 2, 0:1], None, ALU.mult)
            own = c_p[:, h % 2, KEYS0 + 1:KEYS]
            nc.vector.tensor_scalar(own, own, c_rec[:, h % 2, 1:2], None, ALU.mult).then_inc(C.pn_ready, 1)

        def dve_pT(dve, g, h, b):
            dve.wait_ge(C.p_turned, g + 1)
            if h % 2 == 0:
                wait(dve, C.pv_mm, 8 * b + h // 2)
            nc.vector.tensor_copy(c_pT[:, h % 2, :], psHT[:, h % 2, 0:3 * P]).then_inc(C.pT_ready, 1)

        def dve_ao_stats(dve, b):
            for i in range(QT):
                nc.vector.bn_stats(stats[:, bass.ds(2 * b + i, 1), :].rearrange("p a n -> p (a n)"),
                                   psM[:, i * DIM:(i + 1) * DIM]).then_inc(C.ao_stat, 1)


        def dve_batch(dve, b, first, last):
            for h in range(HEADS):
                g = 16 * b + h
                if h == 10 and not last:
                    dve_rows(dve, b + 1)
                if h == 14 and not last:
                    dve_k(dve, b + 1)
                if h == 4 and not first:
                    dve.wait_ge(C.ao_ready, b)
                if not (last and h >= 14):
                    dve_scores_wait(dve, g + 2)
                if not (last and h >= 15):
                    dve_sums(dve, g + 1, (h + 1) % HEADS)
                if not (last and h >= 14):
                    dve_scores(dve, g + 2, (h + 2) % HEADS)
                if h == 4 and not first:
                    dve_ao_stats(dve, b - 1)
                dve_pT(dve, g, h, b)
                if not (last and h >= 15):
                    dve_norm(dve, g + 1, (h + 1) % HEADS)
                if h == 0 and not first:
                    dve_v(dve, b)

        def dve_rstd(dve, mom, n):
            for t in range(TT):
                last = nc.vector.bn_aggr(mom[:, t, :], stats[:, t, :])
            last.then_inc(C.mom_done, 1)
            dve.wait_ge(C.mom_done, n)
            nc.vector.tensor_scalar(rstd[:, :], mom[:, :, 1:2].rearrange("p t o -> p (t o)"), 1e-5, None, ALU.add
                                    ).then_inc(C.var_done, 1)
            dve.wait_ge(C.std_done, n)
            nc.vector.reciprocal(rstd[:, :], std[:, :]).then_inc(C.rstd_done, 1)
            dve.wait_ge(C.rstd_done, n)

        def dve_attention(dve):
            dve.wait_ge(C.stat, TT)
            dve_rstd(dve, mv, 1)
            nc.vector.memset(c_kT[DH:P, 0, :], 0.0).then_inc(C.kT_fixed, 1)
            nc.vector.memset(c_kT[0:DH, 1, :], 0.0).then_inc(C.kT_fixed, 1)
            nc.vector.tensor_copy(c_kT[0:DH, 0, 0:1], nk2[0:DH, :]).then_inc(C.kT_fixed, 1)
            nc.vector.tensor_copy(c_kT[DH:P, 1, 0:1], nk2[DH:P, :]).then_inc(C.kT_fixed, 1)
            dve_rows(dve, 0)
            dve_k(dve, 0)
            dve_v(dve, 0)
            for g in range(2):
                dve_scores_wait(dve, g)
                dve_scores(dve, g, g)
            dve_sums(dve, 0, 0)
            dve_norm(dve, 0, 0)
            batches(dve, dve_batch)
            dve.wait_ge(C.ao_ready, BATCH)
            dve_ao_stats(dve, BATCH - 1)
            dve.wait_ge(C.ao_stat, TT)
            dve_rstd(dve, mv2, 2)

        def pool_bm(pool, b, g, h):
            if h == 0:
                pool.wait_ge(C.mask_ready, 2 * b + 2)
            wait(pool, C.score_ready, g - 1)
            pool.tensor_tensor(c_bm[:, h % 2, :], c_mp, c_bias[:, h, :], ALU.subtract).then_inc(C.bm_ready, 1)

        def pool_batch(pool, b, first, last):
            for h in range(HEADS):
                g = 16 * b + h
                if not (last and h >= 14):
                    pool_bm(pool, b + (h + 2) // HEADS, g + 2, (h + 2) % HEADS)

        def pool_attention(pool):
            pool.wait_ge(C.loaded, C.loads)
            pool.wait_ge(B.combined, TT)
            for a in (0, KEYS0):
                pool.tensor_copy(c_bias[:, :, a:a + 1].rearrange("p h o -> p (h o)"), nullb[:, :]).then_inc(C.bias_ready, 1)
                pool.memset(c_mp[:, a:a + 1], 0.0).then_inc(C.bias_ready, 1)
            for a in (1, KEYS0 + 1 + P):
                own = c_bias[:, :, a:a + P]
                pool.affine_select(out=own, in_=own, compare_op=ALU.is_ge, fill=-HIDDEN_KEY, base=0,
                                   pattern=[[0, HEADS], [-1, P]], channel_multiplier=1).then_inc(C.bias_ready, 1)
            pool.wait_ge(C.bias_ready, 6)
            pool_bm(pool, 0, 0, 0)
            pool_bm(pool, 0, 1, 1)
            batches(pool, pool_batch)

        def dve_combine(dve, st, tile):
            def body(s0, u):
                t = s0 + u
                wait_dma(dve, st.gathered, s0, u)
                tile(s0, u, t)
            steps(dve, TT, body, 0, 0)

        def weighted(st, c, u, t, dst, base):
            return nc.vector.scalar_tensor_tensor(out=dst, in0=gat[:, u, c, :], scalar=gates[:, c, bass.ds(t, 1)], in1=base,
                                                  op0=ALU.mult, op1=ALU.add)

        block = ctx.enter_context(nc.Block())

        out_stored = Use(tokens_stored, TT)

        @block.sync
        def _(sp):
            sp_load_tokens(sp, io["x"], A.token_loaded, A.tok_turned)
            sp.wait_ge(A.tok_turned, TT)
            sp_load_tokens(sp, io["x"], fAs.loaded, fAs.turned)
            sp_store_slots(sp, fA)
            sp_store_tokens(sp, y0_dram, B)
            sp_store_slots(sp, fB)
            sp_store_tokens(sp, z_dram, D)
            wait_dmas(sp, D.token_stored)
            sp.wait_ge(D.tok_turned, TT)
            sp_load_tokens(sp, z_dram, fDs.loaded, fDs.turned)
            sp_store_slots(sp, fD)

            def store_out(s0, u):
                sp.wait_ge(D.combined, s0 + u + 1)
                sp.dma_start(dram_tile(io["out"], s0 + u), xr[:, u, :]).then_inc(out_stored.sems[u], 16)
            steps(sp, TT, store_out, 0, 0)
            wait_dmas(sp, D.slots_stored)
            wait_dmas(sp, out_stored)

        small = [(a_wt, "a_wt"), (condT, "condT"), (a_wgT, "a_wgT"), (b_wg, "b_wg"), (d_gw, "d_gw"), (g_in, "g_in"),
                 (nv2, "nv2"), (nk2, "nk2")]
        spread = [(b_bg, "b_bg"), (d_eb, "d_eb"), (g_out, "g_out"), (nvb, "nvb"), (nullb, "nullb"), (mask8, "mask")]

        def load_all(act, pairs, s):
            for dst, name in pairs:
                act.dma_start(dst[:], io[name]).then_inc(s, 16)

        @block.scalar
        def _(act):
            load_all(act, small, consts_loaded)
            for dst, name in spread:
                ap = dst[:, :, :].rearrange("p b s -> p (b s)") if dst is mask8 else dst[:, :]
                act.dma_start(ap, io[name].to_broadcast([P, io[name].shape[1]])).then_inc(consts_loaded, 16)
            for dst, name in ((a_sgu, "a_sgu"), (a_sdown, "a_sdown"), (a_gu, "a_gu"), (a_down, "a_down")):
                act.dma_start(dst, io[name]).then_inc(A.weights_loaded, 16)
            act_router(act, A)
            act.dma_start(x2[:, :, :], io["x"].rearrange("(t p) d -> p t d", p=P)).then_inc(x_loaded, 16)
            for dst, name in ((b_w1, "b_w1"), (b_w2, "b_w2")):
                act.dma_start(dst, io[name]).then_inc(B.weights_loaded, 16)
            for dst, name in ((b_b1, "b_b1"), (b_b2, "b_b2")):
                act.dma_start(dst.rearrange("p e n -> p (e n)"), io[name].to_broadcast([P, io[name].shape[1]])
                              ).then_inc(B.weights_loaded, 16)
            act_route(act, A)
            act_ffn(act, fAs)
            act_ffn(act, fA)
            act_router(act, B)
            act_route(act, B)
            act.wait_ge(fA.y_mm, A.NT)
            for dst, name in ((c_wq, "c_wq"), (c_wkk, "c_wkk"), (c_wvv, "c_wvv"), (c_wo, "c_wo")):
                act.dma_start(dst, io[name]).then_inc(C.loaded, 16)
            bias = io["fside"].rearrange("h (i p) j -> i p h j", p=P)
            act.dma_start(c_bias[:, :, 1:KEYS0], bias[0, :, :, 0:P]).then_inc(C.loaded, 16)
            act.dma_start(c_bias[:, :, KEYS0 + 1:KEYS], bias[1]).then_inc(C.loaded, 16)
            act_ffn(act, fB)
            act.wait_ge(C.var_done, 1)
            for dst, name in ((d_w13, "d_w13"), (d_w2, "d_w2"), (d_s13, "d_s13"), (d_s2, "d_s2")):
                act.dma_start(dst, io[name]).then_inc(D.weights_loaded, 16)
            for dst, name in ((d_b13, "d_b13"), (d_b2, "d_b2"), (d_sb13, "d_sb13"), (d_sb2, "d_sb2")):
                ap = dst.rearrange("p e n -> p (e n)") if dst.ndim == 3 else dst
                act.dma_start(ap, io[name].to_broadcast([P, io[name].shape[1]])).then_inc(D.weights_loaded, 16)
            act_attention(act)
            act_router(act, D)
            act_route(act, D)
            act_ffn(act, fDs)
            act_ffn(act, fD)

        n_consts = 16 * (len(small) + len(spread))
        cond_step = sem("cond_step")

        @block.gpsimd
        def _(pool):
            pool.memset(ident[:, :], 0.0).then_inc(consts_made, 1)
            pool.memset(ones_f[:, :], 1.0).then_inc(consts_made, 1)
            pool.memset(ones16[:, :], 1.0).then_inc(consts_made, 1)
            pool.memset(not_first[:, :, :], 1.0).then_inc(consts_made, 1)
            pool.iota(iota_p16[:, :], [[1, P]], base=0, channel_multiplier=0, allow_small_or_imprecise_dtypes=True).then_inc(consts_made, 1)
            pool.iota(iota_t[:, :], [[1, 48]], base=0, channel_multiplier=0, allow_small_or_imprecise_dtypes=True).then_inc(consts_made, 1)
            pool.iota(iota_128[:, :], [[P, TT]], base=0, channel_multiplier=0, allow_small_or_imprecise_dtypes=True).then_inc(consts_made, 1)
            pool.iota(token_id[:, :, :], [[0, 2], [P, TT]], base=0, channel_multiplier=1, allow_small_or_imprecise_dtypes=True).then_inc(consts_made, 1)
            pool.iota(rank8[:, :], [[-1, 16]], base=16, channel_multiplier=0, allow_small_or_imprecise_dtypes=True).then_inc(consts_made, 1)
            pool.wait_ge(consts_made, 9)
            pool.affine_select(out=ident[:, :], in_=ident[:, :], compare_op=ALU.not_equal, fill=1.0, base=0,
                               pattern=[[-1, P]], channel_multiplier=1).then_inc(consts_made, 1)
            pool.affine_select(out=before16[:, :], in_=ones16[:, :], compare_op=ALU.is_gt, fill=0.0, base=0,
                               pattern=[[1, P]], channel_multiplier=-1).then_inc(consts_made, 1)
            pool.memset(not_first[:, :, 0:1], 0.0).then_inc(consts_made, 1)
            pool_gather_rows(pool, A)
            pool_gather_results(pool, A)
            pool_gather_rows(pool, B)
            pool_gather_results(pool, B)
            pool_attention(pool)
            pool_gather_rows(pool, D)
            pool_gather_results(pool, D)

        n_made = 12

        @block.tensor
        def _(pe):
            pe.wait_ge(consts_made, n_made)
            pe.wait_ge(consts_loaded, n_consts)
            pe.wait_ge(cond_step, 1)
            pe.matmul(psM[:, 0:64], ones_f[0:64, :], cg[:, :, :].rearrange("p b e -> p (b e)"), start=True, stop=True
                      ).then_inc(cond_step, 1)
            pe_router(pe, A, a_wt, True)
            pe.wait_ge(A.weights_loaded, A.loads)
            pe.wait_ge(cond_step, 3)
            pe_route(pe, A)
            pe.wait_ge(A.routed, 1)
            pe_ffn(pe, fAs)
            pe.wait_ge(fAs.y_out, TT)
            pe_ffn(pe, fA)
            pe_router(pe, B, b_wg, False)
            pe_route(pe, B)
            pe.wait_ge(B.weights_loaded, B.loads)
            pe.wait_ge(B.routed, 1)
            pe.wait_ge(fA.y_out, A.NT)
            pe_ffn(pe, fB)
            pe.wait_ge(fB.y_out, B.NT)
            pe.wait_ge(C.loaded, C.loads)
            pe_attention(pe)
            pe_router(pe, D, d_gw, False)
            pe.wait_ge(D.weights_loaded, D.loads)
            pe_route(pe, D)
            pe.wait_ge(D.routed, 1)
            pe_ffn(pe, fDs)
            pe.wait_ge(fDs.y_out, TT)
            pe_ffn(pe, fD)

        @block.vector
        def _(dve):
            dve.wait_ge(consts_loaded, n_consts)
            for b in range(BATCH):
                last = nc.vector.tensor_scalar(cg[:, b, :], a_wgT[:, :], condT[:, b:b + 1], None, ALU.mult)
            last.then_inc(cond_step, 1)
            dve.wait_ge(cond_step, 2)
            nc.vector.tensor_copy(lg_g[:, :, :].rearrange("p b e -> p (b e)"), psM[:, 0:64]).then_inc(cond_step, 1)
            dve.wait_ge(cond_step, 3)
            dve.wait_ge(consts_made, n_made)
            dve_route(dve, A)
            dve_ffn(dve, fAs)
            dve_ffn(dve, fA)

            def combine_a(s0, u, t):
                wait(dve, B.tok_turned, t - RING + 1)
                wait_slot_free(dve, B.token_stored, s0, u)
                weighted(A, 0, u, t, xr[:, u, :], one(acc[:, :, :], t)).then_inc(A.combine_step, 1)
                dve.wait_ge(A.combine_step, t + 1)
                weighted(A, 1, u, t, xr[:, u, :], xr[:, u, :]).then_inc(B.token_ready, 1)
                dve.wait_ge(B.token_ready, t + 1)
                nc.vector.tensor_copy(std[:, 0:1], xr[:, u, 0:1]).then_inc(A.combined, 1)
            dve_combine(dve, A, combine_a)
            dve_route(dve, B)
            dve_ffn(dve, fB)
            dve.wait_ge(x_loaded, 16)

            def row_stats(t):
                nc.vector.bn_stats(stats[:, bass.ds(t, 1), :].rearrange("p a n -> p (a n)"), one(x2[:, :, :], t)
                                   ).then_inc(C.stat, 1)

            def combine_b(s0, u, t):
                row = one(x2[:, :, :], t)
                weighted(B, 0, u, t, row, row).then_inc(B.combine_step, 1)
                dve.wait_ge(B.combine_step, t + 1)
                wait(dve, B.combined, t)
                weighted(B, 1, u, t, row, row).then_inc(B.combined, 1)
                if live(s0, u - 1, TT):
                    row_stats(t - 1)
            dve_combine(dve, B, combine_b)
            dve.wait_ge(B.combined, TT)
            row_stats(TT - 1)
            dve_attention(dve)

            def normalise(s0, u):
                t = s0 + u
                wait(dve, D.tok_turned, t - RING + 1)
                wait_slot_free(dve, D.token_stored, s0, u)
                nc.vector.tensor_scalar(xr[:, u, :], one(acc[:, :, :], t), mv2[:, bass.ds(t, 1), 0:1].rearrange("p a b -> p (a b)"),
                                        rstd[:, bass.ds(t, 1)], ALU.subtract, ALU.mult).then_inc(C.z_step, 1)
                dve.wait_ge(C.z_step, t + 1)
                nc.vector.tensor_tensor(xr[:, u, :], xr[:, u, :], g_out[:, :], ALU.mult).then_inc(D.token_ready, 1)
            steps(dve, TT, normalise, 0, 0)
            dve_route(dve, D)
            dve.wait_ge(D.weights_loaded, D.loads)
            dve_ffn(dve, fDs)
            dve_ffn(dve, fD)

            def combine_d(s0, u, t):
                wait_slot_free(dve, out_stored, s0, u)
                weighted(D, 0, u, t, xr[:, u, :], one(acc[:, :, :], t)).then_inc(D.combine_step, 1)
                dve.wait_ge(D.combine_step, 2 * t + 1)
                weighted(D, 1, u, t, xr[:, u, :], xr[:, u, :]).then_inc(D.combine_step, 1)
                dve.wait_ge(D.combine_step, 2 * t + 2)
                nc.vector.tensor_tensor(xr[:, u, :], xr[:, u, :], one(x2[:, :, :], t), ALU.add).then_inc(D.combined, 1)
            dve_combine(dve, D, combine_d)


def layout(inputs):
    import numpy as np

    def rows(w):
        return np.ascontiguousarray(w.reshape(-1, 128, w.shape[-1]).transpose(1, 0, 2))

    def expert_rows(w):
        e, k, n = w.shape
        return np.ascontiguousarray(w.reshape(e, k // 128, 128, n).transpose(2, 0, 1, 3))

    i = {k: np.asarray(v) for k, v in inputs.items()}
    cat = np.concatenate
    o = {}
    o["x"] = i["x"].reshape(2048, 256)
    o["condT"] = i["cond_64"].T
    o["a_wt"] = rows(i["L0_cond_wt"].T)
    o["a_wgT"] = i["L0_cond_wg"].T
    o["a_gu"] = expert_rows(cat([i["L0_cond_w_gate"], i["L0_cond_w_up"]], -1))
    o["a_down"] = i["L0_cond_w_down"].transpose(1, 0, 2)
    o["a_sgu"] = rows(cat([i["L0_cond_sw_gate"], i["L0_cond_sw_up"]], -1))
    o["a_sdown"] = rows(i["L0_cond_sw_down"])
    o["b_wg"] = rows(i["L0_ffn_Wg"])
    o["b_bg"] = i["L0_ffn_bg"].reshape(1, -1)
    o["b_w1"] = expert_rows(i["L0_ffn_W1"])
    o["b_w2"] = expert_rows(i["L0_ffn_W2"])
    o["b_b1"] = i["L0_ffn_b1"].reshape(1, -1)
    o["b_b2"] = i["L0_ffn_b2"].reshape(1, -1)
    o["g_in"] = i["L1_cond_g_in"].reshape(2, 128).T
    o["g_out"] = i["L1_cond_g_out"].reshape(1, -1)
    o["nullb"] = i["L1_cond_null_attn_bias"].reshape(1, -1)
    nk, nv = i["cond_64"][0], i["cond_64"][1]
    o["nk2"] = cat([nk, nk]).reshape(-1, 1)
    o["nv2"] = cat([nv, nv]).reshape(-1, 1)
    o["nvb"] = nv.reshape(1, -1)
    wk, wv = i["L1_cond_Wkv"][:, :64], i["L1_cond_Wkv"][:, 64:]
    o["c_wq"] = rows(i["L1_cond_Wq"])
    o["c_wkk"] = rows(cat([wk, wk], 1))
    o["c_wvv"] = rows(cat([wv, wv], 1))
    o["c_wo"] = rows(i["L1_cond_Wo"])
    o["fside"] = i["fside_16xSxS_0"]
    o["mask"] = i["mask_BxS_bk0"].reshape(1, -1)
    o["d_gw"] = rows(i["L1_ffn_gate_w"].T)
    o["d_eb"] = i["L1_ffn_expert_bias"].reshape(1, -1)
    o["d_w13"] = expert_rows(cat([i["L1_ffn_w1"], i["L1_ffn_w3"]], 1).transpose(0, 2, 1))
    o["d_b13"] = cat([i["L1_ffn_b1"], i["L1_ffn_b3"]], 1).reshape(1, -1)
    o["d_w2"] = i["L1_ffn_w2"].transpose(2, 0, 1)
    o["d_b2"] = i["L1_ffn_b2"].reshape(1, -1)
    o["d_s13"] = rows(cat([i["L1_ffn_sw1"], i["L1_ffn_sw3"]], 0).T)
    o["d_sb13"] = cat([i["L1_ffn_sb1"], i["L1_ffn_sb3"]], 0).reshape(1, -1)
    o["d_s2"] = rows(i["L1_ffn_sw2"].T)
    o["d_sb2"] = i["L1_ffn_sb2"].reshape(1, -1)
    return {k: np.ascontiguousarray(v) for k, v in o.items()}


def kernel(**inputs):
    import numpy as np
    import concourse.bacc as bacc
    from concourse.bass_utils import run_bass_kernel_spmd

    nc = bacc.Bacc("TRN2", target_bir_lowering=False, num_devices=1)
    arrays, io = {}, {}
    for name, a in layout(inputs).items():
        arrays[f"in_{name}"] = a
        io[name] = nc.dram_tensor(f"in_{name}", a.shape, mybir.dt.from_np(a.dtype), kind="ExternalInput").ap()
    io["out"] = nc.dram_tensor("out", (TOKENS, DIM), F32, kind="ExternalOutput").ap()
    build(nc, io)
    r = run_bass_kernel_spmd(nc, [arrays], core_ids=[0])
    return r.results[0]["out"].reshape(BATCH, SEQ, DIM)
```

```python
from contextlib import ExitStack

import concourse.bass as bass
from concourse import mybir

F32 = mybir.dt.float32
F16 = mybir.dt.float16
I32 = mybir.dt.int32
U32 = mybir.dt.uint32
U8 = mybir.dt.uint8
ALU = mybir.AluOpType
ACT = mybir.ActivationFunctionType
AX_X = mybir.AxisListType.X

P = 128
BATCH, SEQ, DIM = 8, 256, 256
TOKENS = BATCH * SEQ
TT = TOKENS // P
KD = DIM // P
PAIRS = 2 * TOKENS
RING = 4
HEADS, DH = 16, 64
QT = SEQ // P
KEYS0, KEYS1 = 1 + P, 1 + SEQ
KEYS = KEYS0 + KEYS1
LN_EPS = 1e-5
HIDDEN_KEY = 1e30
LOWEST = -3e38
NPAIR = HEADS // 2
QUAD = 4
CHUNKS = 2


def slot_tiles(experts):
    return (PAIRS - experts) // P + experts


def live(s0, off, n):
    return not isinstance(s0, int) or 0 <= s0 + off < n


def wait(eng, sem, value):
    if not isinstance(value, int) or value > 0:
        eng.wait_ge(sem, value)


def steps(eng, n, body, lead, lag):
    lo = max(RING, -(-lag // RING) * RING)
    hi = lo + (n - lead - lo) // RING * RING
    for s in range(0, lo):
        body(s - s % RING, s % RING)
    with eng.Fori(lo // RING, hi // RING) as i:
        for u in range(RING):
            body(i * RING, u)
    for s in range(hi, n + lag):
        body(s - s % RING, s % RING)


def one(ap, i):
    return ap[:, bass.ds(i, 1), :].rearrange("p o n -> p (o n)")


class Ring:
    def __init__(self, sem, name):
        self.sems = [sem(f"{name}{r}") for r in range(RING)]
        self.count = [0] * RING


class Use:
    def __init__(self, ring, tiles, dmas=1):
        self.sems, self.dmas = ring.sems, dmas
        self.before = list(ring.count)
        for r in range(RING):
            ring.count[r] += 16 * dmas * len(range(r, tiles, RING))
        self.after = list(ring.count)


class Stage:
    def __init__(self, sem, name, experts, src, loads, eps):
        self.name, self.E, self.NT, self.src, self.loads, self.eps = name, experts, slot_tiles(experts), src, loads, eps
        self.weights_loaded = sem(f"{name}_weights_loaded")
        self.tok_turned = sem(f"{name}_tok_turned")
        self.tokT_ready = sem(f"{name}_tokT_ready")
        self.logits_done = sem(f"{name}_logits_done")
        self.route_step = sem(f"{name}_route_step")
        self.exp_wanted = sem(f"{name}_exp_wanted")
        self.exp_done = sem(f"{name}_exp_done")
        self.onehot_ready = sem(f"{name}_onehot_ready")
        self.prefix_done = sem(f"{name}_prefix_done")
        self.eqrow_ready = sem(f"{name}_eqrow_ready")
        self.eqrow_used = sem(f"{name}_eqrow_used")
        self.inv_done = sem(f"{name}_inv_done")
        self.routed = sem(f"{name}_routed")
        self.combined = sem(f"{name}_combined")
        self.combine_step = sem(f"{name}_combine_step")


class Ffn:
    def __init__(self, sem, name, n, hw, hk, kind, st, rows, w_in, w_out, b_in, b_out):
        self.name, self.n, self.hw, self.hk, self.kind, self.st, self.rows = name, n, hw, hk, kind, st, rows
        self.w_in, self.w_out, self.b_in, self.b_out = w_in, w_out, b_in, b_out
        self.turned = sem(f"{name}_turned")
        self.xT_ready = sem(f"{name}_xT_ready")
        self.h_mm = sem(f"{name}_h_mm")
        self.h_pre = sem(f"{name}_h_pre")
        self.h_gate = sem(f"{name}_h_gate")
        self.h_ready = sem(f"{name}_h_ready")
        self.h_turned = sem(f"{name}_h_turned")
        self.hT_ready = sem(f"{name}_hT_ready")
        self.y_mm = sem(f"{name}_y_mm")
        self.y_out = sem(f"{name}_y_out")


class Shared:
    def __init__(self, sem, name, xT, hT, parts, w_in, w_out, b_in):
        self.xT, self.hT, self.parts, self.w_in, self.w_out, self.b_in = xT, hT, parts, w_in, w_out, b_in
        self.kept = sem(f"{name}_kept")
        self.n_parts = parts.shape[2]
        self.h_mm = sem(f"{name}_h_mm")
        self.part_ready = sem(f"{name}_part_ready")
        self.h_leaky = sem(f"{name}_h_leaky")
        self.h_ready = sem(f"{name}_h_ready")
        self.y_mm = sem(f"{name}_y_mm")
        self.y_out = sem(f"{name}_y_out")


class Attention:
    def __init__(self, sem, loads):
        self.loads = loads
        self.loaded = sem("c_loaded")
        self.pairs_loaded = sem("c_pairs_loaded")
        self.out_mom = sem("c_out_mom")
        self.out_rstd = sem("c_out_rstd")
        self.x_biased = sem("c_x_biased")
        self.base_ready = sem("c_base_ready")
        self.var_done = sem("c_var_done")
        self.out_var = sem("c_out_var")
        self.stat = sem("c_stat")
        self.mom_done = sem("c_mom_done")
        self.rstd_done = sem("c_rstd_done")
        self.bias_ready = sem("c_bias_ready")
        self.kT_fixed = sem("c_kT_fixed")
        self.xn_ready = sem("c_xn_ready")
        self.xn_turned = sem("c_xn_turned")
        self.xnT_ready = sem("c_xnT_ready")
        self.kv_mm = sem("c_kv_mm")
        self.kT_ready = sem("c_kT_ready")
        self.v_ready = sem("c_v_ready")
        self.q_mm = sem("c_q_mm")
        self.qT_ready = sem("c_qT_ready")
        self.s_mm = sem("c_s_mm")
        self.mask_ready = sem("c_mask_ready")
        self.bm_ready = sem("c_bm_ready")
        self.score_ready = sem("c_score_ready")
        self.p_ready = sem("c_p_ready")
        self.rec_ready = sem("c_rec_ready")
        self.pn_ready = sem("c_pn_ready")
        self.p_turned = sem("c_p_turned")
        self.pT_ready = sem("c_pT_ready")
        self.pv_mm = sem("c_pv_mm")
        self.o_ready = sem("c_o_ready")
        self.wo_mm = sem("c_wo_mm")
        self.ao_ready = sem("c_ao_ready")
        self.ao_stat = sem("c_ao_stat")
        self.z_step = sem("c_z_step")


def build(nc, io):
    ctx = ExitStack()
    with ctx:
        def sb(name, shape, dt=F32):
            return ctx.enter_context(nc.sbuf_tensor(name, shape, dt))

        def sem(name):
            return ctx.enter_context(nc.semaphore(name))

        def carve(region, sizes):
            at, parts = 0, []
            for n in sizes:
                parts.append(region[:, at:at + n])
                at += n
            return parts

        x2 = sb("x2", [P, TT, DIM])
        acc = sb("acc", [P, TT, DIM])
        region_ac = sb("region_ac", [P, 10784])
        region_bd = sb("region_bd", [P, 22528])
        work = sb("work", [P, 8752])

        a_gu, a_down, a_sgu, a_sdown = carve(region_ac, [4096, 2048, 1024, 512])
        a_gu = a_gu.rearrange("p (e k n) -> p e k n", e=8, k=KD)
        a_down = a_down.rearrange("p (e n) -> p e n", e=8)
        a_sgu = a_sgu.rearrange("p (k n) -> p k n", k=KD)
        a_sdown = a_sdown.rearrange("p (k n) -> p k n", k=2)
        a_xT = x2[:, :, :].rearrange("p t n -> p (t n)")
        a_hT = region_bd[:, 20480:20480 + 2 * CHUNKS * QUAD * P]
        a_parts = region_ac[:, 7680:7680 + 2 * 3 * QUAD * P]
        c_wq, c_wkk, c_wvv, c_wo, c_bias = carve(region_ac, [2048, 256, 256, 2048, HEADS * KEYS])
        c_wq = c_wq.rearrange("p (k n) -> p k n", k=KD)
        c_wkk = c_wkk.rearrange("p (k n) -> p k n", k=KD)
        c_wvv = c_wvv.rearrange("p (k n) -> p k n", k=KD)
        c_wo = c_wo.rearrange("p (j n) -> p j n", j=NPAIR)
        c_bias = c_bias.rearrange("p (h n) -> p h n", h=HEADS)
        b_w1, b_w2, b_b1, b_b2 = carve(region_bd, [8192, 8192, 4096, 2048])
        b_w1 = b_w1.rearrange("p (e k n) -> p e k n", e=8, k=KD)
        b_w2 = b_w2.rearrange("p (e k n) -> p e k n", e=8, k=4)
        b_b1 = b_b1.rearrange("p (e n) -> p e n", e=8)
        b_b2 = b_b2.rearrange("p (e n) -> p e n", e=8)
        d_w13, d_w2, d_s13, d_s2, d_b13, d_b2, d_sb13 = carve(
            region_bd, [8192, 4096, 1024, 512, 4096, 4096, 4])
        d_w13 = d_w13.rearrange("p (e k n) -> p e k n", e=16, k=KD)
        d_w2 = d_w2.rearrange("p (e n) -> p e n", e=16)
        d_s13 = d_s13.rearrange("p (k n) -> p k n", k=KD)
        d_s2 = d_s2.rearrange("p (k n) -> p k n", k=2)
        d_b13 = d_b13.rearrange("p (e n) -> p e n", e=16)
        d_b2 = d_b2.rearrange("p (e n) -> p e n", e=16)

        d_xT, d_hT, d_parts = carve(region_ac, [KD * TOKENS, 2 * CHUNKS * QUAD * P, 2 * 2 * QUAD * P])

        xs, xT, hbuf, hT, ys, xr, xrT, gat = carve(work, [1024, 512, 1024, 1024, 1024, 1024, 512, 2048])
        xs = xs.rearrange("p (r n) -> p r n", r=RING)
        xT = xT.rearrange("p (r k n) -> p r k n", r=2, k=KD)
        hbuf = hbuf.rearrange("p (r n) -> p r n", r=2)
        hT = hT.rearrange("p (r n) -> p r n", r=2)
        xr = xr.rearrange("p (r n) -> p r n", r=RING)
        xrT = xrT.rearrange("p (r k n) -> p r k n", r=2, k=KD)
        rt_lg, rt_key, rt_tmp, rt_oh1, rt_oh2, rt_sc, rt_pos, rt_small = carve(gat, [256] * 8)
        eq_tile = ys[:, 0:768].bitcast(F16)
        eq_row = work[:, 0:TT * P].bitcast(F16).rearrange("p (k n) -> p k n", k=2 * TT)
        ys = ys.rearrange("p (r n) -> p r n", r=RING)
        gat = gat.rearrange("p (r c n) -> p r c n", r=RING, c=2)
        (c_xn, c_xnT, c_qT, c_kT, c_v, c_bm, c_sc, c_p, c_pT, c_oT, c_mp, c_small, c_gat) = carve(
            work, [512, 512, 512, 2 * KEYS1, 128, 2 * KEYS, 2 * KEYS, 2 * KEYS, 768, 2048, KEYS, 32, 1024])
        c_gat = c_gat.rearrange("p (r c n) -> p r c n", r=QT, c=2)
        c_xn = c_xn.rearrange("p (i n) -> p i n", i=QT)
        c_xnT = c_xnT.rearrange("p (k n) -> p k n", k=KD)
        c_qT = c_qT.rearrange("p (r n) -> p r n", r=2)
        c_kT = c_kT.rearrange("p (o n) -> p o n", o=2)
        c_v = c_v.rearrange("p (j n) -> p j n", j=QT)
        c_bm = c_bm.rearrange("p (r n) -> p r n", r=2)
        c_sc = c_sc.rearrange("p (r n) -> p r n", r=2)
        c_p = c_p.rearrange("p (r n) -> p r n", r=2)
        c_pT = c_pT.rearrange("p (r n) -> p r n", r=2)
        c_oT = c_oT.rearrange("p (j n) -> p j n", j=NPAIR)
        c_min = c_small[:, 0:6].rearrange("p (r i) -> p r i", r=3)
        c_sum = c_small[:, 6:12].rearrange("p (r i) -> p r i", r=3)
        c_rec = c_small[:, 12:18].rearrange("p (r i) -> p r i", r=3)

        oh16 = sb("oh16", [P, 256], F16)
        inv = sb("inv", [P, 48], U32)
        home = sb("home", [P, 48], U32)
        inv_c = sb("inv_c", [P, 2, 48])
        slot_u = sb("slot_u", [P, 2 * TT], U32)
        home_f = sb("home_f", [P, 48])
        gates = sb("gates", [P, 2, TT])
        len_te = slot_tiles(16) + 1
        tile_expert = sb("tile_expert", [1, len_te], I32)

        ident = sb("ident", [P, P])
        before16 = sb("before16", [P, P], F16)
        ones16 = sb("ones16", [P, P], F16)
        iota_p16 = sb("iota_p16", [P, P], F16)
        iota_t = sb("iota_t", [P, 48])
        iota_128 = sb("iota_128", [P, TT])
        token_id1 = sb("token_id1", [P, 2, TT])
        past_row = sb("past_row", [P, 48])
        rank8 = sb("rank8", [P, 16])
        not_first = sb("not_first", [P, 16, TT])
        ones_f = sb("ones_f", [P, P])
        a_wt = sb("a_wt", [P, KD, 8])
        b_wg = sb("b_wg", [P, KD, 8])
        b_bg = sb("b_bg", [P, 8])
        d_gw = sb("d_gw", [P, KD, 16])
        d_eb = sb("d_eb", [P, 16])
        condT = sb("condT", [64, BATCH])
        a_wgT = sb("a_wgT", [64, 8])
        cg = sb("cg", [64, BATCH, 8])
        lg_g = sb("lg_g", [P, BATCH, 8])
        g_in = sb("g_in", [P, KD])
        d_sb2 = sb("d_sb2", [P, DIM])
        g_out = sb("g_out", [P, DIM])
        nvb = sb("nvb", [P, DH])
        nv2 = sb("nv2", [P, 1])
        nk2 = sb("nk2", [P, 1])
        nullb = sb("nullb", [P, HEADS])
        mask8 = sb("mask8", [P, BATCH, SEQ], U8)
        stats = sb("stats", [P, TT, 6])
        mv = sb("mv", [P, TT, 2])
        in_stats = sb("in_stats", [P, QT, 6])
        in_mv = sb("in_mv", [P, QT, 2])
        in_rstd = sb("in_rstd", [P, QT])
        rstd = sb("rstd", [P, TT])
        minus_half = sb("minus_half", [P, TT])

        psX = ctx.enter_context(nc.psum_tensor("psX", [P, 512], F32))
        psH = ctx.enter_context(nc.psum_tensor("psH", [P, 2, 512], F32))
        psHT = ctx.enter_context(nc.psum_tensor("psHT", [P, 2, 512], F32))
        psY = ctx.enter_context(nc.psum_tensor("psY", [P, 512], F32))
        psL = ctx.enter_context(nc.psum_tensor("psL", [P, 512], F32))
        psM = ctx.enter_context(nc.psum_tensor("psM", [P, 512], F32))
        router_x = [b[:, 0:DIM].rearrange("p (k n) -> p k n", k=KD) for b in (psX, psY)]
        ffn_x = [b[:, 0:DIM].rearrange("p (k n) -> p k n", k=KD) for b in (psX, psL)]
        shared_y = [b[:, 0:DIM] for b in (psX, psY)]
        ffn_y = [b[:, 0:DIM] for b in (psY, psM)]
        rows_x = psX[:, :].rearrange("p (k i n) -> p k i n", k=KD, i=QT)
        keys_x = psX[:, 0:SEQ]
        values_x = psX[:, SEQ:512].rearrange("p (i n) -> p i n", i=QT)

        y0_dram = nc.dram_tensor("y0_scratch", [TOKENS, DIM], F32, kind="Internal").ap()
        z_dram = nc.dram_tensor("z_scratch", [TOKENS, DIM], F32, kind="Internal").ap()

        def by_tile(dram):
            return dram.rearrange("(t p) d -> t p d", p=P)

        def dram_tile(dram, t):
            return by_tile(dram)[bass.ds(t, 1), :, :].rearrange("o p d -> (o p) d")

        consts_made = sem("consts_made")
        first_loaded = sem("first_loaded")
        consts_loaded = sem("consts_loaded")
        x_loaded = sem("x_loaded")

        def done_dmas(use, s0, off):
            each = 16 * use.dmas
            return (each // RING) * s0 + each * (off // RING + 1) + use.before[off % RING]

        def wait_dma(eng, use, s0, off):
            eng.wait_ge(use.sems[off % RING], done_dmas(use, s0, off))

        def wait_slot_free(eng, use, s0, off):
            wait(eng, use.sems[off % RING], done_dmas(use, s0, off) - 16 * use.dmas)

        def wait_dmas(eng, use):
            for r in range(RING):
                eng.wait_ge(use.sems[r], use.after[r])

        tokens_loaded, rows_gathered, slots_stored, gathered, tokens_stored = (
            Ring(sem, n) for n in ("tokens_loaded", "rows_gathered", "slots_stored", "gathered", "tokens_stored"))

        def stage(name, experts, src, loads, eps):
            s = Stage(sem, name, experts, src, 16 * loads, eps)
            s.pair_dram = nc.dram_tensor(f"{name}_pairs", [PAIRS + s.NT * P, DIM], F32, kind="Internal").ap()
            s.slots_stored = Use(slots_stored, s.NT)
            s.gathered = Use(gathered, TT) if name != "b" else None
            s.token_stored = Use(tokens_stored, TT) if name != "a" else None
            return s

        def ffn(name, n, hw, hk, kind, st, rows, w_in, w_out, b_in, b_out):
            f = Ffn(sem, name, n, hw, hk, kind, st, rows, w_in, w_out, b_in, b_out)
            f.loaded = Use(rows_gathered, n)
            f.h_read = f.h_ready if kind == "leaky" else f.h_pre
            return f

        A = stage("a", 8, io["x"], 4, 1e-20)
        B = stage("b", 8, y0_dram, 4, 1e-9)
        D = stage("d", 16, z_dram, 7, 1e-10)
        fA = ffn("af", A.NT, 256, 1, "leaky", st=A, rows=xs,
                 w_in=lambda k, e: a_gu[:, bass.ds(e, 1), k, :].rearrange("p o n -> p (o n)"),
                 w_out=lambda j, e: one(a_down, e), b_in=None, b_out=None)
        fB = ffn("bf", B.NT, 512, 4, "gelu", st=B, rows=xs,
                 w_in=lambda k, e: b_w1[:, bass.ds(e, 1), k, :].rearrange("p o n -> p (o n)"),
                 w_out=lambda j, e: b_w2[:, bass.ds(e, 1), j, :].rearrange("p o n -> p (o n)"),
                 b_in=lambda e: one(b_b1, e), b_out=lambda e: one(b_b2, e))
        fD = ffn("df", D.NT, 256, 1, "silu", st=D, rows=xs,
                 w_in=lambda k, e: d_w13[:, bass.ds(e, 1), k, :].rearrange("p o n -> p (o n)"),
                 w_out=lambda j, e: one(d_w2, e), b_in=lambda e: one(d_b13, e), b_out=lambda e: one(d_b2, e))

        def shared(name, xT, hT, parts, n, w_in, w_out, b_in):
            return Shared(sem, name, xT.rearrange("p (k t) -> p k t", k=KD),
                          hT.rearrange("p (r c t) -> p r c t", r=2, c=CHUNKS), parts.rearrange("p (r n t) -> p r n t", r=2, n=n),
                          w_in, w_out, b_in)

        A.shared = shared("as", a_xT, a_hT, a_parts, 3, a_sgu, a_sdown, None)
        B.shared = None
        D.shared = shared("ds", d_xT, d_hT, d_parts, 2, d_s13, d_s2, d_sb13)
        B.token_ready, D.token_ready = A.combined, sem("d_token_ready")
        A.ffn, B.ffn, D.ffn = fA, fB, fD

        class Experts:
            def __init__(self, eng, f):
                self.eng, self.f = eng, f
                self.registers = [eng.alloc_register(f"{f.name}_expert{r}") for r in range(RING)]

            def fetch(self, s0, o):
                if live(s0, o, self.f.n):
                    self.eng.reg_load(self.registers[o % RING], tile_expert[0:1, bass.ds(s0 + o, 1)])

            def of(self, o):
                return self.eng.snap(self.registers[o % RING], min_val=0, max_val=self.f.st.E - 1)

        def pe_router(pe, st, w):
            def body(s0, u):
                if live(s0, u, TT):
                    t = s0 + u
                    if st is A:
                        pe.wait_ge(x_chunk.sems[t // QUAD], 16)
                    else:
                        pe.wait_ge(st.token_ready, t + 1)
                    wait(pe, st.shared.kept if st.shared else st.tokT_ready, t - 1)
                    rows = acc[:, t, :] if st is A else xr[:, u, :]
                    for k in range(KD):
                        last = pe.transpose(router_x[u % 2][:, k, :], rows[:, k * P:(k + 1) * P], ident[:, :])
                    last.then_inc(st.tok_turned, 1)
                if live(s0, u - 1, TT):
                    t = s0 + (u - 1)
                    pe.wait_ge(st.tokT_ready, t + 1)
                    for k in range(KD):
                        last = pe.matmul(psL[:, bass.ds(t * st.E, st.E)], xrT[:, (u - 1) % 2, k, :], w[:, k, :],
                                         start=(k == 0), stop=(k == KD - 1))
                    last.then_inc(st.logits_done, 1)
            if st is A:
                for t in range(TT + 1):
                    body(t - t % RING, t % RING)
            else:
                steps(pe, TT, body, 0, 1)

        def pe_counts(pe, st):
            n = TT * st.E
            pe.wait_ge(st.onehot_ready, 1)
            oh_et = oh16[:, 0:n].rearrange("p (t e) -> p e t", e=st.E)
            pe.matmul(psM[:, 0:n], before16[:, :], oh_et, start=True, stop=True)
            pe.matmul(psM[:, 256:256 + n], ones16[:, :], oh_et, start=True, stop=True).then_inc(st.prefix_done, 1)

        def pe_invert(pe, st):
            eq = eq_tile[:, 0:2 * TT * st.NT].rearrange("p (k a) -> p k a", a=st.NT)
            for k in range(2 * TT):
                if k % QUAD == 0:
                    pe.wait_ge(st.eqrow_ready, k // QUAD + 1)
                c = k // TT
                last = pe.matmul(psL[:, 64 * c:64 * c + st.NT], eq_row[:, k, :], eq[:, k, :], start=(k % TT == 0), stop=(k % TT == TT - 1))
            last.then_inc(st.inv_done, 1)

        def pe_shared_in(pe, sh, i):
            q, c = i // CHUNKS, i % CHUNKS
            pe.wait_ge(sh.kept, QUAD * q + QUAD)
            wait(pe, sh.part_ready, sh.n_parts * (i - 1))
            for n, bank in enumerate((psH, psHT)):
                at = (n * CHUNKS + c) * P
                for k in range(KD):
                    last = pe.matmul(bank[:, c, :], sh.w_in[:, k, at:at + P], sh.xT[:, k, q * QUAD * P:(q + 1) * QUAD * P],
                                     start=(k == 0), stop=(k == KD - 1))
            last.then_inc(sh.h_mm, 1)

        def pe_shared_out(pe, sh, q):
            pe.wait_ge(sh.h_ready, CHUNKS * (q + 1))
            for i in range(QUAD):
                t = QUAD * q + i
                wait(pe, sh.y_out, t - 1)
                for c in range(CHUNKS):
                    last = pe.matmul(shared_y[t % 2], sh.hT[:, q % 2, c, i * P:(i + 1) * P], sh.w_out[:, c, :],
                                     start=(c == 0), stop=(c == CHUNKS - 1))
                last.then_inc(sh.y_mm, 1)

        def pe_route_and_shared(pe, st):
            sh = st.shared
            pe_shared_in(pe, sh, 0)
            pe_shared_in(pe, sh, 1)
            pe_counts(pe, st)
            pe_shared_in(pe, sh, 2)
            pe_shared_out(pe, sh, 0)
            pe_shared_in(pe, sh, 3)
            pe_shared_in(pe, sh, 4)
            pe_invert(pe, st)
            pe_shared_out(pe, sh, 1)
            pe_shared_in(pe, sh, 5)
            pe_shared_in(pe, sh, 6)
            pe_shared_out(pe, sh, 2)
            pe_shared_in(pe, sh, 7)
            pe_shared_out(pe, sh, 3)

        def act_shared(act, sh, kind):
            for i, q in ((0, None), (1, None), (2, 0), (3, None), (4, 1), (5, None), (6, 2), (7, 3)):
                act_shared_in(act, sh, i, kind)
                if q is not None:
                    for t in range(QUAD * q, QUAD * q + QUAD):
                        act.wait_ge(sh.y_mm, t + 1)
                        nc.scalar.copy(acc[:, t, :], shared_y[t % 2]).then_inc(sh.y_out, 1)

        def act_shared_in(act, sh, i, kind):
            c = i % CHUNKS
            act.wait_ge(sh.h_mm, i + 1)
            wait(act, sh.h_ready, i - 1)
            gate, up, parts = psH[:, c, :], psHT[:, c, :], sh.parts[:, c, :, :]
            if kind == "leaky":
                nc.scalar.activation(parts[:, 0, :], gate, ACT.Relu).then_inc(sh.part_ready, 1)
                nc.scalar.activation(parts[:, 2, :], gate, ACT.Relu, scale=-0.01).then_inc(sh.part_ready, 1)
                nc.scalar.copy(parts[:, 1, :], up).then_inc(sh.part_ready, 1)
            else:
                nc.scalar.activation(parts[:, 0, :], gate, ACT.Silu, bias=sh.b_in[:, c:c + 1]).then_inc(sh.part_ready, 1)
                nc.scalar.activation(parts[:, 1, :], up, ACT.Identity, bias=sh.b_in[:, CHUNKS + c:CHUNKS + c + 1]
                                     ).then_inc(sh.part_ready, 1)

        def pool_shared_in(pool, sh, i, kind):
            q, c = i // CHUNKS, i % CHUNKS
            parts = sh.parts[:, c, :, :]
            pool.wait_ge(sh.part_ready, sh.n_parts * (i + 1))
            if kind == "leaky":
                pool.tensor_tensor(parts[:, 0, :], parts[:, 0, :], parts[:, 2, :], ALU.subtract).then_inc(sh.h_leaky, 1)
                pool.wait_ge(sh.h_leaky, i + 1)
            wait(pool, sh.y_mm, QUAD * (q - 1))
            pool.tensor_tensor(sh.hT[:, q % 2, c, :], parts[:, 0, :], parts[:, 1, :], ALU.mult).then_inc(sh.h_ready, 1)

        def pool_shared_and_gather(pool, st, kind):
            sh = st.shared
            for i in range(3):
                pool_shared_in(pool, sh, i, kind)
            pool_shared_in(pool, sh, 3, kind)
            pool_shared_in(pool, sh, 4, kind)
            pool_gather_rows(pool, st, 0, RING)
            pool_shared_in(pool, sh, 5, kind)
            pool_shared_in(pool, sh, 6, kind)
            pool_shared_in(pool, sh, 7, kind)

        def pe_ffn(pe, f):
            experts = Experts(pe, f)

            def body(s0, u):
                if live(s0, u + 1, f.n):
                    r, t = (u + 1) % RING, s0 + (u + 1)
                    wait_dma(pe, f.loaded, s0, u + 1)
                    wait(pe, f.xT_ready, t - 1)
                    for k in range(KD):
                        last = pe.transpose(ffn_x[r % 2][:, k, :], f.rows[:, r, k * P:(k + 1) * P], ident[:, :])
                    last.then_inc(f.turned, 1)
                if live(s0, u, f.n):
                    t, h = s0 + u, u % 2
                    e = experts.of(u)
                    pe.wait_ge(f.xT_ready, t + 1)
                    wait(pe, f.h_read, t - 1)
                    for k in range(KD):
                        last = pe.matmul(psH[:, h, 0:f.hw], xT[:, h, k, :], f.w_in(k, e),
                                         start=(k == 0), stop=(k == KD - 1))
                    last.then_inc(f.h_mm, 1)
                experts.fetch(s0, u + 1)
                if live(s0, u - 1, f.n):
                    t, h = s0 + (u - 1), (u - 1) % 2
                    pe.wait_ge(f.h_ready, t + 1)
                    wait(pe, f.hT_ready, t - 1)
                    for j in range(f.hk):
                        last = pe.transpose(psHT[:, h, j * P:(j + 1) * P], hbuf[:, h, j * P:(j + 1) * P], ident[:, :])
                    last.then_inc(f.h_turned, 1)
                if live(s0, u - 2, f.n):
                    t, h = s0 + (u - 2), u % 2
                    e = experts.of(u - 2)
                    pe.wait_ge(f.hT_ready, t + 1)
                    wait(pe, f.y_out, t - 1)
                    for j in range(f.hk):
                        last = pe.matmul(ffn_y[h], hT[:, h, j * P:(j + 1) * P], f.w_out(j, e),
                                         start=(j == 0), stop=(j == f.hk - 1))
                    last.then_inc(f.y_mm, 1)
            experts.fetch(0, 0)
            wait_dma(pe, f.loaded, 0, 0)
            for k in range(KD):
                last = pe.transpose(ffn_x[0][:, k, :], f.rows[:, 0, k * P:(k + 1) * P], ident[:, :])
            last.then_inc(f.turned, 1)
            steps(pe, f.n, body, 1, 2)

        def act_broadcast(act, dst, name, s):
            ap = dst.rearrange("p a n -> p (a n)") if dst.ndim == 3 else dst
            act.dma_start(ap, io[name].to_broadcast([P, io[name].shape[1]])).then_inc(s, 16)

        def act_router(act, st):
            def body(s0, u):
                t = s0 + u
                act.wait_ge(st.tok_turned, t + 1)
                wait(act, st.logits_done, t - 1)
                nc.scalar.copy(xrT[:, u % 2, :, :], router_x[u % 2]).then_inc(st.tokT_ready, 1)
                if st.shared:
                    nc.scalar.copy(st.shared.xT[:, :, bass.ds(t * P, P)], router_x[u % 2]).then_inc(st.shared.kept, 1)
            steps(act, TT, body, 0, 0)

        def act_ffn(act, f):
            def copy_x(s0, o):
                t, h = s0 + o, o % 2
                act.wait_ge(f.turned, t + 1)
                wait(act, f.h_mm, t - 1)
                nc.scalar.copy(xT[:, h, :, :], ffn_x[h]).then_inc(f.xT_ready, 1)

            def body(s0, u):
                if live(s0, u + 1, f.n):
                    copy_x(s0, u + 1)
                if live(s0, u, f.n) and f.kind == "leaky":
                    t, h = s0 + u, u % 2
                    act.wait_ge(f.h_mm, t + 1)
                    wait(act, f.h_turned, t - 1)
                    nc.scalar.mul(hbuf[:, h, 0:f.hw // 2], psH[:, h, 0:f.hw // 2], 0.01).then_inc(f.h_pre, 1)
                elif live(s0, u, f.n):
                    t, h = s0 + u, u % 2
                    act.wait_ge(f.h_pre, t + 1)
                    if f.kind == "gelu":
                        nc.scalar.activation(hbuf[:, h, :], hbuf[:, h, :], ACT.Gelu).then_inc(f.h_ready, 1)
                    else:
                        m = f.hw // 2
                        nc.scalar.activation(hbuf[:, h, 0:m], hbuf[:, h, 0:m], ACT.Silu).then_inc(f.h_gate, 1)
                if live(s0, u - 1, f.n):
                    t, h = s0 + (u - 1), (u - 1) % 2
                    act.wait_ge(f.h_turned, t + 1)
                    wait(act, f.y_mm, t - 1)
                    nc.scalar.copy(hT[:, h, 0:f.hk * P], psHT[:, h, 0:f.hk * P]).then_inc(f.hT_ready, 1)
            copy_x(0, 0)
            steps(act, f.n, body, 1, 2)

        def dve_ffn(dve, f):
            m = f.hw // 2
            experts = Experts(dve, f)

            def body(s0, u):
                if live(s0, u, f.n):
                    t, h = s0 + u, u % 2
                    if f.b_in is not None:
                        e = experts.of(u)
                    dve.wait_ge(f.h_mm, t + 1)
                    wait(dve, f.h_turned, t - 1)
                    if f.kind == "leaky":
                        dve.wait_ge(f.h_pre, t + 1)
                        nc.vector.tensor_tensor(hbuf[:, h, 0:m], hbuf[:, h, 0:m], psH[:, h, 0:m], ALU.max
                                                ).then_inc(f.h_gate, 1)
                        dve.wait_ge(f.h_gate, t + 1)
                        nc.vector.tensor_tensor(hbuf[:, h, 0:m], hbuf[:, h, 0:m], psH[:, h, m:2 * m], ALU.mult
                                                ).then_inc(f.h_ready, 1)
                    else:
                        nc.vector.tensor_tensor(hbuf[:, h, 0:f.hw], psH[:, h, 0:f.hw], f.b_in(e), ALU.add
                                                ).then_inc(f.h_pre, 1)
                if f.b_in is not None:
                    experts.fetch(s0, u + 1)
                if live(s0, u, f.n) and f.kind == "silu":
                    t, h = s0 + u, u % 2
                    dve.wait_ge(f.h_gate, t + 1)
                    nc.vector.tensor_tensor(hbuf[:, h, 0:m], hbuf[:, h, 0:m], hbuf[:, h, m:2 * m], ALU.mult
                                            ).then_inc(f.h_ready, 1)
                if live(s0, u - 2, f.n):
                    t, r = s0 + (u - 2), (u - 2) % RING
                    if f.b_out is not None:
                        e = experts.of(u - 2)
                    dve.wait_ge(f.y_mm, t + 1)
                    wait_slot_free(dve, f.st.slots_stored, s0, u - 2)
                    dst = ys[:, r, :]
                    if f.b_out is None:
                        nc.vector.tensor_copy(dst, ffn_y[u % 2]).then_inc(f.y_out, 1)
                    else:
                        nc.vector.tensor_tensor(dst, ffn_y[u % 2], f.b_out(e), ALU.add).then_inc(f.y_out, 1)
            if f.b_in is not None:
                experts.fetch(0, 0)
            steps(dve, f.n, body, 1, 2)

        def dve_route(dve, st):
            E, NT, n = st.E, st.NT, TT * st.E
            count = [0]

            def done(ins):
                count[0] += 1
                ins.then_inc(st.route_step, 1)
                dve.wait_ge(st.route_step, count[0])

            def te(ap):
                return ap[:, 0:n].rearrange("p (t e) -> p t e", e=E)

            def et(ap):
                return ap[:, 0:n].rearrange("p (e t) -> p e t", e=E)

            def as_te(ap):
                return ap[:, 0:n].rearrange("p (e t) -> p t e", e=E)

            def per_token(ap):
                return ap.unsqueeze(2).to_broadcast([P, TT, E])

            v = nc.vector
            lg, key, tmp, oh1, oh2, sc = (te(a) for a in (rt_lg, rt_key, rt_tmp, rt_oh1, rt_oh2, rt_sc))
            best, w1, w2, den = (rt_small[:, i * TT:(i + 1) * TT] for i in range(4))
            c_e, nt_e, end_e, base_e = (rt_small[:, 64 + i * 16:64 + i * 16 + E] for i in range(4))
            half = rt_small[:, 128:160]
            row_f = rt_small[:, 160:192]
            slot_f = rt_small[:, 192:224]
            dve.wait_ge(st.logits_done, TT)
            lps = psL[:, 0:n].rearrange("p (t e) -> p t e", e=E)
            if st is A:
                lb = lg.rearrange("p (b i) e -> p b i e", i=QT)
                pb = psL[:, 0:n].rearrange("p (b i e) -> p b i e", i=QT, e=E)
                for i in range(QT):
                    done(v.tensor_tensor(lb[:, :, i, :], pb[:, :, i, :], lg_g[:, :, :], ALU.add))
            elif st is B:
                done(v.tensor_tensor(lg, lps, b_bg[:, :].unsqueeze(1).to_broadcast([P, TT, E]), ALU.add))
            else:
                v.tensor_copy(lg, lps).then_inc(st.exp_wanted, 1)
                dve.wait_ge(st.exp_wanted, 1)
                done(v.tensor_tensor(key, lg, d_eb[:, :].unsqueeze(1).to_broadcast([P, TT, E]), ALU.add))
            if st is not D:
                done(v.tensor_reduce(best, lg, AX_X, ALU.max))
                v.tensor_tensor(lg, lg, per_token(best), ALU.subtract).then_inc(st.exp_wanted, 1)
                dve.wait_ge(st.exp_done, 1)
                done(v.tensor_reduce(den, sc, AX_X, ALU.add))
                done(v.reciprocal(den, den))
                done(v.tensor_tensor(sc, sc, per_token(den), ALU.mult))
                key = sc
            rank = rank8[:, 16 - E:16].unsqueeze(1).to_broadcast([P, TT, E])
            for oh, w in ((oh1, w1), (oh2, w2)):
                done(v.tensor_reduce(best, key, AX_X, ALU.max))
                done(v.tensor_tensor(tmp, key, per_token(best), ALU.is_equal))
                done(v.tensor_tensor(tmp, tmp, rank, ALU.mult))
                done(v.tensor_reduce(den, tmp, AX_X, ALU.max))
                done(v.tensor_tensor(oh, tmp, per_token(den), ALU.is_equal))
                if st is D:
                    if oh is oh1:
                        dve.wait_ge(st.exp_done, 1)
                    done(v.tensor_tensor(tmp, oh, sc, ALU.mult))
                    done(v.tensor_reduce(w, tmp, AX_X, ALU.add))
                else:
                    done(v.tensor_copy(w, best))
                if oh is oh1:
                    done(v.scalar_tensor_tensor(out=te(rt_key), in0=oh, scalar=LOWEST, in1=key, op0=ALU.mult, op1=ALU.add))
                    key = te(rt_key)
            v.tensor_tensor(oh16[:, 0:n].rearrange("p (t e) -> p t e", e=E), oh1, oh2, ALU.add).then_inc(st.onehot_ready, 1)
            done(v.tensor_tensor(den, w1, w2, ALU.add))
            done(v.tensor_scalar(den, den, st.eps, None, ALU.add))
            done(v.reciprocal(den, den))
            v.tensor_tensor(gates[:, 0, :], w1, den, ALU.mult)
            done(v.tensor_tensor(gates[:, 1, :], w2, den, ALU.mult))
            dve.wait_ge(st.prefix_done, 1)
            within, total = et(psM[:, 0:256]), et(psM[:, 256:512])
            incl = rt_lg[:, 0:n]
            done(v.tensor_tensor_scan(incl, not_first[:, 0:E, :].rearrange("p e t -> p (e t)"), psM[:, 256:256 + n],
                                      0.0, ALU.mult, ALU.add))
            incl = et(rt_lg)
            done(v.tensor_copy(c_e, incl[:, :, TT - 1:TT].rearrange("p e o -> p (e o)")))
            done(v.tensor_tensor(et(rt_tmp), c_e.unsqueeze(2).to_broadcast([P, E, TT]),
                                 iota_128[:, :].unsqueeze(1).to_broadcast([P, E, TT]), ALU.is_gt))
            done(v.tensor_reduce(nt_e, et(rt_tmp), AX_X, ALU.add))
            done(v.tensor_tensor_scan(end_e, ones_f[:, 0:E], nt_e, 0.0, ALU.mult, ALU.add))
            done(v.tensor_tensor(base_e, end_e, nt_e, ALU.subtract))
            done(v.tensor_scalar(base_e, base_e, float(P), None, ALU.mult))
            done(v.tensor_tensor(et(rt_pos), incl, total, ALU.subtract))
            done(v.tensor_tensor(et(rt_pos), et(rt_pos), within, ALU.add))
            done(v.tensor_tensor(et(rt_pos), et(rt_pos), base_e.unsqueeze(2).to_broadcast([P, E, TT]), ALU.add))
            for c, oh in enumerate((oh1, oh2)):
                done(v.tensor_tensor(tmp, oh, as_te(rt_pos), ALU.mult))
                done(v.tensor_reduce(slot_f[:, c * TT:(c + 1) * TT], tmp, AX_X, ALU.add))
            slot_i = slot_u[:, :]
            done(v.tensor_copy(slot_i, slot_f))
            hi = half.bitcast(I32)
            done(v.tensor_scalar(hi, slot_i.bitcast(I32), P - 1, None, ALU.bitwise_and))
            done(v.tensor_copy(row_f, hi))
            done(v.tensor_scalar(hi, slot_i.bitcast(I32), 7, None, ALU.logical_shift_right))
            done(v.tensor_copy(slot_f, hi))
            eq = eq_tile[:, 0:2 * TT * NT].rearrange("p (k a) -> p k a", a=NT)
            done(v.tensor_tensor(eq, slot_f.unsqueeze(2).to_broadcast([P, 2 * TT, NT]),
                                 iota_t[:, 0:NT].unsqueeze(1).to_broadcast([P, 2 * TT, NT]), ALU.is_equal))
            done(v.tensor_tensor(eq, eq, token_id1[:, :, :].rearrange("p c t -> p (c t)").unsqueeze(2).to_broadcast([P, 2 * TT, NT]),
                                 ALU.mult))
            for k in range(0, 2 * TT, QUAD):
                v.tensor_tensor(eq_row[:, k:k + QUAD, :], row_f[:, k:k + QUAD].unsqueeze(2).to_broadcast([P, QUAD, P]),
                                iota_p16[:, :].unsqueeze(1).to_broadcast([P, QUAD, P]), ALU.is_equal).then_inc(st.eqrow_ready, 1)
            cmp = rt_tmp[0:1, :]
            spare = rt_pos[0:1, 0:len_te]
            for a in range(0, len_te, TT):
                w = TT
                c3 = cmp[:, 0:w * E].rearrange("p (t e) -> p t e", e=E)
                done(v.tensor_tensor(c3, end_e[0:1, :].unsqueeze(1).to_broadcast([1, w, E]),
                                     iota_t[0:1, a:a + w].unsqueeze(2).to_broadcast([1, w, E]), ALU.is_le))
                done(v.tensor_reduce(spare[:, a:a + w], c3, AX_X, ALU.add))
            done(v.tensor_scalar(spare, spare, float(E - 1), None, ALU.min))
            done(v.tensor_copy(tile_expert[0:1, :], spare))
            dve.wait_ge(st.inv_done, 1)
            done(v.tensor_copy(inv_c[:, :, 0:NT], psL[:, 0:128].rearrange("p (c a) -> p c a", c=2)[:, :, 0:NT]))
            both = home_f[:, 0:NT]
            done(v.tensor_tensor(both, inv_c[:, 0, 0:NT], inv_c[:, 1, 0:NT], ALU.add))
            v.tensor_scalar(inv[:, 0:NT], both, -1.0, 0.0, ALU.add, ALU.max).then_inc(st.routed, 1)
            past = inv_c[:, 0, 0:NT]
            done(v.tensor_scalar(inv_c[:, 1, 0:NT], inv_c[:, 1, 0:NT], 0.0, float(TOKENS), ALU.is_gt, ALU.mult))
            done(v.scalar_tensor_tensor(out=past, in0=both, scalar=0.0, in1=past_row[:, 0:NT], op0=ALU.is_equal, op1=ALU.mult))
            done(v.tensor_tensor(both, both, inv_c[:, 1, 0:NT], ALU.add))
            v.scalar_tensor_tensor(out=home[:, 0:NT], in0=both, scalar=-1.0, in1=past, op0=ALU.add, op1=ALU.add
                                   ).then_inc(st.routed, 1)

        def act_route(act, st):
            n = TT * st.E
            act.wait_ge(st.exp_wanted, 1)
            act_f, scale = {"a": (ACT.Exp, 0.5), "b": (ACT.Exp, 0.2), "d": (ACT.Sigmoid, 1.0)}[st.name]
            nc.scalar.activation(rt_sc[:, 0:n], rt_lg[:, 0:n], act_f, scale=scale).then_inc(st.exp_done, 1)

        def pool_gather_rows(pool, st, first, last):
            f = st.ffn
            if first == 0:
                pool.wait_ge(st.routed, 1)
                if st is not A:
                    wait_dmas(pool, st.token_stored)
            for t in range(first, last):
                wait(pool, f.turned, t - RING + 1)
                pool.indirect_dma_start(out=xs[:, t % RING, :], out_offset=None, in_=st.src,
                                        in_offset=bass.IndirectOffsetOnAxis(ap=inv[:, t:t + 1], axis=0)
                                        ).then_inc(f.loaded.sems[t % RING], 16)

        def pool_scatter_rows(pool, st, t):
            if t == 0:
                pool.wait_ge(st.routed, 2)
            pool.wait_ge(st.ffn.y_out, t + 1)
            pool.indirect_dma_start(out=st.pair_dram, out_offset=bass.IndirectOffsetOnAxis(ap=home[:, t:t + 1], axis=0),
                                    in_=ys[:, t % RING, :], in_offset=None).then_inc(st.slots_stored.sems[t % RING], 16)

        def pool_slots(pool, st, between=None):
            behind = RING + 3
            for t in range(RING, st.NT + behind):
                if t < st.NT:
                    pool_gather_rows(pool, st, t, t + 1)
                if t >= behind:
                    pool_scatter_rows(pool, st, t - behind)
                if between is not None:
                    between(pool, t)

        def pair_rows(st, t):
            pairs = st.pair_dram[0:PAIRS, :].rearrange("(c t p) d -> t p c d", c=2, p=P)
            return pairs[bass.ds(t, 1), :, :, :].rearrange("o p c d -> (o p) c d")

        def sp_combine(sp, st, store):
            def load(s0, u):
                sp.dma_start(gat[:, u, :, :], pair_rows(st, s0 + u)).then_inc(st.gathered.sems[u], 16)

            wait_dmas(sp, st.slots_stored)
            for u in range(RING):
                load(0, u)

            def body(s0, u):
                sp.wait_ge(st.combined, s0 + u + 1)
                store(s0, u)
                if live(s0, u + RING, TT):
                    load(s0 + RING, u)
            steps(sp, TT, body, RING, 0)

        C = Attention(sem, 16 * 6)


        def pe_q(pe, pair, j, b):
            if j == 0:
                pe.wait_ge(C.xnT_ready, 2 * b + 2)
            wait(pe, C.qT_ready, pair)
            for k in range(KD):
                last = pe.matmul(psY[:, 0:SEQ], c_wq[:, k, j * P:(j + 1) * P], c_xnT[:, k, :],
                                 start=(k == 0), stop=(k == KD - 1))
            last.then_inc(C.q_mm, 1)

        def pe_scores(pe, g, h, b):
            pe.wait_ge(C.qT_ready, 8 * b + h // 2 + 1)
            if h == 0:
                pe.wait_ge(C.kT_ready, 2 * b + 2)
            wait(pe, C.score_ready, g - 1)
            q = c_qT[:, (h // 2) % 2, :]
            pe.matmul(psH[:, h % 2, 0:KEYS0], q[:, 0:P], c_kT[:, h % 2, 0:KEYS0], start=True, stop=True)
            pe.matmul(psH[:, h % 2, KEYS0:KEYS], q[:, P:2 * P], c_kT[:, h % 2, :], start=True, stop=True
                      ).then_inc(C.s_mm, 1)

        def pe_turn(pe, g, h):
            pe.wait_ge(C.pn_ready, g + 1)
            wait(pe, C.pT_ready, g - 1)
            for n, at in enumerate((1, KEYS0 + 1, KEYS0 + 1 + P)):
                last = pe.transpose(psHT[:, h % 2, n * P:(n + 1) * P], c_p[:, h % 2, at:at + P], ident[:, :])
            last.then_inc(C.p_turned, 1)

        def pe_sum(pe, pair, j, b):
            pe.wait_ge(C.pT_ready, 2 * pair + 2)
            if j == 0:
                pe.wait_ge(C.v_ready, b + 1)
            wait(pe, C.o_ready, pair)
            for n, keys, queries in ((0, 0, slice(0, SEQ)), (1, 1, slice(P, SEQ))):
                at = slice(n * SEQ, n * SEQ + queries.stop - queries.start)
                for o in range(2):
                    last = pe.matmul(psL[DH * o:DH * o + DH, queries], c_v[:, keys, :], c_pT[:, o, at],
                                     start=(n == 0), stop=(n == 1))
            last.then_inc(C.pv_mm, 1)

        def pe_out(pe, b):
            pe.wait_ge(C.o_ready, 8 * b + 8)
            wait(pe, C.ao_ready, b)
            wait(pe, C.ao_stat, 2 * b)
            for i in range(QT):
                for j in range(NPAIR):
                    last = pe.matmul(psM[:, i * DIM:(i + 1) * DIM], c_oT[:, j, i * P:(i + 1) * P], c_wo[:, j, :],
                                     start=(j == 0), stop=(j == NPAIR - 1))
            last.then_inc(C.wo_mm, 1)

        def pe_rows(pe, b):
            pe.wait_ge(C.xn_ready, 2 * b + 2)
            wait(pe, C.v_ready, b)
            for i in range(QT):
                for k in range(KD):
                    last = pe.transpose(rows_x[:, k, i, :], c_xn[:, i, k * P:(k + 1) * P], ident[:, :])
            last.then_inc(C.xn_turned, 1)

        def pe_kv(pe, b):
            pe.wait_ge(C.xnT_ready, 2 * b + 2)
            for k in range(KD):
                pe.matmul(keys_x, c_wkk[:, k, :], c_xnT[:, k, :],
                          start=(k == 0), stop=(k == KD - 1))
            for i in range(QT):
                for k in range(KD):
                    last = pe.matmul(values_x[:, i, :], c_xnT[:, k, i * P:(i + 1) * P], c_wvv[:, k, :],
                                     start=(k == 0), stop=(k == KD - 1))
            last.then_inc(C.kv_mm, 1)

        def pe_batch(pe, b, first, last):
            for h in range(HEADS):
                g = 16 * b + h
                if not (last and h >= 14):
                    pe_scores(pe, g + 2, (h + 2) % HEADS, b + (h + 2) // HEADS)
                if h % 2 == 1 and not (last and h >= 13):
                    j = (h + 3) // 2
                    pe_q(pe, 8 * b + j, j % NPAIR, b + j // NPAIR)
                if h == 1 and not first:
                    pe_out(pe, b - 1)
                if h % 2 == 0 and h > 0:
                    pe_sum(pe, 8 * b + h // 2 - 1, h // 2 - 1, b)
                elif h == 0 and not first:
                    pe_sum(pe, 8 * b - 1, NPAIR - 1, b - 1)
                if h == 11 and not last:
                    pe_rows(pe, b + 1)
                if h == 12 and not last:
                    pe_kv(pe, b + 1)
                pe_turn(pe, g, h)

        def batches(eng, batch, after_first=None):
            batch(eng, 0, True, False)
            if after_first is not None:
                after_first(eng)
            with eng.Fori(1, BATCH - 1) as b:
                batch(eng, b, False, False)
            batch(eng, BATCH - 1, False, True)

        def pe_attention(pe):
            pe.wait_ge(C.kT_fixed, 4)
            pe_rows(pe, 0)
            pe_kv(pe, 0)
            pe_q(pe, 0, 0, 0)
            pe_q(pe, 1, 1, 0)
            pe_scores(pe, 0, 0, 0)
            pe_scores(pe, 1, 1, 0)
            batches(pe, pe_batch)
            pe_sum(pe, NPAIR * BATCH - 1, NPAIR - 1, BATCH - 1)
            pe_out(pe, BATCH - 1)

        def act_rowsT(act, b):
            act.wait_ge(C.xn_turned, b + 1)
            wait(act, C.q_mm, 8 * b)
            wait(act, C.kv_mm, b)
            for k in range(KD):
                nc.scalar.activation(c_xnT[:, k, :], rows_x[:, k, :, :].rearrange("p i n -> p (i n)"), ACT.Identity,
                                     scale=g_in[:, k:k + 1]).then_inc(C.xnT_ready, 1)

        def act_mask(act, b):
            wait(act, C.bm_ready, 16 * b)
            m = mask8[:, bass.ds(b, 1), :].rearrange("p o n -> p (o n)")
            for dst, src in ((c_mp[:, 1:KEYS0], m[:, 0:P]), (c_mp[:, KEYS0 + 1:KEYS], m)):
                nc.scalar.activation(dst, src, ACT.Copy, scale=-HIDDEN_KEY, bias=HIDDEN_KEY).then_inc(C.mask_ready, 1)

        def act_q(act, pair, j):
            act.wait_ge(C.q_mm, pair + 1)
            wait(act, C.s_mm, 2 * pair - 2)
            nc.scalar.mul(c_qT[:, j % 2, :], psY[:, 0:SEQ], -(float(DH) ** -0.5)).then_inc(C.qT_ready, 1)

        def act_exp(act, g, h):
            act.wait_ge(C.score_ready, g + 1)
            wait(act, C.p_turned, g - 1)
            for i, (a, z) in enumerate(((0, KEYS0), (KEYS0, KEYS))):
                nc.scalar.activation(c_p[:, h % 2, a:z], c_sc[:, h % 2, a:z], ACT.Exp, scale=-1.0,
                                     bias=c_min[:, h % 2, i:i + 1], accum_out=c_sum[:, h % 2, i:i + 1]
                                     ).then_inc(C.p_ready, 1)

        def act_o(act, pair, j, b):
            act.wait_ge(C.pv_mm, pair + 1)
            if j == 0:
                wait(act, C.wo_mm, b)
            nc.scalar.activation(c_oT[:, j, :], psL[:, 0:SEQ], ACT.Identity, bias=nv2[:, 0:1]).then_inc(C.o_ready, 1)

        def act_out(act, b):
            act.wait_ge(C.wo_mm, b + 1)
            nc.scalar.copy(acc[:, bass.ds(2 * b, 2), :].rearrange("p i n -> p (i n)"), psM[:, :]).then_inc(C.ao_ready, 1)

        def act_batch(act, b, first, last):
            for h in range(HEADS):
                g = 16 * b + h
                if h % 2 == 1 and not (last and h >= 13):
                    j = (h + 3) // 2
                    act_q(act, 8 * b + j, j % NPAIR)
                if not (last and h >= 14):
                    act_exp(act, g + 2, (h + 2) % HEADS)
                if h == 11 and not last:
                    act_rowsT(act, b + 1)
                if h == 13 and not last:
                    act_mask(act, b + 1)
                if h == 2 and not first:
                    act_out(act, b - 1)
                if h % 2 == 0 and h > 0:
                    act_o(act, 8 * b + h // 2 - 1, h // 2 - 1, b)
                elif h == 0 and not first:
                    act_o(act, 8 * b - 1, NPAIR - 1, b - 1)

        def act_load_d(act):
            act.wait_ge(fB.y_out, B.NT)
            for dst, name in ((d_w13, "d_w13"), (d_w2, "d_w2"), (d_s13, "d_s13"), (d_s2, "d_s2"), (d_sb13, "d_sb13")):
                act.dma_start(dst, io[name]).then_inc(D.weights_loaded, 16)
            for dst, name in ((d_b13, "d_b13"), (d_b2, "d_b2")):
                act_broadcast(act, dst, name, D.weights_loaded)

        def act_attention(act):
            act_rowsT(act, 0)
            act_mask(act, 0)
            act_q(act, 0, 0)
            act_q(act, 1, 1)
            act_exp(act, 0, 0)
            act_exp(act, 1, 1)
            batches(act, act_batch, act_load_d)
            act_o(act, 8 * BATCH - 1, NPAIR - 1, BATCH - 1)
            act_out(act, BATCH - 1)

        def dve_first(dve, b):
            dve.wait_ge(C.pairs_loaded, 32 * b + 32)
            for i in range(QT):
                row = one(x2[:, :, :], 2 * b + i)
                nc.vector.scalar_tensor_tensor(out=row, in0=c_gat[:, i, 0, :], scalar=gates[:, 0, bass.ds(2 * b + i, 1)], in1=row,
                                               op0=ALU.mult, op1=ALU.add).then_inc(B.combine_step, 1)

        def dve_second(dve, b):
            dve.wait_ge(B.combine_step, 2 * b + 2)
            for i in range(QT):
                row = one(x2[:, :, :], 2 * b + i)
                nc.vector.scalar_tensor_tensor(out=row, in0=c_gat[:, i, 1, :], scalar=gates[:, 1, bass.ds(2 * b + i, 1)], in1=row,
                                               op0=ALU.mult, op1=ALU.add).then_inc(B.combined, 1)

        def dve_row_stats(dve, b):
            for i in range(QT):
                nc.vector.bn_stats(in_stats[:, i, :], one(x2[:, :, :], 2 * b + i)).then_inc(C.stat, 1)

        def dve_row_moments(dve, b):
            for i in range(QT):
                nc.vector.bn_aggr(in_mv[:, i, :], in_stats[:, i, :]).then_inc(C.mom_done, 1)

        def dve_row_variances(dve, b):
            dve.wait_ge(C.mom_done, 2 * b + 2)
            nc.vector.tensor_scalar(in_rstd[:, :], in_mv[:, :, 1:2].rearrange("p i o -> p (i o)"), LN_EPS, None, ALU.add
                                    ).then_inc(C.var_done, 1)

        def dve_rows(dve, b):
            dve.wait_ge(C.rstd_done, b + 1)
            wait(dve, C.xn_turned, b)
            for i in range(QT):
                nc.vector.tensor_scalar(c_xn[:, i, :], one(x2[:, :, :], 2 * b + i), in_mv[:, i, 0:1], in_rstd[:, i:i + 1],
                                        ALU.subtract, ALU.mult).then_inc(C.xn_ready, 1)

        def dve_k(dve, b):
            dve.wait_ge(C.kv_mm, b + 1)
            wait(dve, C.s_mm, 16 * b)
            for o in range(2):
                half = slice(DH * o, DH * o + DH)
                nc.vector.tensor_copy(c_kT[half, o, 1:KEYS1], keys_x[half, :]
                                      ).then_inc(C.kT_ready, 1)

        def dve_v(dve, b):
            dve.wait_ge(C.kv_mm, b + 1)
            wait(dve, C.pv_mm, 8 * b)
            nc.vector.tensor_tensor(c_v, values_x[:, :, 0:DH], nvb[:, :].unsqueeze(1).to_broadcast([P, QT, DH]), ALU.subtract
                                    ).then_inc(C.v_ready, 1)

        def dve_scores(dve, g, h):
            for i, (a, z) in enumerate(((0, KEYS0), (KEYS0, KEYS))):
                last = nc.vector.tensor_tensor_reduce(c_sc[:, h % 2, a:z], psH[:, h % 2, a:z], c_bm[:, h % 2, a:z], 1.0, -LOWEST,
                                                      ALU.add, ALU.min, c_min[:, h % 2, i:i + 1])
            last.then_inc(C.score_ready, 1)

        def dve_scores_wait(dve, g):
            dve.wait_ge(C.s_mm, g + 1)
            dve.wait_ge(C.bm_ready, g + 1)

        def dve_sums(dve, g, h):
            dve.wait_ge(C.p_ready, 2 * g + 2)
            nc.vector.reciprocal(c_rec[:, h % 2, :], c_sum[:, h % 2, :]).then_inc(C.rec_ready, 1)

        def dve_norm(dve, g, h):
            dve.wait_ge(C.rec_ready, g + 1)
            nc.vector.tensor_scalar(c_p[:, h % 2, 1:KEYS0], c_p[:, h % 2, 1:KEYS0], c_rec[:, h % 2, 0:1], None, ALU.mult)
            own = c_p[:, h % 2, KEYS0 + 1:KEYS]
            nc.vector.tensor_scalar(own, own, c_rec[:, h % 2, 1:2], None, ALU.mult).then_inc(C.pn_ready, 1)

        def dve_pT(dve, g, h, b):
            dve.wait_ge(C.p_turned, g + 1)
            if h % 2 == 0:
                wait(dve, C.pv_mm, 8 * b + h // 2)
            nc.vector.tensor_copy(c_pT[:, h % 2, :], psHT[:, h % 2, 0:3 * P]).then_inc(C.pT_ready, 1)

        def dve_ao_stats(dve, b):
            for i in range(QT):
                nc.vector.bn_stats(stats[:, bass.ds(2 * b + i, 1), :].rearrange("p a n -> p (a n)"),
                                   psM[:, i * DIM:(i + 1) * DIM]).then_inc(C.ao_stat, 1)


        def dve_batch(dve, b, first, last):
            for h in range(HEADS):
                g = 16 * b + h
                if h == 10 and not last:
                    dve_rows(dve, b + 1)
                if h == 14 and not last:
                    dve_k(dve, b + 1)
                if h == 4 and not first:
                    dve.wait_ge(C.ao_ready, b)
                if h == 5 and not last:
                    dve.wait_ge(B.combined, 2 * b + 4)
                if h == 6 and not last:
                    dve.wait_ge(C.stat, 2 * b + 4)
                if not (last and h >= 14):
                    dve_scores_wait(dve, g + 2)
                if not (last and h >= 15):
                    dve_sums(dve, g + 1, (h + 1) % HEADS)
                if not (last and h >= 14):
                    dve_scores(dve, g + 2, (h + 2) % HEADS)
                if h == 4 and not first:
                    dve_ao_stats(dve, b - 1)
                if h == 5 and not last:
                    dve_row_stats(dve, b + 1)
                if h == 6 and not last:
                    dve_row_moments(dve, b + 1)
                dve_pT(dve, g, h, b)
                if not (last and h >= 15):
                    dve_norm(dve, g + 1, (h + 1) % HEADS)
                if h == 0 and not first:
                    dve_v(dve, b)
                if not last:
                    if h == 2:
                        dve_first(dve, b + 1)
                    elif h == 3:
                        dve_second(dve, b + 1)
                    elif h == 6:
                        dve_row_variances(dve, b + 1)

        def dve_attention(dve):
            nc.vector.memset(c_kT[DH:P, 0, :], 0.0).then_inc(C.kT_fixed, 1)
            nc.vector.memset(c_kT[0:DH, 1, :], 0.0).then_inc(C.kT_fixed, 1)
            nc.vector.tensor_copy(c_kT[0:DH, 0, 0:1], nk2[0:DH, :]).then_inc(C.kT_fixed, 1)
            nc.vector.tensor_copy(c_kT[DH:P, 1, 0:1], nk2[DH:P, :]).then_inc(C.kT_fixed, 1)
            dve.wait_ge(x_loaded, 16)
            dve_first(dve, 0)
            dve_second(dve, 0)
            dve.wait_ge(B.combined, 2)
            dve_row_stats(dve, 0)
            dve.wait_ge(C.stat, 2)
            dve_row_moments(dve, 0)
            dve_row_variances(dve, 0)
            dve_rows(dve, 0)
            dve_k(dve, 0)
            dve_v(dve, 0)
            for g in range(2):
                dve_scores_wait(dve, g)
                dve_scores(dve, g, g)
            dve_sums(dve, 0, 0)
            dve_norm(dve, 0, 0)
            batches(dve, dve_batch)
            dve.wait_ge(C.ao_ready, BATCH)
            dve_ao_stats(dve, BATCH - 1)
            dve.wait_ge(C.ao_stat, TT)
            for t in range(TT):
                last = nc.vector.bn_aggr(mv[:, t, :], stats[:, t, :])
            last.then_inc(C.out_mom, 1)
            dve.wait_ge(C.out_mom, 1)
            nc.vector.tensor_scalar(rstd[:, :], mv[:, :, 1:2].rearrange("p t o -> p (t o)"), LN_EPS, None, ALU.add
                                    ).then_inc(C.out_var, 1)
            dve.wait_ge(C.out_rstd, 1)

        def pool_bm(pool, b, g, h):
            if h == 0:
                pool.wait_ge(C.mask_ready, 2 * b + 2)
            wait(pool, C.score_ready, g - 1)
            pool.tensor_tensor(c_bm[:, h % 2, :], c_mp, c_bias[:, h, :], ALU.subtract).then_inc(C.bm_ready, 1)

        def pool_row_rstd(pool, b):
            pool.wait_ge(C.var_done, b + 1)
            pool.tensor_tensor(in_rstd[:, :], in_rstd[:, :], minus_half[:, 0:QT], ALU.pow).then_inc(C.rstd_done, 1)

        def pool_add_bias(pool, b):
            pool.wait_ge(C.xn_ready, 2 * b + 2)
            for i in range(QT):
                row = one(x2[:, :, :], 2 * b + i)
                pool.tensor_tensor(row, row, d_sb2[:, :], ALU.add).then_inc(C.x_biased, 1)

        def pool_batch(pool, b, first, last):
            for h in range(HEADS):
                g = 16 * b + h
                if h == 9:
                    pool_add_bias(pool, b)
                if not (last and h >= 14):
                    pool_bm(pool, b + (h + 2) // HEADS, g + 2, (h + 2) % HEADS)
                if h == 7 and not last:
                    pool_row_rstd(pool, b + 1)

        def pool_biases(pool, t):
            n = t - RING - 20
            if n == 0:
                pool.wait_ge(C.loaded, C.loads)
            if n in (0, 1):
                a = (0, KEYS0)[n]
                pool.tensor_copy(c_bias[:, :, a:a + 1].rearrange("p h o -> p (h o)"), nullb[:, :]).then_inc(C.bias_ready, 1)
            elif n in (2, 4):
                a = (1, KEYS0 + 1 + P)[(n - 2) // 2]
                own = c_bias[:, :, a:a + P]
                pool.affine_select(out=own, in_=own, compare_op=ALU.is_ge, fill=-HIDDEN_KEY, base=0,
                                   pattern=[[0, HEADS], [-1, P]], channel_multiplier=1).then_inc(C.bias_ready, 1)

        def pool_attention(pool):
            for a in (0, KEYS0):
                pool.memset(c_mp[:, a:a + 1], 0.0).then_inc(C.bias_ready, 1)
            pool.wait_ge(C.bias_ready, 6)
            pool_row_rstd(pool, 0)
            pool_bm(pool, 0, 0, 0)
            pool_bm(pool, 0, 1, 1)
            batches(pool, pool_batch)
            pool.wait_ge(C.out_var, 1)
            pool.tensor_tensor(rstd[:, :], rstd[:, :], minus_half[:, :], ALU.pow).then_inc(C.out_rstd, 1)

        def sp_pairs(sp, b):
            wait(sp, B.combined, 2 * b)
            for i in range(QT):
                sp.dma_start(c_gat[:, i, :, :], pair_rows(B, 2 * b + i)).then_inc(C.pairs_loaded, 16)

        def sp_attention(sp):
            wait_dmas(sp, B.slots_stored)
            sp_pairs(sp, 0)
            with sp.Fori(1, BATCH) as b:
                sp_pairs(sp, b)

        def dve_combine(dve, st, tile):
            def body(s0, u):
                t = s0 + u
                wait_dma(dve, st.gathered, s0, u)
                tile(s0, u, t)
            steps(dve, TT, body, 0, 0)

        def weighted(st, c, u, t, dst, base):
            return nc.vector.scalar_tensor_tensor(out=dst, in0=gat[:, u, c, :], scalar=gates[:, c, bass.ds(t, 1)], in1=base,
                                                  op0=ALU.mult, op1=ALU.add)

        block = ctx.enter_context(nc.Block())

        x_chunk = Use(tokens_loaded, RING)
        out_stored = Use(tokens_stored, TT)

        @block.sync
        def _(sp):
            x_tiles = io["x"].rearrange("(t p) d -> p t d", p=P)
            for q in range(TT // QUAD):
                sp.dma_start(acc[:, q * QUAD:(q + 1) * QUAD, :], x_tiles[:, q * QUAD:(q + 1) * QUAD, :]
                             ).then_inc(x_chunk.sems[q], 16)

            def store_y0(s0, u):
                sp.dma_start(dram_tile(y0_dram, s0 + u), xr[:, u, :]).then_inc(B.token_stored.sems[u], 16)
            sp_combine(sp, A, store_y0)
            sp.wait_ge(fB.turned, RING)
            sp.dma_start(x2[:, :, :], x_tiles).then_inc(x_loaded, 16)
            for n, (dst, name) in enumerate(((c_wq, "c_wq"), (c_wkk, "c_wkk"), (c_wvv, "c_wvv"), (c_wo, "c_wo"))):
                sp.wait_ge(fB.turned, 2 * RING + 2 * n)
                sp.dma_start(dst, io[name]).then_inc(C.loaded, 16)
            bias = io["fside"].rearrange("h (i p) j -> i p h j", p=P)
            sp.dma_start(c_bias[:, :, 1:KEYS0], bias[0, :, :, 0:P]).then_inc(C.loaded, 16)
            sp.wait_ge(fB.turned, 4 * RING)
            sp.dma_start(c_bias[:, :, KEYS0 + 1:KEYS], bias[1]).then_inc(C.loaded, 16)
            sp_attention(sp)

            def store_z(s0, u):
                sp.wait_ge(D.token_ready, s0 + u + 1)
                sp.dma_start(dram_tile(z_dram, s0 + u), xr[:, u, :]).then_inc(D.token_stored.sems[u], 16)
            steps(sp, TT, store_z, 0, 0)

            def store_out(s0, u):
                sp.dma_start(dram_tile(io["out"], s0 + u), xr[:, u, :]).then_inc(out_stored.sems[u], 16)
            sp_combine(sp, D, store_out)
            wait_dmas(sp, out_stored)

        first = [(a_wt, "a_wt"), (condT, "condT"), (a_wgT, "a_wgT")]
        small = [(b_wg, "b_wg"), (d_gw, "d_gw"), (g_in, "g_in"),
                 (nv2, "nv2"), (nk2, "nk2")]
        spread = [(b_bg, "b_bg"), (d_eb, "d_eb"), (g_out, "g_out"), (d_sb2, "d_sb2"), (nvb, "nvb"), (nullb, "nullb"), (mask8, "mask")]

        def load_all(act, pairs, s):
            for dst, name in pairs:
                act.dma_start(dst[:], io[name]).then_inc(s, 16)

        @block.scalar
        def _(act):
            load_all(act, first, first_loaded)
            for dst, name in ((a_sgu, "a_sgu"), (a_sdown, "a_sdown"), (a_gu, "a_gu"), (a_down, "a_down")):
                act.dma_start(dst, io[name]).then_inc(A.weights_loaded, 16)
            act_router(act, A)
            load_all(act, small, consts_loaded)
            for dst, name in spread:
                act_broadcast(act, dst[:], name, consts_loaded)
            for dst, name in ((b_w1, "b_w1"), (b_w2, "b_w2")):
                act.dma_start(dst, io[name]).then_inc(B.weights_loaded, 16)
            act_broadcast(act, b_b1, "b_b1", B.weights_loaded)
            act_route(act, A)
            act_shared(act, A.shared, "leaky")
            act_ffn(act, fA)
            act_router(act, B)
            act_route(act, B)
            act_broadcast(act, b_b2, "b_b2", B.weights_loaded)
            act_ffn(act, fB)
            act_attention(act)
            act_router(act, D)
            act_route(act, D)
            act_shared(act, D.shared, "silu")
            act_ffn(act, fD)

        n_consts = 16 * (len(small) + len(spread))
        cond_step = sem("cond_step")

        @block.gpsimd
        def _(pool):
            pool.memset(ident[:, :], 0.0).then_inc(consts_made, 1)
            pool.memset(ones_f[:, :], 1.0).then_inc(consts_made, 1)
            pool.memset(minus_half[:, :], -0.5).then_inc(consts_made, 1)
            pool.memset(ones16[:, :], 1.0).then_inc(consts_made, 1)
            pool.memset(not_first[:, :, :], 1.0).then_inc(consts_made, 1)
            pool.iota(iota_p16[:, :], [[1, P]], base=0, channel_multiplier=0, allow_small_or_imprecise_dtypes=True).then_inc(consts_made, 1)
            pool.iota(iota_t[:, :], [[1, 48]], base=0, channel_multiplier=0, allow_small_or_imprecise_dtypes=True).then_inc(consts_made, 1)
            pool.iota(iota_128[:, :], [[P, TT]], base=0, channel_multiplier=0, allow_small_or_imprecise_dtypes=True).then_inc(consts_made, 1)
            pool.iota(token_id1[:, :, :], [[0, 2], [P, TT]], base=1, channel_multiplier=1, allow_small_or_imprecise_dtypes=True).then_inc(consts_made, 1)
            pool.iota(past_row[:, :], [[P, 48]], base=PAIRS + 1, channel_multiplier=1, allow_small_or_imprecise_dtypes=True).then_inc(consts_made, 1)
            pool.iota(rank8[:, :], [[-1, 16]], base=16, channel_multiplier=0, allow_small_or_imprecise_dtypes=True).then_inc(consts_made, 1)
            pool.wait_ge(consts_made, 11)
            pool.affine_select(out=ident[:, :], in_=ident[:, :], compare_op=ALU.not_equal, fill=1.0, base=0,
                               pattern=[[-1, P]], channel_multiplier=1).then_inc(consts_made, 1)
            pool.affine_select(out=before16[:, :], in_=ones16[:, :], compare_op=ALU.is_gt, fill=0.0, base=0,
                               pattern=[[1, P]], channel_multiplier=-1).then_inc(consts_made, 1)
            pool.memset(not_first[:, :, 0:1], 0.0).then_inc(consts_made, 1)
            pool_shared_and_gather(pool, A, "leaky")
            pool_slots(pool, A)
            pool_gather_rows(pool, B, 0, RING)
            pool_slots(pool, B, pool_biases)
            pool_attention(pool)
            pool_shared_and_gather(pool, D, "silu")
            pool_slots(pool, D)

        n_made = 14

        @block.tensor
        def _(pe):
            pe.wait_ge(consts_made, n_made)
            pe.wait_ge(first_loaded, 16 * len(first))
            pe.wait_ge(cond_step, 1)
            pe.matmul(psM[:, 0:64], ones_f[0:64, :], cg[:, :, :].rearrange("p b e -> p (b e)"), start=True, stop=True
                      ).then_inc(cond_step, 1)
            pe_router(pe, A, a_wt)
            pe.wait_ge(A.weights_loaded, A.loads)
            pe.wait_ge(cond_step, 3)
            pe_route_and_shared(pe, A)
            pe.wait_ge(A.routed, 1)
            pe.wait_ge(A.shared.y_out, TT)
            pe_ffn(pe, fA)
            pe.wait_ge(consts_loaded, n_consts)
            pe_router(pe, B, b_wg)
            pe_counts(pe, B)
            pe_invert(pe, B)
            pe.wait_ge(B.weights_loaded, B.loads)
            pe.wait_ge(B.routed, 1)
            pe.wait_ge(fA.y_out, A.NT)
            pe_ffn(pe, fB)
            pe.wait_ge(fB.y_out, B.NT)
            pe.wait_ge(C.loaded, C.loads)
            pe_attention(pe)
            pe_router(pe, D, d_gw)
            pe.wait_ge(D.weights_loaded, D.loads)
            pe_route_and_shared(pe, D)
            pe.wait_ge(D.routed, 1)
            pe.wait_ge(D.shared.y_out, TT)
            pe_ffn(pe, fD)

        @block.vector
        def _(dve):
            dve.wait_ge(first_loaded, 16 * len(first))
            for b in range(BATCH):
                last = nc.vector.tensor_scalar(cg[:, b, :], a_wgT[:, :], condT[:, b:b + 1], None, ALU.mult)
            last.then_inc(cond_step, 1)
            dve.wait_ge(cond_step, 2)
            nc.vector.tensor_copy(lg_g[:, :, :].rearrange("p b e -> p (b e)"), psM[:, 0:64]).then_inc(cond_step, 1)
            dve.wait_ge(cond_step, 3)
            dve.wait_ge(consts_made, n_made)
            dve_route(dve, A)
            dve_ffn(dve, fA)

            def combine_a(s0, u, t):
                wait(dve, B.tok_turned, t - RING + 1)
                wait_slot_free(dve, B.token_stored, s0, u)
                weighted(A, 0, u, t, xr[:, u, :], one(acc[:, :, :], t)).then_inc(A.combine_step, 1)
                dve.wait_ge(A.combine_step, t + 1)
                weighted(A, 1, u, t, xr[:, u, :], xr[:, u, :]).then_inc(A.combined, 1)
            dve_combine(dve, A, combine_a)
            dve.wait_ge(consts_loaded, n_consts)
            dve_route(dve, B)
            dve_ffn(dve, fB)
            dve_attention(dve)

            def normalise(s0, u):
                t = s0 + u
                wait(dve, D.tok_turned, t - RING + 1)
                wait_slot_free(dve, D.token_stored, s0, u)
                nc.vector.tensor_scalar(xr[:, u, :], one(acc[:, :, :], t), mv[:, bass.ds(t, 1), 0:1].rearrange("p a b -> p (a b)"),
                                        rstd[:, bass.ds(t, 1)], ALU.subtract, ALU.mult).then_inc(C.z_step, 1)
                dve.wait_ge(C.z_step, t + 1)
                nc.vector.tensor_tensor(xr[:, u, :], xr[:, u, :], g_out[:, :], ALU.mult).then_inc(D.token_ready, 1)
            steps(dve, TT, normalise, 0, 0)
            dve_route(dve, D)
            dve.wait_ge(D.weights_loaded, D.loads)

            def add_x(s0, u):
                row = one(acc[:, :, :], s0 + u)
                dve.wait_ge(D.shared.y_out, s0 + u + 1)
                nc.vector.tensor_tensor(row, row, one(x2[:, :, :], s0 + u), ALU.add).then_inc(C.base_ready, 1)
            dve.wait_ge(C.x_biased, TT)
            steps(dve, TT, add_x, 0, 0)
            dve_ffn(dve, fD)

            def combine_d(s0, u, t):
                wait_slot_free(dve, out_stored, s0, u)
                weighted(D, 0, u, t, xr[:, u, :], one(acc[:, :, :], t)).then_inc(D.combine_step, 1)
                dve.wait_ge(D.combine_step, t + 1)
                weighted(D, 1, u, t, xr[:, u, :], xr[:, u, :]).then_inc(D.combined, 1)
            dve.wait_ge(C.base_ready, TT)
            dve_combine(dve, D, combine_d)


def layout(inputs):
    import numpy as np

    def rows(w):
        return np.ascontiguousarray(w.reshape(-1, 128, w.shape[-1]).transpose(1, 0, 2))

    def expert_rows(w):
        e, k, n = w.shape
        return np.ascontiguousarray(w.reshape(e, k // 128, 128, n).transpose(2, 0, 1, 3))

    i = {k: np.asarray(v) for k, v in inputs.items()}
    cat = np.concatenate
    o = {}
    o["x"] = i["x"].reshape(2048, 256)
    o["condT"] = i["cond_64"].T
    o["a_wt"] = rows(i["L0_cond_wt"].T)
    o["a_wgT"] = i["L0_cond_wg"].T
    o["a_gu"] = expert_rows(cat([i["L0_cond_w_gate"], i["L0_cond_w_up"]], -1))
    o["a_down"] = i["L0_cond_w_down"].transpose(1, 0, 2)
    o["a_sgu"] = rows(cat([i["L0_cond_sw_gate"], i["L0_cond_sw_up"]], -1))
    o["a_sdown"] = rows(i["L0_cond_sw_down"])
    o["b_wg"] = rows(i["L0_ffn_Wg"])
    o["b_bg"] = i["L0_ffn_bg"].reshape(1, -1)
    o["b_w1"] = expert_rows(i["L0_ffn_W1"])
    o["b_w2"] = expert_rows(i["L0_ffn_W2"])
    o["b_b1"] = i["L0_ffn_b1"].reshape(1, -1)
    o["b_b2"] = i["L0_ffn_b2"].reshape(1, -1)
    o["g_in"] = i["L1_cond_g_in"].reshape(2, 128).T
    o["g_out"] = i["L1_cond_g_out"].reshape(1, -1)
    o["nullb"] = i["L1_cond_null_attn_bias"].reshape(1, -1)
    nk, nv = i["cond_64"][0], i["cond_64"][1]
    o["nk2"] = cat([nk, nk]).reshape(-1, 1)
    o["nv2"] = cat([nv, nv]).reshape(-1, 1)
    o["nvb"] = nv.reshape(1, -1)
    wk, wv = i["L1_cond_Wkv"][:, :64], i["L1_cond_Wkv"][:, 64:]
    o["c_wq"] = rows(i["L1_cond_Wq"])
    o["c_wkk"] = rows(cat([wk, wk], 1))
    o["c_wvv"] = rows(cat([wv, wv], 1))
    o["c_wo"] = rows(i["L1_cond_Wo"])
    o["fside"] = i["fside_16xSxS_0"]
    o["mask"] = i["mask_BxS_bk0"].reshape(1, -1)
    o["d_gw"] = rows(i["L1_ffn_gate_w"].T)
    o["d_eb"] = i["L1_ffn_expert_bias"].reshape(1, -1)
    o["d_w13"] = expert_rows(cat([i["L1_ffn_w1"], i["L1_ffn_w3"]], 1).transpose(0, 2, 1))
    o["d_b13"] = cat([i["L1_ffn_b1"], i["L1_ffn_b3"]], 1).reshape(1, -1)
    o["d_w2"] = i["L1_ffn_w2"].transpose(2, 0, 1)
    o["d_b2"] = i["L1_ffn_b2"].reshape(1, -1)
    o["d_s13"] = rows(cat([i["L1_ffn_sw1"], i["L1_ffn_sw3"]], 0).T)
    o["d_sb13"] = cat([i["L1_ffn_sb1"], i["L1_ffn_sb3"]], 0).reshape(-1, 128).T
    o["d_s2"] = rows(i["L1_ffn_sw2"].T)
    o["d_sb2"] = i["L1_ffn_sb2"].reshape(1, -1)
    return {k: np.ascontiguousarray(v) for k, v in o.items()}


def kernel(**inputs):
    import numpy as np
    import concourse.bacc as bacc
    from concourse.bass_utils import run_bass_kernel_spmd

    nc = bacc.Bacc("TRN2", target_bir_lowering=False, num_devices=1)
    arrays, io = {}, {}
    for name, a in layout(inputs).items():
        arrays[f"in_{name}"] = a
        io[name] = nc.dram_tensor(f"in_{name}", a.shape, mybir.dt.from_np(a.dtype), kind="ExternalInput").ap()
    io["out"] = nc.dram_tensor("out", (TOKENS, DIM), F32, kind="ExternalOutput").ap()
    build(nc, io)
    r = run_bass_kernel_spmd(nc, [arrays], core_ids=[0])
    return r.results[0]["out"].reshape(BATCH, SEQ, DIM)
```

```python
from contextlib import ExitStack

import concourse.bass as bass
from concourse import mybir

F32 = mybir.dt.float32
F16 = mybir.dt.float16
I32 = mybir.dt.int32
U32 = mybir.dt.uint32
U8 = mybir.dt.uint8
ALU = mybir.AluOpType
ACT = mybir.ActivationFunctionType
AX_X = mybir.AxisListType.X

P = 128
BATCH, SEQ, DIM = 8, 256, 256
TOKENS = BATCH * SEQ
TT = TOKENS // P
KD = DIM // P
PAIRS = 2 * TOKENS
RING = 4
ROWS = 8
AHEAD = 8
AHEAD_EARLY = 2
HEADS, DH = 16, 64
QT = SEQ // P
KEYS0, KEYS1 = 1 + P, 1 + SEQ
KEYS = KEYS0 + KEYS1
LN_EPS = 1e-5
HIDDEN_KEY = 1e30
LOWEST = -3e38
NPAIR = HEADS // 2
QUAD = 4
CHUNKS = 2
UNITS = CHUNKS * TT // QUAD


def slot_tiles(experts):
    return (PAIRS - experts) // P + experts


def live(s0, off, n):
    return not isinstance(s0, int) or 0 <= s0 + off < n


def wait(eng, sem, value):
    if not isinstance(value, int) or value > 0:
        eng.wait_ge(sem, value)


def steps(eng, n, body, lead, lag, first=RING, by=RING):
    lo = max(first, -(-lag // by) * by)
    hi = lo + (n - lead - lo) // by * by
    for s in range(0, lo):
        body(s - s % by, s % by)
    with eng.Fori(lo // by, hi // by) as i:
        for u in range(by):
            body(i * by, u)
    for s in range(hi, n + lag):
        body(s - s % by, s % by)


def one(ap, i):
    return ap[:, bass.ds(i, 1), :].rearrange("p o n -> p (o n)")


class Ring:
    def __init__(self, sem, name, depth=RING):
        self.sems = [sem(f"{name}{r}") for r in range(depth)]
        self.count = [0] * depth


class Use:
    def __init__(self, ring, tiles, dmas=1):
        self.sems, self.dmas = ring.sems, dmas
        self.before = list(ring.count)
        depth = len(ring.sems)
        for r in range(depth):
            ring.count[r] += 16 * dmas * len(range(r, tiles, depth))
        self.after = list(ring.count)


class Stage:
    def __init__(self, sem, name, experts, src, loads, eps):
        self.name, self.E, self.NT, self.src, self.loads, self.eps = name, experts, slot_tiles(experts), src, loads, eps
        self.weights_loaded = sem(f"{name}_weights_loaded")
        self.tok_turned = sem(f"{name}_tok_turned")
        self.tokT_ready = sem(f"{name}_tokT_ready")
        self.logits_done = sem(f"{name}_logits_done")
        self.route_step = sem(f"{name}_route_step")
        self.exp_wanted = sem(f"{name}_exp_wanted")
        self.exp_done = sem(f"{name}_exp_done")
        self.onehot_ready = sem(f"{name}_onehot_ready")
        self.prefix_done = sem(f"{name}_prefix_done")
        self.eqrow_ready = sem(f"{name}_eqrow_ready")
        self.inv_done = sem(f"{name}_inv_done")
        self.routed = sem(f"{name}_routed")
        self.combined = sem(f"{name}_combined")
        self.combine_step = sem(f"{name}_combine_step")


class Ffn:
    def __init__(self, sem, name, n, hw, hk, kind, st, w_in, w_out, b_in, b_out):
        self.name, self.n, self.hw, self.hk, self.kind, self.st = name, n, hw, hk, kind, st
        self.w_in, self.w_out, self.b_in, self.b_out = w_in, w_out, b_in, b_out
        self.turned = sem(f"{name}_turned")
        self.xT_ready = sem(f"{name}_xT_ready")
        self.h_mm = sem(f"{name}_h_mm")
        self.h_pre = sem(f"{name}_h_pre")
        self.h_gate = sem(f"{name}_h_gate") if kind != "gelu" else None
        self.h_ready = sem(f"{name}_h_ready")
        self.h_turned = sem(f"{name}_h_turned")
        self.hT_ready = sem(f"{name}_hT_ready")
        self.y_mm = sem(f"{name}_y_mm")
        self.y_out = sem(f"{name}_y_out")


class Shared:
    def __init__(self, sem, name, kept, xT, hT, parts, w_in, w_out, b_in, by_vector):
        self.xT, self.hT, self.parts, self.w_in, self.w_out, self.b_in = xT, hT, parts, w_in, w_out, b_in
        self.kept = kept
        self.by_vector = by_vector
        n_parts = parts.shape[2]
        vector_parts = 0 if b_in is None else 1
        self.parts_after = [sum(vector_parts if j in by_vector else n_parts for j in range(i + 1)) for i in range(UNITS)]
        self.leaky_after = [sum(2 if j in by_vector else 1 for j in range(i + 1)) for i in range(UNITS)]
        self.h_mm = sem(f"{name}_h_mm")
        self.part_ready = sem(f"{name}_part_ready")
        self.h_leaky = sem(f"{name}_h_leaky") if b_in is None else None
        self.h_ready = sem(f"{name}_h_ready")
        self.y_mm = sem(f"{name}_y_mm")
        self.y_out = sem(f"{name}_y_out")


class Attention:
    def __init__(self, sem, loads):
        self.loads = loads
        self.loaded = sem("c_loaded")
        self.pairs_loaded = sem("c_pairs_loaded")
        self.out_rstd = sem("c_out_rstd")
        self.x_biased = sem("c_x_biased")
        self.base_ready = sem("c_base_ready")
        self.var_done = sem("c_var_done")
        self.out_var = sem("c_out_var")
        self.row_step = sem("c_row_step")
        self.rstd_done = sem("c_rstd_done")
        self.bias_ready = sem("c_bias_ready")
        self.kT_fixed = sem("c_kT_fixed")
        self.xn_ready = sem("c_xn_ready")
        self.xn_turned = sem("c_xn_turned")
        self.xnT_ready = sem("c_xnT_ready")
        self.kv_mm = sem("c_kv_mm")
        self.kT_ready = sem("c_kT_ready")
        self.v_ready = sem("c_v_ready")
        self.q_mm = sem("c_q_mm")
        self.qT_ready = sem("c_qT_ready")
        self.s_mm = sem("c_s_mm")
        self.mask_ready = sem("c_mask_ready")
        self.bm_ready = sem("c_bm_ready")
        self.score_ready = sem("c_score_ready")
        self.p_ready = sem("c_p_ready")
        self.rec_ready = sem("c_rec_ready")
        self.pn_ready = sem("c_pn_ready")
        self.p_turned = sem("c_p_turned")
        self.pT_ready = [sem("c_pT_even"), sem("c_pT_odd")]
        self.pv_mm = sem("c_pv_mm")
        self.o_ready = sem("c_o_ready")
        self.wo_mm = sem("c_wo_mm")
        self.z_stored = sem("c_z_stored")
        self.out_step = sem("c_out_step")
        self.z_step = sem("c_z_step")
        self.weighted = sem("c_weighted")


def build(nc, io):
    ctx = ExitStack()
    with ctx:
        def sb(name, shape, dt=F32):
            return ctx.enter_context(nc.sbuf_tensor(name, shape, dt))

        def sem(name):
            return ctx.enter_context(nc.semaphore(name))

        def carve(region, sizes):
            at, parts = 0, []
            for n in sizes:
                parts.append(region[:, at:at + n])
                at += n
            return parts

        x2 = sb("x2", [P, TT, DIM])
        acc = sb("acc", [P, TT, DIM])
        region_ac = sb("region_ac", [P, 10784])
        region_bd = sb("region_bd", [P, 22534])
        work = sb("work", [P, 8752])

        a_gu, a_down, a_sgu, a_sdown = carve(region_ac, [4096, 2048, 1024, 512])
        a_gu = a_gu.rearrange("p (e k n) -> p e k n", e=8, k=KD)
        a_down = a_down.rearrange("p (e n) -> p e n", e=8)
        a_sgu = a_sgu.rearrange("p (k n) -> p k n", k=KD)
        a_sdown = a_sdown.rearrange("p (k n) -> p k n", k=2)
        a_xT = x2[:, :, :].rearrange("p t n -> p (t n)")
        a_hT = region_bd[:, 20480:20480 + 2 * CHUNKS * QUAD * P]
        a_parts = region_ac[:, 7680:7680 + 2 * 3 * QUAD * P]
        c_wq, c_wkk, c_wvv, c_wo, c_bias = carve(region_ac, [2048, 256, 256, 2048, HEADS * KEYS])
        c_wq = c_wq.rearrange("p (k n) -> p k n", k=KD)
        c_wkk = c_wkk.rearrange("p (k n) -> p k n", k=KD)
        c_wvv = c_wvv.rearrange("p (k n) -> p k n", k=KD)
        c_wo = c_wo.rearrange("p (j n) -> p j n", j=NPAIR)
        c_bias = c_bias.rearrange("p (h n) -> p h n", h=HEADS)
        b_w1, b_w2, b_b1, b_b2 = carve(region_bd, [8192, 8192, 4096, 2048])
        b_w1 = b_w1.rearrange("p (e k n) -> p e k n", e=8, k=KD)
        b_w2 = b_w2.rearrange("p (e k n) -> p e k n", e=8, k=4)
        b_b1 = b_b1.rearrange("p (e n) -> p e n", e=8)
        b_b2 = b_b2.rearrange("p (e n) -> p e n", e=8)
        d_w13, d_w2, d_s13, d_s2, d_b13, d_b2, d_sb13, c_kT_odd = carve(
            region_bd, [8192, 4096, 1024, 512, 4096, 4096, 4, 2 * KEYS1])
        d_w13 = d_w13.rearrange("p (e k n) -> p e k n", e=16, k=KD)
        d_w2 = d_w2.rearrange("p (e n) -> p e n", e=16)
        d_s13 = d_s13.rearrange("p (k n) -> p k n", k=KD)
        d_s2 = d_s2.rearrange("p (k n) -> p k n", k=2)
        d_b13 = d_b13.rearrange("p (e n) -> p e n", e=16)
        d_b2 = d_b2.rearrange("p (e n) -> p e n", e=16)

        d_xT, d_hT, d_parts = carve(region_ac, [KD * TOKENS, 2 * CHUNKS * QUAD * P, 2 * 2 * QUAD * P])

        rings = [1024, 512, 1024, 1024, 1024, 1024, 512, 2048]
        xs, xT, hbuf, hT, ys, xr, xrT, gat = carve(work, rings)
        ahead_at = sum(rings[:6])
        xs = xs.rearrange("p (r n) -> p r n", r=RING)
        xT = xT.rearrange("p (r k n) -> p r k n", r=2, k=KD)
        hbuf = hbuf.rearrange("p (r n) -> p r n", r=2)
        logitsT = hbuf
        hT = hT.rearrange("p (r n) -> p r n", r=2)
        xr = xr.rearrange("p (r n) -> p r n", r=RING)
        xrT = xrT.rearrange("p (r k n) -> p r k n", r=2, k=KD)
        rt_lg, rt_key, rt_tmp, rt_oh1, rt_oh2, rt_sc, rt_pos, rt_small = carve(gat, [256] * 8)
        xs_ahead = work[:, ahead_at:ahead_at + AHEAD * DIM].rearrange("p (r n) -> p r n", r=AHEAD)
        eq_tile = ys[:, 0:768].bitcast(F16)
        eq_row = work[:, 0:TT * P].bitcast(F16).rearrange("p (k n) -> p k n", k=2 * TT)
        ys = ys.rearrange("p (r n) -> p r n", r=RING)
        gat = gat.rearrange("p (r c n) -> p r c n", r=RING, c=2)
        (c_xn, c_xnT, c_qT, c_kT, c_v, c_bm, c_sc, c_p, c_pT, c_oT, c_mp, c_small, c_gat) = carve(
            work, [512, 512, 512, 2 * KEYS1, 128, 2 * KEYS, 2 * KEYS, 2 * KEYS, 768, 2048, KEYS, 32, 1024])
        c_gat = c_gat.rearrange("p (r c n) -> p r c n", r=QT, c=2)
        c_xn = c_xn.rearrange("p (i n) -> p i n", i=QT)
        c_xnT = c_xnT.rearrange("p (k n) -> p k n", k=KD)
        c_qT = c_qT.rearrange("p (r n) -> p r n", r=2)
        c_kT = [a.rearrange("p (o n) -> p o n", o=2) for a in (c_kT, c_kT_odd)]
        c_v = c_v.rearrange("p (j n) -> p j n", j=QT)
        c_bm = c_bm.rearrange("p (r n) -> p r n", r=2)
        c_sc = c_sc.rearrange("p (r n) -> p r n", r=2)
        c_p = c_p.rearrange("p (r n) -> p r n", r=2)
        c_pT = c_pT.rearrange("p (r n) -> p r n", r=2)
        c_oT = c_oT.rearrange("p (j n) -> p j n", j=NPAIR)
        c_min = c_small[:, 0:6].rearrange("p (r i) -> p r i", r=3)
        c_sum = c_small[:, 6:12].rearrange("p (r i) -> p r i", r=3)
        c_rec = c_small[:, 12:18].rearrange("p (r i) -> p r i", r=3)

        oh16 = sb("oh16", [P, 256], F16)
        inv = sb("inv", [P, 48], U32)
        home = sb("home", [P, 48], U32)
        inv_c = sb("inv_c", [P, 2, 48])
        slot_u = sb("slot_u", [P, 2 * TT], U32)
        home_f = sb("home_f", [P, 48])
        gates = sb("gates", [P, 2, TT])
        len_te = slot_tiles(16) + 1
        tile_expert = sb("tile_expert", [1, len_te], I32)

        ident = sb("ident", [P, P])
        before16 = sb("before16", [P, P], F16)
        ones16 = sb("ones16", [P, P], F16)
        iota_p16 = sb("iota_p16", [P, P], F16)
        iota_t = sb("iota_t", [P, 48])
        iota_128 = sb("iota_128", [P, TT])
        token_id1 = sb("token_id1", [P, 2, TT])
        past_row = sb("past_row", [P, 48])
        rank8 = sb("rank8", [P, 16])
        not_first = sb("not_first", [P, 16, TT])
        ones_f = sb("ones_f", [P, P])
        a_wt = sb("a_wt", [P, KD, 8])
        b_wg = sb("b_wg", [P, KD, 8])
        b_bg = sb("b_bg", [P, 8])
        d_gw = sb("d_gw", [P, KD, 16])
        d_eb = sb("d_eb", [P, 16])
        condT = sb("condT", [64, BATCH])
        a_wgT = sb("a_wgT", [64, 8])
        cg = sb("cg", [64, BATCH, 8])
        lg_g = sb("lg_g", [P, BATCH, 8])
        g_in = sb("g_in", [P, KD])
        d_sb2 = sb("d_sb2", [P, DIM])
        g_out = sb("g_out", [P, DIM])
        nvb = sb("nvb", [P, DH])
        nv2 = sb("nv2", [P, 1])
        nk2 = sb("nk2", [P, 1])
        nullb = sb("nullb", [P, HEADS])
        mask8 = sb("mask8", [P, BATCH, SEQ], U8)
        in_stats = sb("in_stats", [P, QT, 6])
        in_mv = sb("in_mv", [P, QT, 2])
        in_rstd = sb("in_rstd", [P, QT])
        out_stats = sb("out_stats", [P, QT, 6])
        out_mv = sb("out_mv", [P, QT, 2])
        out_rstd = sb("out_rstd", [P, QT])
        minus_half = sb("minus_half", [P, QT])

        psX = ctx.enter_context(nc.psum_tensor("psX", [P, 512], F32))
        psH = ctx.enter_context(nc.psum_tensor("psH", [P, 2, 512], F32))
        psHT = ctx.enter_context(nc.psum_tensor("psHT", [P, 2, 512], F32))
        psY = ctx.enter_context(nc.psum_tensor("psY", [P, 512], F32))
        psL = ctx.enter_context(nc.psum_tensor("psL", [P, 512], F32))
        psM = ctx.enter_context(nc.psum_tensor("psM", [P, 512], F32))
        router_x = [b[:, 0:DIM].rearrange("p (k n) -> p k n", k=KD) for b in (psX, psY)]
        ffn_x = [b[:, 0:DIM].rearrange("p (k n) -> p k n", k=KD) for b in (psX, psL)]
        quad_x = [b[:, 0:DIM].rearrange("p (k n) -> p k n", k=KD) for b in (psX, psY, psHT[:, 0, :], psHT[:, 1, :])]
        shared_y = [b[:, 0:DIM] for b in (psX, psY)]
        ffn_y = [b[:, 0:DIM] for b in (psY, psM)]
        rows_x = psX[:, :].rearrange("p (k i n) -> p k i n", k=KD, i=QT)
        keys_x = psX[:, 0:SEQ]
        values_x = psX[:, SEQ:512].rearrange("p (i n) -> p i n", i=QT)

        y0_dram = nc.dram_tensor("y0_scratch", [TOKENS, DIM], F32, kind="Internal").ap()
        z_dram = nc.dram_tensor("z_scratch", [TOKENS, DIM], F32, kind="Internal").ap()

        def by_tile(dram):
            return dram.rearrange("(t p) d -> t p d", p=P)

        def dram_tile(dram, t):
            return by_tile(dram)[bass.ds(t, 1), :, :].rearrange("o p d -> (o p) d")

        consts_made = sem("consts_made")
        first_loaded = sem("first_loaded")
        consts_loaded = sem("consts_loaded")
        x_loaded = sem("x_loaded")
        logitsT_done, logitsT_ready = sem("logitsT_done"), sem("logitsT_ready")

        def done_dmas(use, s0, off):
            each, depth = 16 * use.dmas, len(use.sems)
            return (each // depth) * s0 + each * (off // depth + 1) + use.before[off % depth]

        def wait_dma(eng, use, s0, off):
            eng.wait_ge(use.sems[off % RING], done_dmas(use, s0, off))

        def wait_slot_free(eng, use, s0, off):
            wait(eng, use.sems[off % RING], done_dmas(use, s0, off) - 16 * use.dmas)

        def wait_dmas(eng, use):
            for r in range(RING):
                eng.wait_ge(use.sems[r], use.after[r])

        slots_stored, gathered, tokens_stored = (Ring(sem, n) for n in ("slots_stored", "gathered", "tokens_stored"))
        rows_gathered = Ring(sem, "rows_gathered", ROWS)
        x_chunk = Use(gathered, RING)

        rows_ahead = Ring(sem, "rows_ahead", AHEAD // 2)

        def is_ahead(s0, off):
            return isinstance(s0, int) and ROWS <= s0 + off < ROWS + AHEAD

        def slot_rows(s0, off):
            if is_ahead(s0, off):
                return xs_ahead[:, s0 + off - ROWS, :]
            r = off % ROWS
            return xs[:, r, :] if r < RING else xr[:, r - RING, :]

        def rows_landed(f, s0, off):
            if is_ahead(s0, off):
                pair = (s0 + off - ROWS) // 2
                return f.ahead.sems[pair], f.ahead.after[pair]
            skipped = 0 if isinstance(s0, int) and s0 + off < ROWS else AHEAD // ROWS
            return f.loaded.sems[off % ROWS], done_dmas(f.loaded, s0, off) - 16 * skipped

        def stage(name, experts, src, loads, eps):
            s = Stage(sem, name, experts, src, 16 * loads, eps)
            s.pair_dram = nc.dram_tensor(f"{name}_pairs", [PAIRS + s.NT * P, DIM], F32, kind="Internal").ap()
            s.slots_stored = Use(slots_stored, s.NT)
            s.gathered = Use(gathered, TT) if name != "b" else None
            s.token_stored = Use(tokens_stored, TT) if name == "b" else None
            return s

        def ffn(name, n, hw, hk, kind, st, w_in, w_out, b_in, b_out):
            f = Ffn(sem, name, n, hw, hk, kind, st, w_in, w_out, b_in, b_out)
            f.loaded = Use(rows_gathered, n - AHEAD)
            f.ahead = Use(rows_ahead, AHEAD // 2, dmas=2)
            f.h_read = f.h_ready if kind == "leaky" else f.h_pre
            return f

        A = stage("a", 8, io["x"], 4, 1e-20)
        B = stage("b", 8, y0_dram, 4, 1e-9)
        D = stage("d", 16, z_dram, 7, 1e-10)
        fA = ffn("af", A.NT, 256, 1, "leaky", st=A,
                 w_in=lambda k, e: a_gu[:, bass.ds(e, 1), k, :].rearrange("p o n -> p (o n)"),
                 w_out=lambda j, e: one(a_down, e), b_in=None, b_out=None)
        fB = ffn("bf", B.NT, 512, 4, "gelu", st=B,
                 w_in=lambda k, e: b_w1[:, bass.ds(e, 1), k, :].rearrange("p o n -> p (o n)"),
                 w_out=lambda j, e: b_w2[:, bass.ds(e, 1), j, :].rearrange("p o n -> p (o n)"),
                 b_in=lambda e: one(b_b1, e), b_out=lambda e: one(b_b2, e))
        fD = ffn("df", D.NT, 256, 1, "silu", st=D,
                 w_in=lambda k, e: d_w13[:, bass.ds(e, 1), k, :].rearrange("p o n -> p (o n)"),
                 w_out=lambda j, e: one(d_w2, e), b_in=lambda e: one(d_b13, e), b_out=lambda e: one(d_b2, e))

        def shared(name, kept, xT, hT, parts, n, w_in, w_out, b_in, by_vector):
            return Shared(sem, name, kept, xT.rearrange("p (k t) -> p k t", k=KD),
                          hT.rearrange("p (r c t) -> p r c t", r=2, c=CHUNKS), parts.rearrange("p (r n t) -> p r n t", r=2, n=n),
                          w_in, w_out, b_in, by_vector)

        A.shared = shared("as", A.tokT_ready, a_xT, a_hT, a_parts, 3, a_sgu, a_sdown, None, (5, 6, 7))
        B.shared = None
        D.shared = shared("ds", D.tokT_ready, d_xT, d_hT, d_parts, 2, d_s13, d_s2, d_sb13, (4, 5))
        B.token_ready, D.token_ready = A.combined, sem("d_token_ready")
        A.ffn, B.ffn, D.ffn = fA, fB, fD

        class Experts:
            def __init__(self, eng, f):
                self.eng, self.f = eng, f
                self.registers = [eng.alloc_register(f"{f.name}_expert{r}") for r in range(RING)]

            def fetch(self, s0, o):
                if live(s0, o, self.f.n):
                    self.eng.reg_load(self.registers[o % RING], tile_expert[0:1, bass.ds(s0 + o, 1)])

            def of(self, o):
                return self.eng.snap(self.registers[o % RING], min_val=0, max_val=self.f.st.E - 1)

        def pe_turn_tokens(pe, st, rows, t, banks, u):
            wait(pe, st.tokT_ready, t - len(banks) + 1)
            for k in range(KD):
                last = pe.transpose(banks[u % len(banks)][:, k, :], rows[:, k * P:(k + 1) * P], ident[:, :])
            last.then_inc(st.tok_turned, 1)

        def pe_router_quads(pe, st, w, before):
            def turn_back(q):
                pe.wait_ge(logitsT_ready, before + q + 1)
                for t in range(QUAD * q, QUAD * q + QUAD):
                    at = (t % QUAD) * P
                    pe.transpose(psL[:, t * st.E:(t + 1) * st.E], logitsT[0:st.E, q % 2, at:at + P], ident[0:st.E, 0:st.E]
                                 ).then_inc(st.logits_done, 1)

            quads = TT // QUAD
            for q in range(quads + 2):
                if q < quads and st is A:
                    pe.wait_ge(x_chunk.sems[q], 16)
                for t in range(QUAD * q, min(QUAD * q + QUAD, TT)):
                    if st is not A:
                        pe.wait_ge(st.token_ready, t + 1)
                    pe_turn_tokens(pe, st, acc[:, t, :], t, quad_x, t)
                if 1 <= q <= quads:
                    pe.wait_ge(st.tokT_ready, QUAD * q)
                    for k in range(KD):
                        last = pe.matmul(psH[0:st.E, (q - 1) % 2, :], w[:, k, :],
                                         st.shared.xT[:, k, (q - 1) * QUAD * P:q * QUAD * P], start=(k == 0), stop=(k == KD - 1))
                    last.then_inc(logitsT_done, 1)
                if q >= 2:
                    turn_back(q - 2)

        def pe_router(pe, st, w):
            def body(s0, u):
                if live(s0, u, TT):
                    t = s0 + u
                    pe.wait_ge(st.token_ready, t + 1)
                    pe_turn_tokens(pe, st, xr[:, u, :], t, router_x, u)
                if live(s0, u - 1, TT):
                    t = s0 + (u - 1)
                    pe.wait_ge(st.tokT_ready, t + 1)
                    for k in range(KD):
                        last = pe.matmul(psL[:, bass.ds(t * st.E, st.E)], xrT[:, (u - 1) % 2, k, :], w[:, k, :],
                                         start=(k == 0), stop=(k == KD - 1))
                    last.then_inc(st.logits_done, 1)
            steps(pe, TT, body, 0, 1)

        def pe_counts(pe, st):
            n = TT * st.E
            pe.wait_ge(st.onehot_ready, 1)
            oh_et = oh16[:, 0:n].rearrange("p (t e) -> p e t", e=st.E)
            pe.matmul(psM[:, 0:n], before16[:, :], oh_et, start=True, stop=True)
            pe.matmul(psM[:, n:2 * n], ones16[:, :], oh_et, start=True, stop=True).then_inc(st.prefix_done, 1)

        def pe_invert(pe, st):
            eq = eq_tile[:, 0:2 * TT * st.NT].rearrange("p (k a) -> p k a", a=st.NT)
            for k in range(2 * TT):
                if k % QUAD == 0:
                    pe.wait_ge(st.eqrow_ready, k // QUAD + 1)
                c = k // TT
                last = pe.matmul(psL[:, 64 * c:64 * c + st.NT], eq_row[:, k, :], eq[:, k, :], start=(k % TT == 0), stop=(k % TT == TT - 1))
            last.then_inc(st.inv_done, 1)

        def pe_shared_in(pe, sh, i):
            q, c = i // CHUNKS, i % CHUNKS
            pe.wait_ge(sh.kept, QUAD * q + QUAD)
            if i >= 2 and i - 2 in sh.by_vector:
                pe.wait_ge(sh.h_ready, i - 1)
            elif i >= 2:
                pe.wait_ge(sh.part_ready, sh.parts_after[i - 2])
            for n, bank in enumerate((psH, psHT)):
                at = (n * CHUNKS + c) * P
                for k in range(KD):
                    last = pe.matmul(bank[:, c, :], sh.w_in[:, k, at:at + P], sh.xT[:, k, q * QUAD * P:(q + 1) * QUAD * P],
                                     start=(k == 0), stop=(k == KD - 1))
            last.then_inc(sh.h_mm, 1)

        def pe_shared_out(pe, sh, q):
            pe.wait_ge(sh.h_ready, CHUNKS * (q + 1))
            for i in range(QUAD):
                t = QUAD * q + i
                wait(pe, sh.y_out, t - 1)
                for c in range(CHUNKS):
                    last = pe.matmul(shared_y[t % 2], sh.hT[:, q % 2, c, i * P:(i + 1) * P], sh.w_out[:, c, :],
                                     start=(c == 0), stop=(c == CHUNKS - 1))
                last.then_inc(sh.y_mm, 1)

        def pe_route_and_shared(pe, st):
            sh = st.shared
            pe_shared_in(pe, sh, 0)
            pe_shared_in(pe, sh, 1)
            pe_counts(pe, st)
            pe_shared_in(pe, sh, 2)
            pe_shared_out(pe, sh, 0)
            pe_shared_in(pe, sh, 3)
            pe_shared_in(pe, sh, 4)
            pe_invert(pe, st)
            pe_shared_out(pe, sh, 1)
            pe_shared_in(pe, sh, 5)

        def pe_shared_rest(pe, sh):
            pe_shared_in(pe, sh, 6)
            pe_shared_in(pe, sh, 7)
            pe_shared_out(pe, sh, 2)
            pe_shared_out(pe, sh, 3)

        shared_first = ((0, None), (1, None), (2, 0), (3, None), (4, 1), (5, None))
        shared_rest = ((6, None), (7, 2), (None, 3))
        tiles_first = 2 * QUAD

        def act_shared(act, sh, kind, order):
            for i, q in order:
                if i is not None and not (kind == "leaky" and i in sh.by_vector):
                    act_shared_in(act, sh, i, kind)
                if q is not None:
                    for t in range(QUAD * q, QUAD * q + QUAD):
                        act.wait_ge(sh.y_mm, t + 1)
                        nc.scalar.copy(acc[:, t, :], shared_y[t % 2]).then_inc(sh.y_out, 1)

        def act_shared_in(act, sh, i, kind):
            c = i % CHUNKS
            act.wait_ge(sh.h_mm, i + 1)
            wait(act, sh.h_ready, i - 1)
            gate, up, parts = psH[:, c, :], psHT[:, c, :], sh.parts[:, c, :, :]
            if i in sh.by_vector:
                nc.scalar.activation(parts[:, 0, :], gate, ACT.Silu, bias=sh.b_in[:, c:c + 1]).then_inc(sh.part_ready, 1)
            elif kind == "leaky":
                nc.scalar.activation(parts[:, 0, :], gate, ACT.Relu).then_inc(sh.part_ready, 1)
                nc.scalar.activation(parts[:, 2, :], gate, ACT.Relu, scale=-0.01).then_inc(sh.part_ready, 1)
                nc.scalar.copy(parts[:, 1, :], up).then_inc(sh.part_ready, 1)
            else:
                nc.scalar.activation(parts[:, 0, :], gate, ACT.Silu, bias=sh.b_in[:, c:c + 1]).then_inc(sh.part_ready, 1)
                nc.scalar.activation(parts[:, 1, :], up, ACT.Identity, bias=sh.b_in[:, CHUNKS + c:CHUNKS + c + 1]
                                     ).then_inc(sh.part_ready, 1)

        def pool_shared_in(pool, sh, i, kind):
            q, c = i // CHUNKS, i % CHUNKS
            parts = sh.parts[:, c, :, :]
            pool.wait_ge(sh.part_ready, sh.parts_after[i])
            wait(pool, sh.h_ready, i)
            if kind == "leaky":
                pool.tensor_tensor(parts[:, 0, :], parts[:, 0, :], parts[:, 2, :], ALU.subtract).then_inc(sh.h_leaky, 1)
                pool.wait_ge(sh.h_leaky, sh.leaky_after[i])
            wait(pool, sh.y_mm, QUAD * (q - 1))
            pool.tensor_tensor(sh.hT[:, q % 2, c, :], parts[:, 0, :], parts[:, 1, :], ALU.mult).then_inc(sh.h_ready, 1)

        def pool_shared(pool, sh, kind, order):
            for i, _ in order:
                if i is not None and i not in sh.by_vector:
                    pool_shared_in(pool, sh, i, kind)

        def dve_shared(dve, sh, kind, order):
            for i in [i for i, _ in order if i in sh.by_vector]:
                q, c = i // CHUNKS, i % CHUNKS
                gate, up, hidden, act_gate = psH[:, c, :], psHT[:, c, :], sh.hT[:, q % 2, c, :], sh.parts[:, c, 0, :]
                dve.wait_ge(sh.h_ready, i)
                dve.wait_ge(sh.y_mm, QUAD * (q - 1))
                if kind == "leaky":
                    dve.wait_ge(sh.h_mm, i + 1)
                    nc.vector.tensor_scalar(act_gate, gate, 0.01, None, ALU.mult).then_inc(sh.h_leaky, 1)
                    dve.wait_ge(sh.h_leaky, sh.leaky_after[i] - 1)
                    nc.vector.tensor_tensor(act_gate, act_gate, gate, ALU.max).then_inc(sh.h_leaky, 1)
                    dve.wait_ge(sh.h_leaky, sh.leaky_after[i])
                    nc.vector.tensor_tensor(hidden, act_gate, up, ALU.mult).then_inc(sh.h_ready, 1)
                else:
                    dve.wait_ge(sh.part_ready, sh.parts_after[i])
                    nc.vector.scalar_tensor_tensor(out=hidden, in0=up, scalar=sh.b_in[:, CHUNKS + c:CHUNKS + c + 1], in1=act_gate,
                                                   op0=ALU.add, op1=ALU.mult).then_inc(sh.h_ready, 1)

        def pe_ffn(pe, f):
            experts = Experts(pe, f)

            def body(s0, u):
                if live(s0, u + 1, f.n):
                    r, t = (u + 1) % RING, s0 + (u + 1)
                    pe.wait_ge(*rows_landed(f, s0, u + 1))
                    wait(pe, f.xT_ready, t - 1)
                    for k in range(KD):
                        last = pe.transpose(ffn_x[r % 2][:, k, :], slot_rows(s0, u + 1)[:, k * P:(k + 1) * P], ident[:, :])
                    last.then_inc(f.turned, 1)
                if live(s0, u, f.n):
                    t, h = s0 + u, u % 2
                    e = experts.of(u)
                    pe.wait_ge(f.xT_ready, t + 1)
                    wait(pe, f.h_read, t - 1)
                    for k in range(KD):
                        last = pe.matmul(psH[:, h, 0:f.hw], xT[:, h, k, :], f.w_in(k, e),
                                         start=(k == 0), stop=(k == KD - 1))
                    last.then_inc(f.h_mm, 1)
                experts.fetch(s0, u + 1)
                if live(s0, u - 1, f.n):
                    t, h = s0 + (u - 1), (u - 1) % 2
                    pe.wait_ge(f.h_ready, t + 1)
                    wait(pe, f.hT_ready, t - 1)
                    for j in range(f.hk):
                        last = pe.transpose(psHT[:, h, j * P:(j + 1) * P], hbuf[:, h, j * P:(j + 1) * P], ident[:, :])
                    last.then_inc(f.h_turned, 1)
                if live(s0, u - 2, f.n):
                    t, h = s0 + (u - 2), u % 2
                    e = experts.of(u - 2)
                    pe.wait_ge(f.hT_ready, t + 1)
                    wait(pe, f.y_out, t - 1)
                    for j in range(f.hk):
                        last = pe.matmul(ffn_y[h], hT[:, h, j * P:(j + 1) * P], f.w_out(j, e),
                                         start=(j == 0), stop=(j == f.hk - 1))
                    last.then_inc(f.y_mm, 1)
            experts.fetch(0, 0)
            pe.wait_ge(*rows_landed(f, 0, 0))
            for k in range(KD):
                last = pe.transpose(ffn_x[0][:, k, :], slot_rows(0, 0)[:, k * P:(k + 1) * P], ident[:, :])
            last.then_inc(f.turned, 1)
            steps(pe, f.n, body, 1, 2, ROWS + AHEAD, ROWS)

        def load_broadcast(eng, dst, name, s):
            ap = dst.rearrange("p a n -> p (a n)") if dst.ndim == 3 else dst
            eng.dma_start(ap, io[name].to_broadcast([P, io[name].shape[1]])).then_inc(s, 16)

        def act_router_quads(act, st, before):
            def logits(q):
                act.wait_ge(logitsT_done, before + q + 1)
                if q >= 2:
                    act.wait_ge(st.logits_done, QUAD * (q - 1))
                nc.scalar.copy(logitsT[0:st.E, q % 2, :], psH[0:st.E, q % 2, :]).then_inc(logitsT_ready, 1)

            for t in range(TT):
                act.wait_ge(st.tok_turned, t + 1)
                nc.scalar.copy(st.shared.xT[:, :, t * P:(t + 1) * P], quad_x[t % QUAD]).then_inc(st.tokT_ready, 1)
                if t >= QUAD and t % QUAD == QUAD - 1:
                    logits(t // QUAD - 1)
            logits(TT // QUAD - 1)

        def act_router(act, st):
            def body(s0, u):
                t = s0 + u
                act.wait_ge(st.tok_turned, t + 1)
                wait(act, st.logits_done, t - 1)
                nc.scalar.copy(xrT[:, u % 2, :, :], router_x[u % 2]).then_inc(st.tokT_ready, 1)
            steps(act, TT, body, 0, 0)

        def act_ffn(act, f):
            def copy_x(s0, o):
                t, h = s0 + o, o % 2
                act.wait_ge(f.turned, t + 1)
                wait(act, f.h_mm, t - 1)
                nc.scalar.copy(xT[:, h, :, :], ffn_x[h]).then_inc(f.xT_ready, 1)

            def body(s0, u):
                if live(s0, u + 1, f.n):
                    copy_x(s0, u + 1)
                if live(s0, u, f.n) and f.kind == "leaky":
                    t, h = s0 + u, u % 2
                    act.wait_ge(f.h_mm, t + 1)
                    wait(act, f.h_turned, t - 1)
                    nc.scalar.mul(hbuf[:, h, 0:f.hw // 2], psH[:, h, 0:f.hw // 2], 0.01).then_inc(f.h_pre, 1)
                elif live(s0, u, f.n):
                    t, h = s0 + u, u % 2
                    act.wait_ge(f.h_pre, t + 1)
                    if f.kind == "gelu":
                        nc.scalar.activation(hbuf[:, h, :], hbuf[:, h, :], ACT.Gelu).then_inc(f.h_ready, 1)
                    else:
                        m = f.hw // 2
                        nc.scalar.activation(hbuf[:, h, 0:m], hbuf[:, h, 0:m], ACT.Silu).then_inc(f.h_gate, 1)
                if live(s0, u - 1, f.n):
                    t, h = s0 + (u - 1), (u - 1) % 2
                    act.wait_ge(f.h_turned, t + 1)
                    wait(act, f.y_mm, t - 1)
                    nc.scalar.copy(hT[:, h, 0:f.hk * P], psHT[:, h, 0:f.hk * P]).then_inc(f.hT_ready, 1)
            copy_x(0, 0)
            steps(act, f.n, body, 1, 2)

        def dve_ffn(dve, f):
            m = f.hw // 2
            experts = Experts(dve, f)

            def body(s0, u):
                if live(s0, u, f.n):
                    t, h = s0 + u, u % 2
                    if f.b_in is not None:
                        e = experts.of(u)
                    dve.wait_ge(f.h_mm, t + 1)
                    wait(dve, f.h_turned, t - 1)
                    if f.kind == "leaky":
                        dve.wait_ge(f.h_pre, t + 1)
                        nc.vector.tensor_tensor(hbuf[:, h, 0:m], hbuf[:, h, 0:m], psH[:, h, 0:m], ALU.max
                                                ).then_inc(f.h_gate, 1)
                        dve.wait_ge(f.h_gate, t + 1)
                        nc.vector.tensor_tensor(hbuf[:, h, 0:m], hbuf[:, h, 0:m], psH[:, h, m:2 * m], ALU.mult
                                                ).then_inc(f.h_ready, 1)
                    else:
                        nc.vector.tensor_tensor(hbuf[:, h, 0:f.hw], psH[:, h, 0:f.hw], f.b_in(e), ALU.add
                                                ).then_inc(f.h_pre, 1)
                if f.b_in is not None:
                    experts.fetch(s0, u + 1)
                if live(s0, u, f.n) and f.kind == "silu":
                    t, h = s0 + u, u % 2
                    dve.wait_ge(f.h_gate, t + 1)
                    nc.vector.tensor_tensor(hbuf[:, h, 0:m], hbuf[:, h, 0:m], hbuf[:, h, m:2 * m], ALU.mult
                                            ).then_inc(f.h_ready, 1)
                if live(s0, u - 2, f.n):
                    t, r = s0 + (u - 2), (u - 2) % RING
                    if f.b_out is not None:
                        e = experts.of(u - 2)
                    dve.wait_ge(f.y_mm, t + 1)
                    wait_slot_free(dve, f.st.slots_stored, s0, u - 2)
                    dst = ys[:, r, :]
                    if f.b_out is None:
                        nc.vector.tensor_copy(dst, ffn_y[u % 2]).then_inc(f.y_out, 1)
                    else:
                        nc.vector.tensor_tensor(dst, ffn_y[u % 2], f.b_out(e), ALU.add).then_inc(f.y_out, 1)
            if f.b_in is not None:
                experts.fetch(0, 0)
            steps(dve, f.n, body, 1, 2)

        def dve_route(dve, st):
            E, NT, n = st.E, st.NT, TT * st.E
            count = [0]

            def done(ins):
                count[0] += 1
                ins.then_inc(st.route_step, 1)
                dve.wait_ge(st.route_step, count[0])

            def te(ap):
                return ap[:, 0:n].rearrange("p (t e) -> p t e", e=E)

            def et(ap):
                return ap[:, 0:n].rearrange("p (e t) -> p e t", e=E)

            def as_te(ap):
                return ap[:, 0:n].rearrange("p (e t) -> p t e", e=E)

            def per_token(ap):
                return ap.unsqueeze(2).to_broadcast([P, TT, E])

            v = nc.vector
            lg, key, tmp, oh1, oh2, sc = (te(a) for a in (rt_lg, rt_key, rt_tmp, rt_oh1, rt_oh2, rt_sc))
            best, w1, w2, den = (rt_small[:, i * TT:(i + 1) * TT] for i in range(4))
            c_e, nt_e, end_e, base_e = (rt_small[:, 64 + i * 16:64 + i * 16 + E] for i in range(4))
            half = rt_small[:, 128:160]
            row_f = rt_small[:, 160:192]
            slot_f = rt_small[:, 192:224]
            dve.wait_ge(st.logits_done, TT)
            lps = psL[:, 0:n].rearrange("p (t e) -> p t e", e=E)
            if st is A:
                lb = lg.rearrange("p (b i) e -> p b i e", i=QT)
                pb = psL[:, 0:n].rearrange("p (b i e) -> p b i e", i=QT, e=E)
                for i in range(QT):
                    done(v.tensor_tensor(lb[:, :, i, :], pb[:, :, i, :], lg_g[:, :, :], ALU.add))
            elif st is B:
                done(v.tensor_tensor(lg, lps, b_bg[:, :].unsqueeze(1).to_broadcast([P, TT, E]), ALU.add))
            else:
                v.tensor_copy(lg, lps).then_inc(st.exp_wanted, 1)
                dve.wait_ge(st.exp_wanted, 1)
                done(v.tensor_tensor(key, lg, d_eb[:, :].unsqueeze(1).to_broadcast([P, TT, E]), ALU.add))
            if st is not D:
                key = lg
            rank = rank8[:, 16 - E:16].unsqueeze(1).to_broadcast([P, TT, E])
            for oh, top in ((oh1, w1), (oh2, best)):
                done(v.tensor_reduce(top, key, AX_X, ALU.max))
                done(v.tensor_tensor(tmp, key, per_token(top), ALU.is_equal))
                done(v.tensor_tensor(tmp, tmp, rank, ALU.mult))
                done(v.tensor_reduce(den, tmp, AX_X, ALU.max))
                done(v.tensor_tensor(oh, tmp, per_token(den), ALU.is_equal))
                if oh is oh1:
                    done(v.scalar_tensor_tensor(out=te(rt_key), in0=oh, scalar=LOWEST, in1=key, op0=ALU.mult, op1=ALU.add))
                    key = te(rt_key)
            v.tensor_tensor(oh16[:, 0:n].rearrange("p (t e) -> p t e", e=E), oh1, oh2, ALU.add).then_inc(st.onehot_ready, 1)
            if st is not D:
                v.tensor_tensor(sc, lg, per_token(w1), ALU.subtract).then_inc(st.exp_wanted, 1)
            dve.wait_ge(st.prefix_done, 1)
            dve.wait_ge(st.exp_done if st is D else st.exp_wanted, 1)
            within, total, earlier = et(psM[:, 0:n]), et(psM[:, n:2 * n]), et(rt_lg)
            done(v.tensor_tensor_scan(rt_lg[:, 0:n], psM[:, n - 1:2 * n - 1], not_first[:, 0:E, :].rearrange("p e t -> p (e t)"),
                                      0.0, ALU.add, ALU.mult))
            last = slice(TT - 1, TT)
            done(v.tensor_tensor(c_e, earlier[:, :, last].rearrange("p e o -> p (e o)"),
                                 total[:, :, last].rearrange("p e o -> p (e o)"), ALU.add))
            done(v.tensor_tensor(et(rt_tmp), c_e.unsqueeze(2).to_broadcast([P, E, TT]),
                                 iota_128[:, :].unsqueeze(1).to_broadcast([P, E, TT]), ALU.is_gt))
            done(v.tensor_reduce(nt_e, et(rt_tmp), AX_X, ALU.add))
            done(v.tensor_tensor_scan(end_e, ones_f[:, 0:E], nt_e, 0.0, ALU.mult, ALU.add))
            done(v.tensor_tensor(base_e, end_e, nt_e, ALU.subtract))
            done(v.tensor_scalar(base_e, base_e, float(P), None, ALU.mult))
            done(v.tensor_tensor(et(rt_pos), earlier, within, ALU.add))
            done(v.tensor_tensor(et(rt_pos), et(rt_pos), base_e.unsqueeze(2).to_broadcast([P, E, TT]), ALU.add))
            for c, oh in enumerate((oh1, oh2)):
                done(v.tensor_tensor(tmp, oh, as_te(rt_pos), ALU.mult))
                done(v.tensor_reduce(slot_f[:, c * TT:(c + 1) * TT], tmp, AX_X, ALU.add))
            slot_i = slot_u[:, :]
            done(v.tensor_copy(slot_i, slot_f))
            hi = half.bitcast(I32)
            done(v.tensor_scalar(hi, slot_i.bitcast(I32), P - 1, None, ALU.bitwise_and))
            done(v.tensor_copy(row_f, hi))
            done(v.tensor_scalar(hi, slot_i.bitcast(I32), 7, None, ALU.logical_shift_right))
            done(v.tensor_copy(slot_f, hi))
            eq = eq_tile[:, 0:2 * TT * NT].rearrange("p (k a) -> p k a", a=NT)
            done(v.tensor_tensor(eq, slot_f.unsqueeze(2).to_broadcast([P, 2 * TT, NT]),
                                 iota_t[:, 0:NT].unsqueeze(1).to_broadcast([P, 2 * TT, NT]), ALU.is_equal))
            done(v.tensor_tensor(eq, eq, token_id1[:, :, :].rearrange("p c t -> p (c t)").unsqueeze(2).to_broadcast([P, 2 * TT, NT]),
                                 ALU.mult))
            for k in range(0, 2 * TT, QUAD):
                v.tensor_tensor(eq_row[:, k:k + QUAD, :], row_f[:, k:k + QUAD].unsqueeze(2).to_broadcast([P, QUAD, P]),
                                iota_p16[:, :].unsqueeze(1).to_broadcast([P, QUAD, P]), ALU.is_equal).then_inc(st.eqrow_ready, 1)
            dve.wait_ge(st.inv_done, 1)
            done(v.tensor_copy(inv_c[:, :, 0:NT], psL[:, 0:128].rearrange("p (c a) -> p c a", c=2)[:, :, 0:NT]))
            both = home_f[:, 0:NT]
            done(v.tensor_tensor(both, inv_c[:, 0, 0:NT], inv_c[:, 1, 0:NT], ALU.add))
            v.tensor_scalar(inv[:, 0:NT], both, -1.0, 0.0, ALU.add, ALU.max).then_inc(st.routed, 1)
            cmp = rt_tmp[0:1, :]
            spare = rt_pos[0:1, 0:len_te]
            for a in range(0, len_te, TT):
                w = TT
                c3 = cmp[:, 0:w * E].rearrange("p (t e) -> p t e", e=E)
                done(v.tensor_tensor(c3, end_e[0:1, :].unsqueeze(1).to_broadcast([1, w, E]),
                                     iota_t[0:1, a:a + w].unsqueeze(2).to_broadcast([1, w, E]), ALU.is_le))
                done(v.tensor_reduce(spare[:, a:a + w], c3, AX_X, ALU.add))
            done(v.tensor_scalar(spare, spare, float(E - 1), None, ALU.min))
            v.tensor_copy(tile_expert[0:1, :], spare).then_inc(st.routed, 1)
            dve.wait_ge(st.routed, 2)
            past = inv_c[:, 0, 0:NT]
            done(v.tensor_scalar(inv_c[:, 1, 0:NT], inv_c[:, 1, 0:NT], 0.0, float(TOKENS), ALU.is_gt, ALU.mult))
            done(v.scalar_tensor_tensor(out=past, in0=both, scalar=0.0, in1=past_row[:, 0:NT], op0=ALU.is_equal, op1=ALU.mult))
            done(v.tensor_tensor(both, both, inv_c[:, 1, 0:NT], ALU.add))
            v.scalar_tensor_tensor(out=home[:, 0:NT], in0=both, scalar=-1.0, in1=past, op0=ALU.add, op1=ALU.add
                                   ).then_inc(st.routed, 1)
            dve.wait_ge(st.exp_done, 1)
            if st is not D:
                done(v.tensor_reduce(den, sc, AX_X, ALU.add))
                done(v.reciprocal(den, den))
                done(v.tensor_tensor(sc, sc, per_token(den), ALU.mult))
            for oh, w in ((oh1, w1), (oh2, w2)):
                done(v.tensor_tensor(tmp, oh, sc, ALU.mult))
                done(v.tensor_reduce(w, tmp, AX_X, ALU.add))
            done(v.tensor_tensor(den, w1, w2, ALU.add))
            done(v.tensor_scalar(den, den, st.eps, None, ALU.add))
            done(v.reciprocal(den, den))
            done(v.tensor_tensor(gates[:, 0, :], w1, den, ALU.mult))
            v.tensor_tensor(gates[:, 1, :], w2, den, ALU.mult).then_inc(st.routed, 1)
            dve.wait_ge(st.routed, 4)

        def act_route(act, st):
            n = TT * st.E
            act.wait_ge(st.exp_wanted, 1)
            act_f, scale = {"a": (ACT.Exp, 0.5), "b": (ACT.Exp, 0.2), "d": (ACT.Sigmoid, 1.0)}[st.name]
            src = rt_lg if st is D else rt_sc
            nc.scalar.activation(rt_sc[:, 0:n], src[:, 0:n], act_f, scale=scale).then_inc(st.exp_done, 1)

        def pool_gather_rows(pool, st, first, last):
            f = st.ffn
            if first == 0:
                pool.wait_ge(st.routed, 1)
                if st is B:
                    wait_dmas(pool, st.token_stored)
                elif st is D:
                    pool.wait_ge(C.z_stored, 16 * TT)
            for t in range(first, last):
                if t == ROWS + AHEAD_EARLY:
                    pool.wait_ge(st.routed, 4)
                elif t >= ROWS + AHEAD:
                    before = t - ROWS if t >= 2 * ROWS + AHEAD else t - ROWS - AHEAD
                    pool.wait_ge(f.turned, before + 1)
                landed, _ = rows_landed(f, 0, t)
                pool.indirect_dma_start(out=slot_rows(0, t), out_offset=None, in_=st.src,
                                        in_offset=bass.IndirectOffsetOnAxis(ap=inv[:, t:t + 1], axis=0)).then_inc(landed, 16)

        def pool_scatter_rows(pool, st, t):
            if t == 0:
                pool.wait_ge(st.routed, 3)
            pool.wait_ge(st.ffn.y_out, t + 1)
            pool.indirect_dma_start(out=st.pair_dram, out_offset=bass.IndirectOffsetOnAxis(ap=home[:, t:t + 1], axis=0),
                                    in_=ys[:, t % RING, :], in_offset=None).then_inc(st.slots_stored.sems[t % RING], 16)

        def pool_slots(pool, st, between=None):
            sent, behind = 0, ROWS + 4
            for t in range(ROWS + AHEAD, st.NT + behind):
                upto = t - behind if t >= 2 * ROWS + AHEAD else t - ROWS - AHEAD - 3
                for done in range(sent, upto + 1):
                    pool_scatter_rows(pool, st, done)
                sent = max(sent, upto + 1)
                if t < st.NT:
                    pool_gather_rows(pool, st, t, t + 1)
                if between is not None:
                    between(pool, t)

        def pair_rows(st, t):
            pairs = st.pair_dram[0:PAIRS, :].rearrange("(c t p) d -> t p c d", c=2, p=P)
            return pairs[bass.ds(t, 1), :, :, :].rearrange("o p c d -> (o p) c d")

        def sp_combine(sp, st, store):
            def load(s0, u):
                sp.dma_start(gat[:, u, :, :], pair_rows(st, s0 + u)).then_inc(st.gathered.sems[u], 16)

            wait_dmas(sp, st.slots_stored)
            for u in range(RING):
                load(0, u)

            def body(s0, u):
                sp.wait_ge(st.combined, s0 + u + 1)
                store(s0, u)
                if live(s0, u + RING, TT):
                    load(s0 + RING, u)
            steps(sp, TT, body, RING, 0)

        C = Attention(sem, 16 * 6)


        def pe_q(pe, pair, j, b):
            if j == 0:
                pe.wait_ge(C.xnT_ready, 2 * b + 2)
            wait(pe, C.qT_ready, pair)
            for k in range(KD):
                last = pe.matmul(psY[:, 0:SEQ], c_wq[:, k, j * P:(j + 1) * P], c_xnT[:, k, :],
                                 start=(k == 0), stop=(k == KD - 1))
            last.then_inc(C.q_mm, 1)

        def pe_scores(pe, g, h, b, odd):
            pe.wait_ge(C.qT_ready, 8 * b + h // 2 + 1)
            if h < 2:
                pe.wait_ge(C.kT_ready, 2 * b + h + 1)
            wait(pe, C.score_ready, g - 1)
            q = c_qT[:, (h // 2) % 2, :]
            pe.matmul(psH[:, h % 2, 0:KEYS0], q[:, 0:P], c_kT[odd][:, h % 2, 0:KEYS0], start=True, stop=True)
            pe.matmul(psH[:, h % 2, KEYS0:KEYS], q[:, P:2 * P], c_kT[odd][:, h % 2, :], start=True, stop=True
                      ).then_inc(C.s_mm, 1)

        def pe_turn(pe, g, h, b):
            pe.wait_ge(C.pn_ready, g + 1)
            wait(pe, C.pT_ready[h % 2], 8 * b + h // 2)
            for n, at in enumerate((1, KEYS0 + 1, KEYS0 + 1 + P)):
                last = pe.transpose(psHT[:, h % 2, n * P:(n + 1) * P], c_p[:, h % 2, at:at + P], ident[:, :])
            last.then_inc(C.p_turned, 1)

        def pe_sum(pe, pair, j, b):
            for s in C.pT_ready:
                pe.wait_ge(s, pair + 1)
            if j == 0:
                pe.wait_ge(C.v_ready, b + 1)
            wait(pe, C.o_ready, pair)
            for n, keys, queries in ((0, 0, slice(0, SEQ)), (1, 1, slice(P, SEQ))):
                at = slice(n * SEQ, n * SEQ + queries.stop - queries.start)
                for o in range(2):
                    last = pe.matmul(psL[DH * o:DH * o + DH, queries], c_v[:, keys, :], c_pT[:, o, at],
                                     start=(n == 0), stop=(n == 1))
            last.then_inc(C.pv_mm, 1)

        def pe_out(pe, b):
            pe.wait_ge(C.o_ready, 8 * b + 8)
            wait(pe, C.z_step, 2 * b)
            for i in range(QT):
                for j in range(NPAIR):
                    last = pe.matmul(psM[:, i * DIM:(i + 1) * DIM], c_oT[:, j, i * P:(i + 1) * P], c_wo[:, j, :],
                                     start=(j == 0), stop=(j == NPAIR - 1))
            last.then_inc(C.wo_mm, 1)

        def pe_rows(pe, b):
            pe.wait_ge(C.xn_ready, 2 * b + 2)
            wait(pe, C.v_ready, b)
            for i in range(QT):
                for k in range(KD):
                    last = pe.transpose(rows_x[:, k, i, :], c_xn[:, i, k * P:(k + 1) * P], ident[:, :])
            last.then_inc(C.xn_turned, 1)

        def pe_kv(pe, b):
            pe.wait_ge(C.xnT_ready, 2 * b + 2)
            for k in range(KD):
                pe.matmul(keys_x, c_wkk[:, k, :], c_xnT[:, k, :],
                          start=(k == 0), stop=(k == KD - 1))
            for i in range(QT):
                for k in range(KD):
                    last = pe.matmul(values_x[:, i, :], c_xnT[:, k, i * P:(i + 1) * P], c_wvv[:, k, :],
                                     start=(k == 0), stop=(k == KD - 1))
            last.then_inc(C.kv_mm, 1)

        def pe_batch(pe, b, odd, first, last):
            for h in range(HEADS):
                g = 16 * b + h
                if not (last and h >= 14):
                    pe_scores(pe, g + 2, (h + 2) % HEADS, b + (h + 2) // HEADS, (odd + (h + 2) // HEADS) % 2)
                if h % 2 == 0 and not (last and h >= 12):
                    j = (h + 4) // 2
                    pe_q(pe, 8 * b + j, j % NPAIR, b + j // NPAIR)
                if h == 2 and not first:
                    pe_out(pe, b - 1)
                if h % 2 == 1 and h > 1:
                    pe_sum(pe, 8 * b + h // 2 - 1, h // 2 - 1, b)
                elif h == 1 and not first:
                    pe_sum(pe, 8 * b - 1, NPAIR - 1, b - 1)
                if h == 10 and not last:
                    pe_rows(pe, b + 1)
                if h == 12 and not last:
                    pe_kv(pe, b + 1)
                pe_turn(pe, g, h, b)

        def batches(eng, batch):
            batch(eng, 0, 0, True, False)
            with eng.Fori(0, (BATCH - 2) // 2) as i:
                for u in (1, 2):
                    batch(eng, 2 * i + u, u % 2, False, False)
            batch(eng, BATCH - 1, 1, False, True)

        def pe_attention(pe):
            pe.wait_ge(C.kT_fixed, 8)
            pe_rows(pe, 0)
            pe_kv(pe, 0)
            pe_q(pe, 0, 0, 0)
            pe_q(pe, 1, 1, 0)
            pe_scores(pe, 0, 0, 0, 0)
            pe_scores(pe, 1, 1, 0, 0)
            batches(pe, pe_batch)
            pe_sum(pe, NPAIR * BATCH - 1, NPAIR - 1, BATCH - 1)
            pe_out(pe, BATCH - 1)

        def act_rowsT(act, b):
            act.wait_ge(C.xn_turned, b + 1)
            wait(act, C.q_mm, 8 * b)
            wait(act, C.kv_mm, b)
            for k in range(KD):
                nc.scalar.activation(c_xnT[:, k, :], rows_x[:, k, :, :].rearrange("p i n -> p (i n)"), ACT.Identity,
                                     scale=g_in[:, k:k + 1]).then_inc(C.xnT_ready, 1)

        def act_mask(act, b):
            wait(act, C.bm_ready, 16 * b)
            m = mask8[:, bass.ds(b, 1), :].rearrange("p o n -> p (o n)")
            for dst, src in ((c_mp[:, 1:KEYS0], m[:, 0:P]), (c_mp[:, KEYS0 + 1:KEYS], m)):
                nc.scalar.activation(dst, src, ACT.Copy, scale=-HIDDEN_KEY, bias=HIDDEN_KEY).then_inc(C.mask_ready, 1)

        def act_q(act, pair, j):
            act.wait_ge(C.q_mm, pair + 1)
            wait(act, C.s_mm, 2 * pair - 2)
            nc.scalar.mul(c_qT[:, j % 2, :], psY[:, 0:SEQ], -(float(DH) ** -0.5)).then_inc(C.qT_ready, 1)

        def act_exp(act, g, h):
            act.wait_ge(C.score_ready, g + 1)
            wait(act, C.p_turned, g - 1)
            for i, (a, z) in enumerate(((0, KEYS0), (KEYS0, KEYS))):
                nc.scalar.activation(c_p[:, h % 2, a:z], c_sc[:, h % 2, a:z], ACT.Exp, scale=-1.0,
                                     bias=c_min[:, h % 2, i:i + 1], accum_out=c_sum[:, h % 2, i:i + 1]
                                     ).then_inc(C.p_ready, 1)

        def act_pT(act, g, h, b):
            act.wait_ge(C.p_turned, g + 1)
            wait(act, C.pv_mm, 8 * b + h // 2)
            nc.scalar.copy(c_pT[:, 0, :], psHT[:, 0, 0:3 * P]).then_inc(C.pT_ready[0], 1)

        def act_o(act, pair, j, b):
            act.wait_ge(C.pv_mm, pair + 1)
            if j == 0:
                wait(act, C.wo_mm, b)
            nc.scalar.activation(c_oT[:, j, :], psL[:, 0:SEQ], ACT.Identity, bias=nv2[:, 0:1]).then_inc(C.o_ready, 1)

        def act_batch(act, b, odd, first, last):
            for h in range(HEADS):
                g = 16 * b + h
                if h % 2 == 1:
                    act_pT(act, g - 1, h - 1, b)
                if not (last and h >= 14):
                    act_exp(act, g + 2, (h + 2) % HEADS)
                if h % 2 == 0 and not (last and h >= 12):
                    j = (h + 4) // 2
                    act_q(act, 8 * b + j, j % NPAIR)
                if h == 10 and not last:
                    act_rowsT(act, b + 1)
                if h == 12 and not last:
                    act_mask(act, b + 1)
                if h % 2 == 1 and h > 1:
                    act_o(act, 8 * b + h // 2 - 1, h // 2 - 1, b)
                elif h == 1 and not first:
                    act_o(act, 8 * b - 1, NPAIR - 1, b - 1)

        def act_attention(act):
            act_rowsT(act, 0)
            act_mask(act, 0)
            act_q(act, 0, 0)
            act_q(act, 1, 1)
            act_exp(act, 0, 0)
            act_exp(act, 1, 1)
            batches(act, act_batch)
            act_o(act, 8 * BATCH - 1, NPAIR - 1, BATCH - 1)

        def dve_first(dve, b):
            dve.wait_ge(C.pairs_loaded, 32 * b + 32)
            for i in range(QT):
                row = one(x2[:, :, :], 2 * b + i)
                nc.vector.scalar_tensor_tensor(out=row, in0=c_gat[:, i, 0, :], scalar=gates[:, 0, bass.ds(2 * b + i, 1)], in1=row,
                                               op0=ALU.mult, op1=ALU.add).then_inc(B.combine_step, 1)

        def dve_second(dve, b):
            dve.wait_ge(B.combine_step, 2 * b + 2)
            for i in range(QT):
                row = one(x2[:, :, :], 2 * b + i)
                nc.vector.scalar_tensor_tensor(out=row, in0=c_gat[:, i, 1, :], scalar=gates[:, 1, bass.ds(2 * b + i, 1)], in1=row,
                                               op0=ALU.mult, op1=ALU.add).then_inc(B.combined, 1)

        def dve_row_stats(dve, b):
            for i in range(QT):
                nc.vector.bn_stats(in_stats[:, i, :], one(x2[:, :, :], 2 * b + i)).then_inc(C.row_step, 1)

        def dve_row_moments(dve, b):
            for i in range(QT):
                nc.vector.bn_aggr(in_mv[:, i, :], in_stats[:, i, :]).then_inc(C.row_step, 1)

        def dve_row_variances(dve, b):
            dve.wait_ge(C.row_step, 4 * b + 4)
            nc.vector.tensor_scalar(in_rstd[:, :], in_mv[:, :, 1:2].rearrange("p i o -> p (i o)"), LN_EPS, None, ALU.add
                                    ).then_inc(C.var_done, 1)

        def dve_rows(dve, b):
            dve.wait_ge(C.rstd_done, b + 1)
            wait(dve, C.xn_turned, b)
            for i in range(QT):
                nc.vector.tensor_scalar(c_xn[:, i, :], one(x2[:, :, :], 2 * b + i), in_mv[:, i, 0:1], in_rstd[:, i:i + 1],
                                        ALU.subtract, ALU.mult).then_inc(C.xn_ready, 1)

        def dve_k(dve, b, odd):
            dve.wait_ge(C.kv_mm, b + 1)
            wait(dve, C.s_mm, 16 * b - 16)
            for o in range(2):
                half = slice(DH * o, DH * o + DH)
                nc.vector.tensor_copy(c_kT[odd][half, o, 1:KEYS1], keys_x[half, :]
                                      ).then_inc(C.kT_ready, 1)

        def dve_v(dve, b):
            dve.wait_ge(C.kv_mm, b + 1)
            wait(dve, C.pv_mm, 8 * b)
            nc.vector.tensor_tensor(c_v, values_x[:, :, 0:DH], nvb[:, :].unsqueeze(1).to_broadcast([P, QT, DH]), ALU.subtract
                                    ).then_inc(C.v_ready, 1)

        def dve_scores(dve, g, h):
            for i, (a, z) in enumerate(((0, KEYS0), (KEYS0, KEYS))):
                last = nc.vector.tensor_tensor_reduce(c_sc[:, h % 2, a:z], psH[:, h % 2, a:z], c_bm[:, h % 2, a:z], 1.0, -LOWEST,
                                                      ALU.add, ALU.min, c_min[:, h % 2, i:i + 1])
            last.then_inc(C.score_ready, 1)

        def dve_scores_wait(dve, g):
            dve.wait_ge(C.s_mm, g + 1)
            dve.wait_ge(C.bm_ready, g + 1)

        def dve_sums(dve, g, h):
            dve.wait_ge(C.p_ready, 2 * g + 2)
            nc.vector.reciprocal(c_rec[:, h % 2, :], c_sum[:, h % 2, :]).then_inc(C.rec_ready, 1)

        def dve_norm(dve, g, h):
            dve.wait_ge(C.rec_ready, g + 1)
            nc.vector.tensor_scalar(c_p[:, h % 2, 1:KEYS0], c_p[:, h % 2, 1:KEYS0], c_rec[:, h % 2, 0:1], None, ALU.mult)
            own = c_p[:, h % 2, KEYS0 + 1:KEYS]
            nc.vector.tensor_scalar(own, own, c_rec[:, h % 2, 1:2], None, ALU.mult).then_inc(C.pn_ready, 1)

        def dve_pT(dve, g, h, b):
            dve.wait_ge(C.p_turned, g + 1)
            wait(dve, C.pv_mm, 8 * b + h // 2)
            nc.vector.tensor_copy(c_pT[:, 1, :], psHT[:, 1, 0:3 * P]).then_inc(C.pT_ready[1], 1)

        def dve_out_stats(dve):
            for i in range(QT):
                nc.vector.bn_stats(out_stats[:, i, :], psM[:, i * DIM:(i + 1) * DIM]).then_inc(C.out_step, 1)

        def dve_out_moments(dve):
            for i in range(QT):
                nc.vector.bn_aggr(out_mv[:, i, :], out_stats[:, i, :]).then_inc(C.out_step, 1)

        def dve_out_variances(dve, b):
            dve.wait_ge(C.out_step, 4 * b + 4)
            nc.vector.tensor_scalar(out_rstd[:, :], out_mv[:, :, 1:2].rearrange("p i o -> p (i o)"), LN_EPS, None, ALU.add
                                    ).then_inc(C.out_var, 1)

        def dve_out(dve, b):
            dve.wait_ge(C.out_rstd, b + 1)
            for i in range(QT):
                nc.vector.tensor_scalar(one(acc[:, :, :], 2 * b + i), psM[:, i * DIM:(i + 1) * DIM], out_mv[:, i, 0:1],
                                        out_rstd[:, i:i + 1], ALU.subtract, ALU.mult).then_inc(C.z_step, 1)

        def dve_batch(dve, b, odd, first, last):
            for h in range(HEADS):
                g = 16 * b + h
                if h == 9 and not last:
                    dve_rows(dve, b + 1)
                if h == 4 and not first:
                    dve.wait_ge(C.wo_mm, b)
                if h == 5 and not first:
                    dve.wait_ge(C.out_step, 4 * b - 2)
                if h == 5 and not last:
                    dve.wait_ge(B.combined, 2 * b + 4)
                if h == 6 and not last:
                    dve.wait_ge(C.row_step, 4 * b + 6)
                if not (last and h >= 14):
                    dve_scores_wait(dve, g + 2)
                if not (last and h >= 15):
                    dve_sums(dve, g + 1, (h + 1) % HEADS)
                if not (last and h >= 14):
                    dve_scores(dve, g + 2, (h + 2) % HEADS)
                if h == 13 and not last:
                    dve_k(dve, b + 1, 1 - odd)
                if h == 4 and not first:
                    dve_out_stats(dve)
                if h == 5 and not first:
                    dve_out_moments(dve)
                if h == 5 and not last:
                    dve_row_stats(dve, b + 1)
                if h == 6 and not last:
                    dve_row_moments(dve, b + 1)
                if h % 2 == 1:
                    dve_pT(dve, g, h, b)
                if not (last and h >= 15):
                    dve_norm(dve, g + 1, (h + 1) % HEADS)
                if h == 1 and not first:
                    dve_v(dve, b)
                if h == 5 and not first:
                    dve_out_variances(dve, b - 1)
                if h == 10 and not first:
                    dve_out(dve, b - 1)
                if not last:
                    if h == 6:
                        dve_row_variances(dve, b + 1)

        def dve_attention(dve):
            dve.wait_ge(fB.y_out, B.NT)
            for k in c_kT:
                nc.vector.memset(k[DH:P, 0, :], 0.0).then_inc(C.kT_fixed, 1)
                nc.vector.memset(k[0:DH, 1, :], 0.0).then_inc(C.kT_fixed, 1)
                nc.vector.tensor_copy(k[0:DH, 0, 0:1], nk2[0:DH, :]).then_inc(C.kT_fixed, 1)
                nc.vector.tensor_copy(k[DH:P, 1, 0:1], nk2[DH:P, :]).then_inc(C.kT_fixed, 1)
            dve.wait_ge(x_loaded, 16)
            dve_first(dve, 0)
            dve_second(dve, 0)
            dve.wait_ge(B.combined, 2)
            dve_row_stats(dve, 0)
            dve.wait_ge(C.row_step, 2)
            dve_row_moments(dve, 0)
            dve_row_variances(dve, 0)
            dve_rows(dve, 0)
            dve_k(dve, 0, 0)
            dve_v(dve, 0)
            for g in range(2):
                dve_scores_wait(dve, g)
                dve_scores(dve, g, g)
            dve_sums(dve, 0, 0)
            dve_norm(dve, 0, 0)
            batches(dve, dve_batch)
            dve.wait_ge(C.wo_mm, BATCH)
            dve_out_stats(dve)
            dve.wait_ge(C.out_step, 4 * BATCH - 2)
            dve_out_moments(dve)
            dve_out_variances(dve, BATCH - 1)
            dve_out(dve, BATCH - 1)

        def pool_bm(pool, b, g, h):
            if h == 0:
                pool.wait_ge(C.mask_ready, 2 * b + 2)
            wait(pool, C.score_ready, g - 1)
            pool.tensor_tensor(c_bm[:, h % 2, :], c_mp, c_bias[:, h, :], ALU.subtract).then_inc(C.bm_ready, 1)

        def pool_pairs_wait(pool, b, h):
            if h == 0:
                pool.wait_ge(C.pairs_loaded, 32 * b + 32)
            else:
                pool.wait_ge(C.weighted, 4 * b - 4 + h)
            if h > 0 and h % 2 == 0:
                pool.wait_ge(B.combine_step, 2 * b + h // 2)

        def pool_pairs(pool, b, h):
            if h > 0:
                i, c = divmod(h - 1, 2)
                row = one(x2[:, :, :], 2 * b + i)
                pool.tensor_tensor(row, row, c_gat[:, i, c, :], ALU.add).then_inc(B.combined if c else B.combine_step, 1)
            if h < 2 * QT:
                i, c = divmod(h, 2)
                result, gate = c_gat[:, i, c, :], gates[:, c, bass.ds(2 * b + i, 1)]
                pool.tensor_tensor(result, result, gate.to_broadcast([P, DIM]), ALU.mult).then_inc(C.weighted, 1)

        def pool_row_rstd(pool, b):
            pool.wait_ge(C.var_done, b + 1)
            pool.tensor_tensor(in_rstd[:, :], in_rstd[:, :], minus_half[:, 0:QT], ALU.pow).then_inc(C.rstd_done, 1)

        def pool_add_bias(pool, b):
            for i in range(QT):
                row = one(x2[:, :, :], 2 * b + i)
                pool.tensor_tensor(row, row, d_sb2[:, :], ALU.add).then_inc(C.x_biased, 1)

        def pool_out_rstd(pool, b):
            pool.wait_ge(C.out_var, b + 1)
            pool.tensor_tensor(out_rstd[:, :], out_rstd[:, :], minus_half[:, 0:QT], ALU.pow).then_inc(C.out_rstd, 1)

        def pool_out(pool, b):
            pool.wait_ge(C.z_step, 2 * b + 2)
            for i in range(QT):
                row = one(acc[:, :, :], 2 * b + i)
                pool.tensor_tensor(row, row, g_out[:, :], ALU.mult).then_inc(D.token_ready, 1)

        def pool_batch(pool, b, odd, first, last):
            for h in range(HEADS):
                g = 16 * b + h
                if h <= 2 * QT and not last:
                    pool_pairs_wait(pool, b + 1, h)
                if h == 10:
                    pool.wait_ge(C.xn_ready, 2 * b + 2)
                if not (last and h >= 14):
                    pool_bm(pool, b + (h + 2) // HEADS, g + 2, (h + 2) % HEADS)
                if h <= 2 * QT and not last:
                    pool_pairs(pool, b + 1, h)
                if h == 10:
                    pool_add_bias(pool, b)
                if h == 6 and not first:
                    pool_out_rstd(pool, b - 1)
                if h == 7 and not last:
                    pool_row_rstd(pool, b + 1)
                if h == 11 and not first:
                    pool_out(pool, b - 1)

        def pool_biases(pool, t):
            n = t - RING - 20
            if n == 0:
                pool.wait_ge(C.loaded, C.loads)
            if n in (0, 1):
                a = (0, KEYS0)[n]
                pool.tensor_copy(c_bias[:, :, a:a + 1].rearrange("p h o -> p (h o)"), nullb[:, :]).then_inc(C.bias_ready, 1)
            elif n in (2, 4):
                a = (1, KEYS0 + 1 + P)[(n - 2) // 2]
                own = c_bias[:, :, a:a + P]
                pool.affine_select(out=own, in_=own, compare_op=ALU.is_ge, fill=-HIDDEN_KEY, base=0,
                                   pattern=[[0, HEADS], [-1, P]], channel_multiplier=1).then_inc(C.bias_ready, 1)

        def pool_attention(pool):
            for a in (0, KEYS0):
                pool.memset(c_mp[:, a:a + 1], 0.0).then_inc(C.bias_ready, 1)
            pool.wait_ge(C.bias_ready, 6)
            pool_row_rstd(pool, 0)
            pool_bm(pool, 0, 0, 0)
            pool_bm(pool, 0, 1, 1)
            batches(pool, pool_batch)
            pool_out_rstd(pool, BATCH - 1)
            pool_out(pool, BATCH - 1)

        def sp_pairs(sp, b):
            wait(sp, B.combined, 2 * b)
            for i in range(QT):
                sp.dma_start(c_gat[:, i, :, :], pair_rows(B, 2 * b + i)).then_inc(C.pairs_loaded, 16)

        def sp_store_z(sp, b):
            sp.wait_ge(D.token_ready, 2 * b + 2)
            for i in range(QT):
                sp.dma_start(dram_tile(z_dram, 2 * b + i), one(acc[:, :, :], 2 * b + i)).then_inc(C.z_stored, 16)

        def sp_load_d(sp):
            sp.wait_ge(fB.y_out, B.NT)
            for dst, name in ((d_w13, "d_w13"), (d_w2, "d_w2"), (d_s13, "d_s13"), (d_s2, "d_s2"), (d_sb13, "d_sb13")):
                sp.dma_start(dst, io[name]).then_inc(D.weights_loaded, 16)
            for dst, name in ((d_b13, "d_b13"), (d_b2, "d_b2")):
                load_broadcast(sp, dst, name, D.weights_loaded)

        def sp_attention(sp):
            wait_dmas(sp, B.slots_stored)
            sp_pairs(sp, 0)
            sp_pairs(sp, 1)
            sp_load_d(sp)
            with sp.Fori(2, BATCH) as b:
                sp_pairs(sp, b)
                sp_store_z(sp, b - 2)
            sp_store_z(sp, BATCH - 2)
            sp_store_z(sp, BATCH - 1)

        def dve_combine(dve, st, tile, first, last):
            def body(s0, u):
                wait_dma(dve, st.gathered, s0 + first, u)
                tile(s0 + first, u, s0 + first + u)
            steps(dve, last - first, body, 0, 0)

        def weighted(st, c, u, t, dst, base):
            return nc.vector.scalar_tensor_tensor(out=dst, in0=gat[:, u, c, :], scalar=gates[:, c, bass.ds(t, 1)], in1=base,
                                                  op0=ALU.mult, op1=ALU.add)

        block = ctx.enter_context(nc.Block())

        out_stored = Use(tokens_stored, TT)

        first = [(a_wt, "a_wt"), (condT, "condT"), (a_wgT, "a_wgT")]

        def load_all(eng, pairs, s):
            for dst, name in pairs:
                eng.dma_start(dst[:], io[name]).then_inc(s, 16)

        @block.sync
        def _(sp):
            x_tiles = io["x"].rearrange("(t p) d -> p t d", p=P)
            for q in range(TT // QUAD):
                sp.dma_start(acc[:, q * QUAD:(q + 1) * QUAD, :], x_tiles[:, q * QUAD:(q + 1) * QUAD, :]
                             ).then_inc(x_chunk.sems[q], 16)
                if q == 0:
                    load_all(sp, first, first_loaded)
            for dst, name in ((a_sgu, "a_sgu"), (a_sdown, "a_sdown"), (a_gu, "a_gu"), (a_down, "a_down")):
                sp.dma_start(dst, io[name]).then_inc(A.weights_loaded, 16)

            def store_y0(s0, u):
                sp.dma_start(dram_tile(y0_dram, s0 + u), xr[:, u, :]).then_inc(B.token_stored.sems[u], 16)
            sp_combine(sp, A, store_y0)
            sp.wait_ge(fB.turned, RING)
            sp.dma_start(x2[:, :, :], x_tiles).then_inc(x_loaded, 16)
            for n, (dst, name) in enumerate(((c_wq, "c_wq"), (c_wkk, "c_wkk"), (c_wvv, "c_wvv"), (c_wo, "c_wo"))):
                sp.wait_ge(fB.turned, 2 * RING + 2 * n)
                sp.dma_start(dst, io[name]).then_inc(C.loaded, 16)
            bias = io["fside"].rearrange("h (i p) j -> i p h j", p=P)
            sp.dma_start(c_bias[:, :, 1:KEYS0], bias[0, :, :, 0:P]).then_inc(C.loaded, 16)
            sp.wait_ge(fB.turned, 4 * RING)
            sp.dma_start(c_bias[:, :, KEYS0 + 1:KEYS], bias[1]).then_inc(C.loaded, 16)
            sp_attention(sp)

            def store_out(s0, u):
                sp.dma_start(dram_tile(io["out"], s0 + u), xr[:, u, :]).then_inc(out_stored.sems[u], 16)
            sp_combine(sp, D, store_out)
            wait_dmas(sp, out_stored)

        small = [(b_wg, "b_wg"), (d_gw, "d_gw"), (g_in, "g_in"),
                 (nv2, "nv2"), (nk2, "nk2")]
        spread = [(b_bg, "b_bg"), (d_eb, "d_eb"), (g_out, "g_out"), (d_sb2, "d_sb2"), (nvb, "nvb"), (nullb, "nullb"), (mask8, "mask")]

        @block.scalar
        def _(act):
            act_router_quads(act, A, 0)
            load_all(act, small, consts_loaded)
            for dst, name in spread:
                load_broadcast(act, dst[:], name, consts_loaded)
            for dst, name in ((b_w1, "b_w1"), (b_w2, "b_w2")):
                act.dma_start(dst, io[name]).then_inc(B.weights_loaded, 16)
            load_broadcast(act, b_b1, "b_b1", B.weights_loaded)
            act_route(act, A)
            act_shared(act, A.shared, "leaky", shared_first)
            act_ffn(act, fA)
            act_shared(act, A.shared, "leaky", shared_rest)
            act_router(act, B)
            act_route(act, B)
            load_broadcast(act, b_b2, "b_b2", B.weights_loaded)
            act_ffn(act, fB)
            act_attention(act)
            act_router_quads(act, D, TT // QUAD)
            act_route(act, D)
            act.wait_ge(C.z_stored, 16 * TT)
            act_shared(act, D.shared, "silu", shared_first)
            act_ffn(act, fD)
            act_shared(act, D.shared, "silu", shared_rest)

        n_consts = 16 * (len(small) + len(spread))
        cond_step = sem("cond_step")

        @block.gpsimd
        def _(pool):
            pool.memset(ident[:, :], 0.0).then_inc(consts_made, 1)
            pool.memset(ones_f[:, :], 1.0).then_inc(consts_made, 1)
            pool.memset(minus_half[:, :], -0.5).then_inc(consts_made, 1)
            pool.memset(ones16[:, :], 1.0).then_inc(consts_made, 1)
            pool.memset(not_first[:, :, :], 1.0).then_inc(consts_made, 1)
            pool.iota(iota_p16[:, :], [[1, P]], base=0, channel_multiplier=0, allow_small_or_imprecise_dtypes=True).then_inc(consts_made, 1)
            pool.iota(iota_t[:, :], [[1, 48]], base=0, channel_multiplier=0, allow_small_or_imprecise_dtypes=True).then_inc(consts_made, 1)
            pool.iota(iota_128[:, :], [[P, TT]], base=0, channel_multiplier=0, allow_small_or_imprecise_dtypes=True).then_inc(consts_made, 1)
            pool.iota(token_id1[:, :, :], [[0, 2], [P, TT]], base=1, channel_multiplier=1, allow_small_or_imprecise_dtypes=True).then_inc(consts_made, 1)
            pool.iota(past_row[:, :], [[P, 48]], base=PAIRS + 1, channel_multiplier=1, allow_small_or_imprecise_dtypes=True).then_inc(consts_made, 1)
            pool.iota(rank8[:, :], [[-1, 16]], base=16, channel_multiplier=0, allow_small_or_imprecise_dtypes=True).then_inc(consts_made, 1)
            pool.wait_ge(consts_made, 11)
            pool.affine_select(out=ident[:, :], in_=ident[:, :], compare_op=ALU.not_equal, fill=1.0, base=0,
                               pattern=[[-1, P]], channel_multiplier=1).then_inc(consts_made, 1)
            pool.affine_select(out=before16[:, :], in_=ones16[:, :], compare_op=ALU.is_gt, fill=0.0, base=0,
                               pattern=[[1, P]], channel_multiplier=-1).then_inc(consts_made, 1)
            pool.memset(not_first[:, :, 0:1], 0.0).then_inc(consts_made, 1)
            pool_shared(pool, A.shared, "leaky", shared_first + shared_rest)
            pool_gather_rows(pool, A, 0, ROWS + AHEAD)
            pool_slots(pool, A)
            pool_gather_rows(pool, B, 0, ROWS + AHEAD)
            pool_slots(pool, B, pool_biases)
            pool_attention(pool)
            pool_shared(pool, D.shared, "silu", shared_first)
            pool_gather_rows(pool, D, 0, ROWS + AHEAD)
            pool_slots(pool, D)
            pool_shared(pool, D.shared, "silu", shared_rest)

        n_made = 14

        @block.tensor
        def _(pe):
            pe.wait_ge(consts_made, n_made)
            pe.wait_ge(first_loaded, 16 * len(first))
            pe_router_quads(pe, A, a_wt, 0)
            pe.wait_ge(cond_step, 1)
            pe.matmul(psM[:, 0:64], ones_f[0:64, :], cg[:, :, :].rearrange("p b e -> p (b e)"), start=True, stop=True
                      ).then_inc(cond_step, 1)
            pe.wait_ge(A.weights_loaded, A.loads)
            pe_route_and_shared(pe, A)
            pe.wait_ge(A.routed, 2)
            pe.wait_ge(A.shared.y_out, tiles_first)
            pe.wait_ge(A.shared.h_ready, len(shared_first))
            pe_ffn(pe, fA)
            pe.wait_ge(fA.y_out, A.NT)
            pe_shared_rest(pe, A.shared)
            pe.wait_ge(A.shared.y_out, TT)
            pe.wait_ge(consts_loaded, n_consts)
            pe_router(pe, B, b_wg)
            pe_counts(pe, B)
            pe_invert(pe, B)
            pe.wait_ge(B.weights_loaded, B.loads)
            pe.wait_ge(B.routed, 2)
            pe.wait_ge(fA.y_out, A.NT)
            pe_ffn(pe, fB)
            pe.wait_ge(fB.y_out, B.NT)
            pe.wait_ge(C.loaded, C.loads)
            pe_attention(pe)
            pe_router_quads(pe, D, d_gw, TT // QUAD)
            pe.wait_ge(D.weights_loaded, D.loads)
            pe_route_and_shared(pe, D)
            pe.wait_ge(D.routed, 2)
            pe.wait_ge(D.shared.y_out, tiles_first)
            pe.wait_ge(D.shared.h_ready, len(shared_first))
            pe_ffn(pe, fD)
            pe.wait_ge(fD.y_out, D.NT)
            pe_shared_rest(pe, D.shared)

        @block.vector
        def _(dve):
            dve.wait_ge(first_loaded, 16 * len(first))
            for b in range(BATCH):
                last = nc.vector.tensor_scalar(cg[:, b, :], a_wgT[:, :], condT[:, b:b + 1], None, ALU.mult)
            last.then_inc(cond_step, 1)
            dve.wait_ge(cond_step, 2)
            nc.vector.tensor_copy(lg_g[:, :, :].rearrange("p b e -> p (b e)"), psM[:, 0:64]).then_inc(cond_step, 1)
            dve.wait_ge(cond_step, 3)
            dve.wait_ge(consts_made, n_made)
            dve_route(dve, A)
            dve_shared(dve, A.shared, "leaky", shared_first)
            dve_ffn(dve, fA)
            dve_shared(dve, A.shared, "leaky", shared_rest)

            def combine_a(s0, u, t):
                dve.wait_ge(A.shared.y_out, t + 1)
                wait(dve, B.tok_turned, t - RING + 1)
                wait_slot_free(dve, B.token_stored, s0, u)
                weighted(A, 0, u, t, xr[:, u, :], one(acc[:, :, :], t)).then_inc(A.combine_step, 1)
                dve.wait_ge(A.combine_step, t + 1)
                weighted(A, 1, u, t, xr[:, u, :], xr[:, u, :]).then_inc(A.combined, 1)
            dve_combine(dve, A, combine_a, 0, TT)
            dve.wait_ge(consts_loaded, n_consts)
            dve_route(dve, B)
            dve_ffn(dve, fB)
            dve_attention(dve)

            dve_route(dve, D)
            dve.wait_ge(D.weights_loaded, D.loads)
            dve_shared(dve, D.shared, "silu", shared_first)

            def add_x(first, last):
                for t in range(first, last):
                    dve.wait_ge(D.shared.y_out, t + 1)
                    nc.vector.tensor_tensor(acc[:, t, :], acc[:, t, :], x2[:, t, :], ALU.add).then_inc(C.base_ready, 1)

            def combine_d(s0, u, t):
                wait_slot_free(dve, out_stored, s0, u)
                weighted(D, 0, u, t, xr[:, u, :], one(acc[:, :, :], t)).then_inc(D.combine_step, 1)
                dve.wait_ge(D.combine_step, t + 1)
                weighted(D, 1, u, t, xr[:, u, :], xr[:, u, :]).then_inc(D.combined, 1)
            dve.wait_ge(C.x_biased, TT)
            add_x(0, tiles_first)
            dve_ffn(dve, fD)
            dve.wait_ge(C.base_ready, tiles_first)
            dve_combine(dve, D, combine_d, 0, tiles_first)
            add_x(tiles_first, TT)
            dve.wait_ge(C.base_ready, TT)
            dve_combine(dve, D, combine_d, tiles_first, TT)


def layout(inputs):
    import numpy as np

    def rows(w):
        return np.ascontiguousarray(w.reshape(-1, 128, w.shape[-1]).transpose(1, 0, 2))

    def expert_rows(w):
        e, k, n = w.shape
        return np.ascontiguousarray(w.reshape(e, k // 128, 128, n).transpose(2, 0, 1, 3))

    i = {k: np.asarray(v) for k, v in inputs.items()}
    cat = np.concatenate
    o = {}
    o["x"] = i["x"].reshape(2048, 256)
    o["condT"] = i["cond_64"].T
    o["a_wt"] = rows(i["L0_cond_wt"].T)
    o["a_wgT"] = i["L0_cond_wg"].T
    o["a_gu"] = expert_rows(cat([i["L0_cond_w_gate"], i["L0_cond_w_up"]], -1))
    o["a_down"] = i["L0_cond_w_down"].transpose(1, 0, 2)
    o["a_sgu"] = rows(cat([i["L0_cond_sw_gate"], i["L0_cond_sw_up"]], -1))
    o["a_sdown"] = rows(i["L0_cond_sw_down"])
    o["b_wg"] = rows(i["L0_ffn_Wg"])
    o["b_bg"] = i["L0_ffn_bg"].reshape(1, -1)
    o["b_w1"] = expert_rows(i["L0_ffn_W1"])
    o["b_w2"] = expert_rows(i["L0_ffn_W2"])
    o["b_b1"] = i["L0_ffn_b1"].reshape(1, -1)
    o["b_b2"] = i["L0_ffn_b2"].reshape(1, -1)
    o["g_in"] = i["L1_cond_g_in"].reshape(2, 128).T
    o["g_out"] = i["L1_cond_g_out"].reshape(1, -1)
    o["nullb"] = i["L1_cond_null_attn_bias"].reshape(1, -1)
    nk, nv = i["cond_64"][0], i["cond_64"][1]
    o["nk2"] = cat([nk, nk]).reshape(-1, 1)
    o["nv2"] = cat([nv, nv]).reshape(-1, 1)
    o["nvb"] = nv.reshape(1, -1)
    wk, wv = i["L1_cond_Wkv"][:, :64], i["L1_cond_Wkv"][:, 64:]
    o["c_wq"] = rows(i["L1_cond_Wq"])
    o["c_wkk"] = rows(cat([wk, wk], 1))
    o["c_wvv"] = rows(cat([wv, wv], 1))
    o["c_wo"] = rows(i["L1_cond_Wo"])
    o["fside"] = i["fside_16xSxS_0"]
    o["mask"] = i["mask_BxS_bk0"].reshape(1, -1)
    o["d_gw"] = rows(i["L1_ffn_gate_w"].T)
    o["d_eb"] = i["L1_ffn_expert_bias"].reshape(1, -1)
    o["d_w13"] = expert_rows(cat([i["L1_ffn_w1"], i["L1_ffn_w3"]], 1).transpose(0, 2, 1))
    o["d_b13"] = cat([i["L1_ffn_b1"], i["L1_ffn_b3"]], 1).reshape(1, -1)
    o["d_w2"] = i["L1_ffn_w2"].transpose(2, 0, 1)
    o["d_b2"] = i["L1_ffn_b2"].reshape(1, -1)
    o["d_s13"] = rows(cat([i["L1_ffn_sw1"], i["L1_ffn_sw3"]], 0).T)
    o["d_sb13"] = cat([i["L1_ffn_sb1"], i["L1_ffn_sb3"]], 0).reshape(-1, 128).T
    o["d_s2"] = rows(i["L1_ffn_sw2"].T)
    o["d_sb2"] = i["L1_ffn_sb2"].reshape(1, -1)
    return {k: np.ascontiguousarray(v) for k, v in o.items()}


def kernel(**inputs):
    import numpy as np
    import concourse.bacc as bacc
    from concourse.bass_utils import run_bass_kernel_spmd

    nc = bacc.Bacc("TRN2", target_bir_lowering=False, num_devices=1)
    arrays, io = {}, {}
    for name, a in layout(inputs).items():
        arrays[f"in_{name}"] = a
        io[name] = nc.dram_tensor(f"in_{name}", a.shape, mybir.dt.from_np(a.dtype), kind="ExternalInput").ap()
    io["out"] = nc.dram_tensor("out", (TOKENS, DIM), F32, kind="ExternalOutput").ap()
    build(nc, io)
    r = run_bass_kernel_spmd(nc, [arrays], core_ids=[0])
    return r.results[0]["out"].reshape(BATCH, SEQ, DIM)
```
